# Optimizing a Trainium2 kernel written in Bass

```python
import numpy as np
import jax
import jax.numpy as jnp

def _softmax(x, axis=-1):
    return jax.nn.softmax(x, axis=axis)

def _gelu(x):
    return jax.nn.gelu(x, approximate=True)

def _silu(x):
    return jax.nn.silu(x)

def _sigmoid(x):
    return jax.nn.sigmoid(x)

def _layernorm(x, axis=-1, eps=1e-05):
    m = jnp.mean(x, axis=axis, keepdims=True)
    v = jnp.var(x, axis=axis, keepdims=True)
    return (x - m) / jnp.sqrt(v + eps)

def _scatter_add(tgt, idx, src, axis=0):
    return tgt.at[idx].add(src)

def _segment_sum(src, seg, n):
    return jax.ops.segment_sum(src, seg, n)
kernel_name = 'mk_xattn_ffn_d2_seqx_r8_c2759c'

def setup_inputs(seed: int=0):
    np.random.seed(seed)
    _w = jnp.asarray

    def _rec_inputs():
        import jax
        import jax.numpy as jnp
        _rk = jax.random.key(seed)
        x = -0.0002928 + 1 * jax.random.normal(jax.random.fold_in(_rk, 1), (8, 128, 256), jnp.float32)
        _lenS = 128 - jax.random.randint(jax.random.fold_in(_rk, 7), (8,), 0, max(1, 128 // 4) + 1, jnp.int32)
        _lenS2 = 128 - jax.random.randint(jax.random.fold_in(_rk, 8), (8,), 0, max(1, 128 // 4) + 1, jnp.int32)
        _ctx_2048P = jax.random.normal(jax.random.fold_in(_rk, 11), (8, 16, 256), jnp.float32)
        _ctx_2048c = jax.random.dirichlet(jax.random.fold_in(_rk, 511), 0.3 * jnp.ones((16,), jnp.float32), (8, 128))
        _ctx_2048t = jnp.einsum('bsk,bkd->bsd', _ctx_2048c, _ctx_2048P)
        _ctx_2048t = _ctx_2048t * jax.lax.rsqrt(jnp.mean(jnp.square(_ctx_2048t)) + 1e-12) * 0.953939
        ctx_2048 = 4.13588e-05 + 0.999923 * (_ctx_2048t + 0.3 * jax.random.normal(jax.random.fold_in(_rk, 611), (8, 128, 256), jnp.float32))
        _validS = jnp.arange(128)[None, :] < _lenS[:, None]
        _validS2 = jnp.arange(128)[None, :] < _lenS2[:, None]
        _causal = jnp.tril(jnp.ones((128, 128), dtype=bool))
        mask_1xSxS2_ff0 = jnp.where(jnp.ones((1, 128, 128), dtype=bool), 0.0, -1000000000.0).astype(jnp.float32)
        return (x, ctx_2048, mask_1xSxS2_ff0)
    x, ctx_2048, mask_1xSxS2_ff0 = _rec_inputs()

    def _L0_xattn_setup():
        import jax, jax.numpy as jnp
        import numpy as np
        H = 256
        NH = 16
        NKV = 4
        HD = 128
        GROUPS = NH // NKV
        EPS = 1e-06
        B, S, SE = (1, 256, 512)

        def _rmsnorm(x, w, eps=EPS):
            xf = x.astype(jnp.float32)
            var = jnp.mean(xf * xf, axis=-1, keepdims=True)
            return (xf * jax.lax.rsqrt(var + eps)).astype(x.dtype) * w
        key = jax.random.key(seed)
        ks = jax.random.split(key, 12)
        sc = 0.02
        return {'hidden_states': jax.random.normal(ks[0], (B, S, H), jnp.float32), 'encoder_hidden_states': jax.random.normal(ks[1], (B, SE, H), jnp.float32), 'attention_mask': jnp.zeros((B, S, SE), jnp.float32), 'Wq': jax.random.normal(ks[2], (H, NH * HD), jnp.float32) * sc, 'bq': jax.random.normal(ks[3], (NH * HD,), jnp.float32) * sc, 'Wk': jax.random.normal(ks[4], (H, NKV * HD), jnp.float32) * sc, 'bk': jax.random.normal(ks[5], (NKV * HD,), jnp.float32) * sc, 'Wv': jax.random.normal(ks[6], (H, NKV * HD), jnp.float32) * sc, 'bv': jax.random.normal(ks[7], (NKV * HD,), jnp.float32) * sc, 'Wo': jax.random.normal(ks[8], (NH * HD, H), jnp.float32) * sc, 'qn_w': jnp.ones((HD,), jnp.float32), 'kn_w': jnp.ones((HD,), jnp.float32)}
    _L0_xattn_all = _L0_xattn_setup()
    _L0_xattn_in = {k: v for k, v in _L0_xattn_all.items() if k in ('Wq', 'bq', 'Wk', 'bk', 'Wv', 'bv', 'Wo', 'qn_w', 'kn_w')}
    del _L0_xattn_all

    def _L0_ffn_setup():
        import jax, jax.numpy as jnp
        import numpy as np
        NUM_EXPERTS = 32
        TOP_K = 8
        THRESHOLD = 0.8
        HIDDEN = 256
        INTER = 96
        key = jax.random.key(seed)
        k1, k2, k3, k4 = jax.random.split(key, 4)
        hidden_states = jax.random.normal(k1, (2, 128, HIDDEN), jnp.float32)
        gate_weight = jax.random.normal(k2, (NUM_EXPERTS, HIDDEN), jnp.float32) * 0.02
        gate_up_proj = jax.random.normal(k3, (NUM_EXPERTS, 2 * INTER, HIDDEN), jnp.float32) * 0.02
        down_proj = jax.random.normal(k4, (NUM_EXPERTS, HIDDEN, INTER), jnp.float32) * 0.02
        return {'hidden_states': hidden_states, 'gate_weight': gate_weight, 'gate_up_proj': gate_up_proj, 'down_proj': down_proj}
    _L0_ffn_all = _L0_ffn_setup()
    _L0_ffn_in = {k: v for k, v in _L0_ffn_all.items() if k in ('gate_weight', 'gate_up_proj', 'down_proj')}
    del _L0_ffn_all

    def _L1_xattn_setup():
        import jax, jax.numpy as jnp
        import numpy as np
        NUM_HEADS = 16

        def _qdq(x):
            s = jnp.maximum(jnp.max(jnp.abs(x), axis=-1, keepdims=True) / 127.0, 1e-08)
            return jnp.clip(jnp.round(x / s), -127.0, 127.0) * s
        key = jax.random.key(seed)
        ks = jax.random.split(key, 8)
        B, N, M, D = (2, 512, 64, 256)
        w_std = 0.02
        return {'x': jax.random.normal(ks[0], (B, N, D), jnp.float32), 'cond': jax.random.normal(ks[1], (B, M, D), jnp.float32), 'wq': jax.random.normal(ks[2], (D, D), jnp.float32) * w_std, 'bq': jax.random.normal(ks[3], (D,), jnp.float32) * w_std, 'wkv': jax.random.normal(ks[4], (2 * D, D), jnp.float32) * w_std, 'bkv': jax.random.normal(ks[5], (2 * D,), jnp.float32) * w_std, 'wp': jax.random.normal(ks[6], (D, D), jnp.float32) * w_std, 'bp': jax.random.normal(ks[7], (D,), jnp.float32) * w_std}
    _L1_xattn_all = _L1_xattn_setup()
    _L1_xattn_in = {k: v for k, v in _L1_xattn_all.items() if k in ('wq', 'bq', 'wkv', 'bkv', 'wp', 'bp')}
    del _L1_xattn_all

    def _L1_ffn_setup():
        import jax, jax.numpy as jnp
        import numpy as np
        D_MODEL = 256
        HIDDEN = 4 * D_MODEL
        B, S = (2, 512)

        def bit_linear(x, w, b):
            gamma_x = jnp.clip(jnp.max(jnp.abs(x), axis=-1, keepdims=True), 1e-05, None)
            scale_x = 127.0 / gamma_x
            x_dq = jnp.clip(jnp.round(x * scale_x), -128.0, 127.0) / scale_x
            x_ste = x + jax.lax.stop_gradient(x_dq - x)
            gamma_w = jnp.clip(jnp.mean(jnp.abs(w)), 1e-05, None)
            w_dq = jnp.clip(jnp.round(w / gamma_w), -1.0, 1.0) * gamma_w
            w_ste = w + jax.lax.stop_gradient(w_dq - w)
            return jnp.einsum('bsd,hd->bsh', x_ste, w_ste) + b
        key = jax.random.key(seed)
        ks = jax.random.split(key, 7)
        std = 0.02
        return {'x': jax.random.normal(ks[0], (B, S, D_MODEL), dtype=jnp.float32), 'gate_w': jax.random.normal(ks[1], (HIDDEN, D_MODEL), dtype=jnp.float32) * std, 'gate_b': jnp.zeros((HIDDEN,), dtype=jnp.float32), 'val_w': jax.random.normal(ks[2], (HIDDEN, D_MODEL), dtype=jnp.float32) * std, 'val_b': jnp.zeros((HIDDEN,), dtype=jnp.float32), 'out_w': jax.random.normal(ks[3], (D_MODEL, HIDDEN), dtype=jnp.float32) * std, 'out_b': jnp.zeros((D_MODEL,), dtype=jnp.float32)}
    _L1_ffn_all = _L1_ffn_setup()
    _L1_ffn_in = {k: v for k, v in _L1_ffn_all.items() if k in ('gate_w', 'gate_b', 'val_w', 'val_b', 'out_w', 'out_b')}
    del _L1_ffn_all
    return {'x': x, 'ctx_2048': ctx_2048, 'mask_1xSxS2_ff0': mask_1xSxS2_ff0, 'L0_xattn_Wq': _L0_xattn_in['Wq'], 'L0_xattn_bq': _L0_xattn_in['bq'], 'L0_xattn_Wk': _L0_xattn_in['Wk'], 'L0_xattn_bk': _L0_xattn_in['bk'], 'L0_xattn_Wv': _L0_xattn_in['Wv'], 'L0_xattn_bv': _L0_xattn_in['bv'], 'L0_xattn_Wo': _L0_xattn_in['Wo'], 'L0_xattn_qn_w': _L0_xattn_in['qn_w'], 'L0_xattn_kn_w': _L0_xattn_in['kn_w'], 'L0_ffn_gate_weight': _L0_ffn_in['gate_weight'], 'L0_ffn_gate_up_proj': _L0_ffn_in['gate_up_proj'], 'L0_ffn_down_proj': _L0_ffn_in['down_proj'], 'L1_xattn_wq': _L1_xattn_in['wq'], 'L1_xattn_bq': _L1_xattn_in['bq'], 'L1_xattn_wkv': _L1_xattn_in['wkv'], 'L1_xattn_bkv': _L1_xattn_in['bkv'], 'L1_xattn_wp': _L1_xattn_in['wp'], 'L1_xattn_bp': _L1_xattn_in['bp'], 'L1_ffn_gate_w': _L1_ffn_in['gate_w'], 'L1_ffn_gate_b': _L1_ffn_in['gate_b'], 'L1_ffn_val_w': _L1_ffn_in['val_w'], 'L1_ffn_val_b': _L1_ffn_in['val_b'], 'L1_ffn_out_w': _L1_ffn_in['out_w'], 'L1_ffn_out_b': _L1_ffn_in['out_b']}

def reference(x, ctx_2048, mask_1xSxS2_ff0, L0_xattn_Wq, L0_xattn_bq, L0_xattn_Wk, L0_xattn_bk, L0_xattn_Wv, L0_xattn_bv, L0_xattn_Wo, L0_xattn_qn_w, L0_xattn_kn_w, L0_ffn_gate_weight, L0_ffn_gate_up_proj, L0_ffn_down_proj, L1_xattn_wq, L1_xattn_bq, L1_xattn_wkv, L1_xattn_bkv, L1_xattn_wp, L1_xattn_bp, L1_ffn_gate_w, L1_ffn_gate_b, L1_ffn_val_w, L1_ffn_val_b, L1_ffn_out_w, L1_ffn_out_b):
    import jax
    import jax.numpy as jnp

    def _L0_xattn_ref(hidden_states, encoder_hidden_states, attention_mask, Wq, bq, Wk, bk, Wv, bv, Wo, qn_w, kn_w):
        import jax, jax.numpy as jnp
        import numpy as np
        H = 256
        NH = 16
        NKV = 4
        HD = 128
        GROUPS = NH // NKV
        EPS = 1e-06
        B, S, SE = (1, 256, 512)

        def _rmsnorm(x, w, eps=EPS):
            xf = x.astype(jnp.float32)
            var = jnp.mean(xf * xf, axis=-1, keepdims=True)
            return (xf * jax.lax.rsqrt(var + eps)).astype(x.dtype) * w
        b, s, _ = hidden_states.shape
        se = encoder_hidden_states.shape[1]
        q = (hidden_states @ Wq + bq).reshape(b, s, NH, HD).transpose(0, 2, 1, 3)
        k = (encoder_hidden_states @ Wk + bk).reshape(b, se, NKV, HD).transpose(0, 2, 1, 3)
        v = (encoder_hidden_states @ Wv + bv).reshape(b, se, NKV, HD).transpose(0, 2, 1, 3)
        k = jnp.repeat(k, GROUPS, axis=1)
        v = jnp.repeat(v, GROUPS, axis=1)
        q = _rmsnorm(q, qn_w)
        k = _rmsnorm(k, kn_w)
        scale = 1.0 / np.sqrt(HD).astype(np.float32)
        scores = jnp.einsum('bhsd,bhed->bhse', q, k) * scale
        scores = scores + attention_mask[:, None, :, :]
        probs = jax.nn.softmax(scores.astype(jnp.float32), axis=-1).astype(q.dtype)
        out = jnp.einsum('bhse,bhed->bhsd', probs, v)
        out = out.transpose(0, 2, 1, 3).reshape(b, s, NH * HD)
        return out @ Wo

    def _L0_ffn_ref(hidden_states, gate_weight, gate_up_proj, down_proj):
        import jax, jax.numpy as jnp
        import numpy as np
        NUM_EXPERTS = 32
        TOP_K = 8
        THRESHOLD = 0.8
        HIDDEN = 256
        INTER = 96
        B, S, H = hidden_states.shape
        x = hidden_states.reshape(-1, H)
        logits = x @ gate_weight.T
        probs = jax.nn.softmax(logits.astype(jnp.float32), axis=-1).astype(logits.dtype)
        top_vals, top_idx = jax.lax.top_k(probs, TOP_K)
        renorm = top_vals / jnp.clip(jnp.sum(top_vals, axis=-1, keepdims=True), 1e-12)
        cum = jnp.cumsum(renorm, axis=-1)
        num_keep = jnp.minimum(jnp.sum((cum < THRESHOLD).astype(jnp.int32), axis=-1) + 1, TOP_K)
        active = jnp.arange(TOP_K)[None, :] < num_keep[:, None]
        rw = top_vals * active.astype(top_vals.dtype)
        rw = rw / jnp.clip(jnp.sum(rw, axis=-1, keepdims=True), 1e-12)
        combine = jnp.sum(jax.nn.one_hot(top_idx, NUM_EXPERTS, dtype=rw.dtype) * rw[..., None], axis=1)

        def body(acc, params):
            w_gu, w_d, ce = params
            gu = x @ w_gu.T
            g, u = jnp.split(gu, 2, axis=-1)
            h = jax.nn.silu(g) * u
            return (acc + h @ w_d.T * ce[:, None], None)
        out, _ = jax.lax.scan(body, jnp.zeros_like(x), (gate_up_proj, down_proj, combine.T))
        return out.reshape(B, S, H)

    def _L1_xattn_ref(x, cond, wq, bq, wkv, bkv, wp, bp):
        import jax, jax.numpy as jnp
        import numpy as np
        NUM_HEADS = 16

        def _qdq(x):
            s = jnp.maximum(jnp.max(jnp.abs(x), axis=-1, keepdims=True) / 127.0, 1e-08)
            return jnp.clip(jnp.round(x / s), -127.0, 127.0) * s
        B, N, C = x.shape
        M = cond.shape[1]
        H = NUM_HEADS
        Dh = C // H
        q = _qdq(x) @ _qdq(wq).T + bq
        kv = cond @ wkv.T + bkv
        k, v = jnp.split(kv, 2, axis=-1)
        q = q.reshape(B, N, H, Dh)
        k = k.reshape(B, M, H, Dh)
        v = v.reshape(B, M, H, Dh)
        scale = 1.0 / np.sqrt(Dh)
        attn = jax.nn.softmax(jnp.einsum('bnhd,bmhd->bhnm', q, k) * scale, axis=-1)
        o = jnp.einsum('bhnm,bmhd->bnhd', attn, v).reshape(B, N, C)
        out = _qdq(o) @ _qdq(wp).T + bp
        return out

    def _L1_ffn_ref(x, gate_w, gate_b, val_w, val_b, out_w, out_b):
        import jax, jax.numpy as jnp
        import numpy as np
        D_MODEL = 256
        HIDDEN = 4 * D_MODEL
        B, S = (2, 512)

        def bit_linear(x, w, b):
            gamma_x = jnp.clip(jnp.max(jnp.abs(x), axis=-1, keepdims=True), 1e-05, None)
            scale_x = 127.0 / gamma_x
            x_dq = jnp.clip(jnp.round(x * scale_x), -128.0, 127.0) / scale_x
            x_ste = x + jax.lax.stop_gradient(x_dq - x)
            gamma_w = jnp.clip(jnp.mean(jnp.abs(w)), 1e-05, None)
            w_dq = jnp.clip(jnp.round(w / gamma_w), -1.0, 1.0) * gamma_w
            w_ste = w + jax.lax.stop_gradient(w_dq - w)
            return jnp.einsum('bsd,hd->bsh', x_ste, w_ste) + b
        gate = jax.nn.silu(bit_linear(x, gate_w, gate_b))
        val = bit_linear(x, val_w, val_b)
        return bit_linear(gate * val, out_w, out_b)
    x = x + _L0_xattn_ref(_layernorm(x, axis=-1), ctx_2048, mask_1xSxS2_ff0, L0_xattn_Wq, L0_xattn_bq, L0_xattn_Wk, L0_xattn_bk, L0_xattn_Wv, L0_xattn_bv, L0_xattn_Wo, L0_xattn_qn_w, L0_xattn_kn_w)
    x = x + _L0_ffn_ref(_layernorm(x, axis=-1), L0_ffn_gate_weight, L0_ffn_gate_up_proj, L0_ffn_down_proj)
    x = x + _L1_xattn_ref(_layernorm(x, axis=-1), ctx_2048, L1_xattn_wq, L1_xattn_bq, L1_xattn_wkv, L1_xattn_bkv, L1_xattn_wp, L1_xattn_bp)
    x = x + _L1_ffn_ref(_layernorm(x, axis=-1), L1_ffn_gate_w, L1_ffn_gate_b, L1_ffn_val_w, L1_ffn_val_b, L1_ffn_out_w, L1_ffn_out_b)
    return x

_drawn_inputs = setup_inputs


def setup_inputs(seed=0):
    import zlib

    import numpy as np

    out = dict(_drawn_inputs(seed))
    spreads = {'L0_xattn_qn_w': (1.0, 0.6),
     'L0_xattn_kn_w': (1.0, 0.6),
     'L1_ffn_gate_b': (0.0, 0.8),
     'L1_ffn_val_b': (0.0, 0.8),
     'L1_ffn_out_b': (0.0, 0.417)}
    factors = {'L0_xattn_bq': 8.0,
     'L0_xattn_bk': 8.0,
     'L0_xattn_bv': 3.317,
     'L0_ffn_gate_weight': 8.0,
     'L0_ffn_gate_up_proj': 8.0,
     'L0_ffn_down_proj': 8.0,
     'L1_xattn_wq': 64.0,
     'L1_xattn_bq': 64.0,
     'L1_xattn_bkv': 40.324,
     'L1_xattn_bp': 12.531,
     'L1_ffn_gate_w': 4.62,
     'L1_ffn_val_w': 4.331,
     'L1_ffn_out_w': 3.866,
     'L1_xattn_wkv': 4.562,
     'L1_xattn_wp': 3.518}
    for name, (base, spread) in spreads.items():
        noise = np.random.default_rng([zlib.crc32(name.encode()), seed]).standard_normal(out[name].shape)
        drawn = base * np.exp(spread * noise) if base else spread * noise
        out[name] = jnp.asarray(drawn.astype(out[name].dtype))
    for name, factor in factors.items():
        out[name] = (out[name] * factor).astype(out[name].dtype)
    return out
```

```python
from contextlib import ExitStack

import concourse.bass as bass
from concourse import mybir

P = 128
BANK = 512
F32 = mybir.dt.float32
F32R = mybir.dt.float32r
BF16 = mybir.dt.bfloat16
ALU = mybir.AluOpType
ACT = mybir.ActivationFunctionType
AX_X = mybir.AxisListType.X

B, S, D = 8, 128, 256
T = B * S
KC = D // P
NH0, NKV0, HD0 = 16, 4, 128
GH = NH0 // NKV0
NE, TOPK, INTER = 32, 8, 96
MT = NE * INTER // P
THRESHOLD = 0.8
NH1 = 16
HD1 = D // NH1
HC = P // HD1
HIDDEN = 4 * D
RND = 12582912.0
WA = KC * GH * HD0 + KC * 2 * HD0 + GH * D
WQ_AT, WKV_AT, WO_AT = 0, KC * GH * HD0, KC * GH * HD0 + KC * 2 * HD0
WM = 2 * KC * P + D
BQ, BP, BG, BV, BO = (slice(a, a + n) for a, n in (
    (0, D), (D, D), (2 * D, HIDDEN), (2 * D + HIDDEN, HIDDEN), (2 * D + 2 * HIDDEN, D)))


class Mem:

    held = []

    def __init__(self, nc, ctx):
        self.nc, self.ctx = nc, ctx

    def sb(self, name, shape, dt=F32):
        return self.ctx.enter_context(self.nc.sbuf_tensor(name, shape, dt))

    def sem(self, name):
        self.held.append(self.nc.alloc_semaphore(name=name))
        return self.held[-1]

    def end_of_layer(self):
        self.nc.clear_and_free_semaphores(self.held)
        self.held.clear()
        self.nc.all_engine_barrier()


def banks(k, first=0, n=8, width=1):
    return [k.psum[:, (first + i * width) * BANK:(first + (i + 1) * width) * BANK] for i in range(n)]


def cols(t, at, n):
    return bass.ds(t * n + at, n)


def constants_and_first_norm(nc, io, k):
    with ExitStack() as ctx:
        m = Mem(nc, ctx)
        bank = banks(k, 0, 2)
        raw = m.sb("a_raw", [P, 2, WA])
        stats = m.sb("a_stats", [P, B, 6])
        mv = m.sb("a_mv", [P, B, 2])
        rstd = m.sb("a_rstd", [P, B])
        vpe = m.sb("a_vpe", [P, B])
        xn = m.sb("a_xn", [P, 2, D])
        s_x, s_ctx, s_mask, s_bias, s_norm_w = (m.sem(f"a_{n}") for n in ("x", "ctx", "mask", "bias", "norm_w"))
        s_raw = [m.sem("a_raw0"), m.sem("a_raw1")]
        zeroed, half, ident_done, hm_steps = (m.sem(f"a_{n}") for n in ("zeroed", "half", "ident", "hm"))
        stats_done, mv_done, vpe_done, rstd_done = (m.sem(f"a_{n}") for n in ("stats_d", "mv_d", "vpe_d", "rstd_d"))
        xn_done, xt_done, xt_read, hi_done, lo_done = (m.sem(f"a_{n}") for n in ("xn_d", "xt_d", "xt_r", "hi_d", "lo_d"))
        nw_mul = m.sem("a_nw_mul")
        block = ctx.enter_context(nc.Block())

        @block.sync
        def _(sp):
            sp.dma_start(k.x_res[:, :, :], io["x"].rearrange("b p d -> p b d")).then_inc(s_x, 16)
            for g in range(NKV0):
                if g >= 2:
                    sp.wait_ge(hi_done, g - 1)
                    sp.wait_ge(lo_done, g - 1)
                sp.dma_start(raw[:, g % 2, :], io["wa"][g]).then_inc(s_raw[g % 2], 16)

        @block.gpsimd
        def _(pool):
            nc.gpsimd.memset(k.ident[:, :], 0.0).then_inc(zeroed, 1)
            nc.gpsimd.memset(k.neg_half[:, :], -0.5).then_inc(half, 1)
            nc.gpsimd.memset(k.eps_a[:, :], HD0 * 1e-6)
            nc.gpsimd.memset(k.head_mask[:, :], 1.0).then_inc(hm_steps, 1)
            pool.wait_ge(zeroed, 1)
            nc.gpsimd.affine_select(out=k.ident[:, :], in_=k.ident[:, :], compare_op=ALU.not_equal, fill=1.0,
                                    base=0, pattern=[[-1, P]], channel_multiplier=1).then_inc(ident_done, 1)
            pool.wait_ge(hm_steps, 1)
            nc.gpsimd.affine_select(out=k.head_mask[:, :], in_=k.head_mask[:, :], compare_op=ALU.is_ge, fill=0.0,
                                    base=0, pattern=[[-HD1, HC]], channel_multiplier=1).then_inc(hm_steps, 1)
            pool.wait_ge(hm_steps, 2)
            nc.gpsimd.affine_select(out=k.head_mask[:, :], in_=k.head_mask[:, :], compare_op=ALU.is_ge, fill=0.0,
                                    base=HD1 - 1, pattern=[[HD1, HC]], channel_multiplier=-1).then_inc(hm_steps, 1)
            pool.wait_ge(mv_done, B)
            nc.gpsimd.tensor_scalar(vpe[:, :], mv[:, :, 1], 1e-5, None, ALU.add).then_inc(vpe_done, 1)
            pool.wait_ge(vpe_done, 1)
            pool.wait_ge(half, 1)
            nc.gpsimd.tensor_tensor(rstd[:, :], vpe[:, :], k.neg_half[:, 0:B], ALU.pow).then_inc(rstd_done, 1)

        @block.vector
        def _(dve):
            dve.wait_ge(s_x, 16)
            for t in range(B):
                nc.vector.bn_stats(stats[:, t, :], k.x_res[:, t, :]).then_inc(stats_done, 1)
            for t in range(B):
                dve.wait_ge(stats_done, t + 1)
                nc.vector.bn_aggr(mv[:, t, :], stats[:, t, :]).then_inc(mv_done, 1)
            dve.wait_ge(s_norm_w, 16)
            nc.vector.scalar_tensor_tensor(k.key_scale[:, :], k.norm_w[:, 0:1], float(HD0) ** 0.5, k.norm_w[:, 1:2],
                                           ALU.mult, ALU.mult).then_inc(nw_mul, 1)
            dve.wait_ge(rstd_done, 1)
            dve.sem_inc(xt_read, 2)
            with dve.Fori(0, B // 2) as i:
                for j in range(2):
                    t = i * 2 + j
                    dve.wait_ge(xt_read, t + 1)
                    nc.vector.tensor_scalar(xn[:, j, :], k.x_res[:, bass.ds(t, 1), :], mv[:, bass.ds(t, 1), 0],
                                            rstd[:, bass.ds(t, 1)], ALU.subtract, ALU.mult).then_inc(xn_done, 1)
            for g in range(NKV0):
                dve.wait_ge(hi_done, g + 1)
                nc.vector.tensor_tensor(k.wa_lo[:, g, :], raw[:, g % 2, :], k.wa_hi[:, g, :].bitcast(F32),
                                        ALU.subtract).then_inc(lo_done, 1)

        @block.tensor
        def _(pe):
            pe.wait_ge(ident_done, 1)
            with pe.Fori(0, B // 2) as i:
                for j in range(2):
                    pe.wait_ge(xn_done, i * 2 + (j + 1))
                    for c in range(KC):
                        last = nc.tensor.transpose(bank[j][:, c * P:(c + 1) * P], xn[:, j, c * P:(c + 1) * P], k.ident[:, :])
                    last.then_inc(xt_done, 1)

        @block.scalar
        def _(act):
            act.dma_start(k.ctx_t[:, :, :], io["ctx_t"]).then_inc(s_ctx, 16)
            act.dma_start(k.mask[:, :], io["mask"][0]).then_inc(s_mask, 16)
            act.dma_start(k.bias_a[:, :], io["bias_a"].partition_broadcast(P)).then_inc(s_bias, 16)
            act.dma_start(k.norm_w[:, :], io["norm_w"]).then_inc(s_norm_w, 16)
            with act.Fori(0, B // 2) as i:
                for j in range(2):
                    act.wait_ge(xt_done, i * 2 + (j + 1))
                    nc.scalar.activation(k.xn_t[:, :, cols(i * 2 + j, 0, P)], bank[j][:, 0:D].rearrange("p (c n) -> p c n", c=KC),
                                         ACT.Copy).then_inc(xt_read, 1)
            for g in range(NKV0):
                act.wait_ge(s_raw[g % 2], 16 * (g // 2 + 1))
                nc.scalar.activation(k.wa_hi[:, g, :], raw[:, g % 2, :], ACT.Copy).then_inc(hi_done, 1)
            act.wait_ge(s_ctx, 16)
            act.wait_ge(s_mask, 16)
            act.wait_ge(s_bias, 16)


def layer0_attention(nc, io, k):
    with ExitStack() as ctx:
        m = Mem(nc, ctx)
        ps_s, ps_q, ps_kv, ps_pt, ps_qt, ps_kt, ps_o, ps_y = banks(k)
        xh, xl, ch, cl = (m.sb(f"b_{n}", [P, KC, P], F32R) for n in ("xh", "xl", "ch", "cl"))
        qkv = m.sb("b_qkv", [P, 2, 6 * P])
        sq = m.sb("b_sq", [P, 5 * P])
        ssum = m.sb("b_ssum", [P, 5])
        sume = m.sb("b_sume", [P, 5])
        rnorm = m.sb("b_rnorm", [P, NKV0, 5])
        kn = m.sb("b_kn", [P, P])
        qt = m.sb("b_qt", [P, NKV0, GH * P])
        kt = m.sb("b_kt", [P, NKV0, P])
        v = m.sb("b_v", [P, NKV0, P])
        sc = m.sb("b_sc", [P, GH * P])
        nmax = m.sb("b_nmax", [P, GH])
        prob = m.sb("b_prob", [P, GH * P])
        rsum = m.sb("b_rsum", [P, GH])
        rinv = m.sb("b_rinv", [P, GH])
        probn = m.sb("b_probn", [P, GH * P])
        pt = m.sb("b_pt", [P, GH * P])
        oh = m.sb("b_oh", [P, GH * P], F32R)
        ol = m.sb("b_ol", [P, GH * P], F32R)
        ahead = ("qkv_ready", "pt_ready", "ol_ready", "scores_read", "y_added", "exp_done", "sq_done", "qt_ready",
                 "kt_ready", "q_turned", "k_turned", "pv_done", "wo_done", "p_turned", "probn_done", "kn_done",
                 "v_ready", "ssum_done", "rnorm_done")
        plain = ("slot_hi", "slot_lo", "proj_done", "sume_done", "scores_done", "nmax_done", "rinv_done", "oh_ready")
        s = {n: m.sem(f"b_{n}") for n in ahead + plain}
        block = ctx.enter_context(nc.Block())

        def done(eng, name, n):
            eng.wait_ge(s[name], n + (2 if name in ahead else 1))

        def freed(eng, name, n):
            eng.wait_ge(s[name], n + 1)

        def start_ahead(eng, *names):
            for name in names:
                eng.sem_inc(s[name], 1)

        def stage(b, g, lag, work):
            b, g = (b, g - lag) if g >= lag else (b - 1, g - lag + NKV0)
            if type(b) is not int or 0 <= b < B:
                work(b, g, b * NKV0 + g)

        def program(eng, step, before=None):
            for b in (-1, 0):
                if before:
                    before(b + 1)
                for g in range(NKV0):
                    step(b, g)
            with eng.Fori(1, B - 1) as b:
                if before:
                    before(b + 1)
                for g in range(NKV0):
                    step(b, g)
            for g in range(NKV0):
                step(B - 1, g)
            for g in range(2):
                step(B, g)

        @block.tensor
        def _(pe):
            def scores(b, g, n):
                done(pe, "qt_ready", n)
                done(pe, "kt_ready", n)
                freed(pe, "scores_read", n)
                for r in range(GH):
                    last = nc.tensor.matmul(ps_s[:, r * P:(r + 1) * P], qt[:, g, r * P:(r + 1) * P], kt[:, g, :],
                                            start=True, stop=True)
                last.then_inc(s["scores_done"], 1)

            def turn_probs(b, g, n):
                done(pe, "probn_done", n)
                freed(pe, "pt_ready", n)
                for r in range(GH):
                    last = nc.tensor.transpose(ps_pt[:, r * P:(r + 1) * P], probn[:, r * P:(r + 1) * P], k.ident[:, :])
                last.then_inc(s["p_turned"], 1)

            def attend(b, g, n):
                done(pe, "pt_ready", n)
                done(pe, "v_ready", n)
                freed(pe, "ol_ready", n)
                nc.tensor.matmul(ps_o[:, :], v[:, g, :], pt[:, :], start=True, stop=True).then_inc(s["pv_done"], 1)

            def out_proj(b, g, n):
                done(pe, "ol_ready", n)
                if g == 0:
                    freed(pe, "y_added", b)
                for r in range(GH):
                    w_hi = k.wa_hi[:, g, WO_AT + r * D:WO_AT + (r + 1) * D]
                    w_lo = k.wa_lo[:, g, WO_AT + r * D:WO_AT + (r + 1) * D]
                    o_hi, o_lo = oh[:, r * P:(r + 1) * P], ol[:, r * P:(r + 1) * P]
                    nc.tensor.matmul(ps_y[:, 0:D], o_hi, w_hi, start=g == 0 and r == 0, stop=False)
                    nc.tensor.matmul(ps_y[:, 0:D], o_hi, w_lo, start=False, stop=False)
                    last = nc.tensor.matmul(ps_y[:, 0:D], o_lo, w_hi, start=False, stop=g == NKV0 - 1 and r == GH - 1)
                last.then_inc(s["wo_done"], 1)

            def project(b, g, n):
                if g == 0:
                    done(pe, "slot_hi", b)
                    done(pe, "slot_lo", b)
                freed(pe, "qkv_ready", n)
                for ps, a_hi, a_lo, at, w in ((ps_q, xh, xl, WQ_AT, GH * HD0), (ps_kv, ch, cl, WKV_AT, 2 * HD0)):
                    for c in range(KC):
                        w_hi = k.wa_hi[:, g, at + c * w:at + (c + 1) * w]
                        w_lo = k.wa_lo[:, g, at + c * w:at + (c + 1) * w]
                        nc.tensor.matmul(ps[:, 0:w], a_hi[:, c, :], w_hi, start=c == 0, stop=False)
                        nc.tensor.matmul(ps[:, 0:w], a_hi[:, c, :], w_lo, start=False, stop=False)
                        last = nc.tensor.matmul(ps[:, 0:w], a_lo[:, c, :], w_hi, start=False, stop=c == KC - 1)
                last.then_inc(s["proj_done"], 1)

            def turn_q(b, g, n):
                done(pe, "qkv_ready", n)
                freed(pe, "qt_ready", n)
                for r in range(GH):
                    last = nc.tensor.transpose(ps_qt[:, r * P:(r + 1) * P], qkv[:, g % 2, r * P:(r + 1) * P], k.ident[:, :])
                last.then_inc(s["q_turned"], 1)

            def turn_k(b, g, n):
                done(pe, "kn_done", n)
                freed(pe, "kt_ready", n)
                nc.tensor.transpose(ps_kt[:, 0:P], kn[:, :], k.ident[:, :]).then_inc(s["k_turned"], 1)

            def step(b, g):
                stage(b, g, 0, scores)
                stage(b, g, 1, turn_probs)
                stage(b + 1, g, 1, turn_q)
                stage(b + 1, g, 0, project)
                stage(b, g, 1, attend)
                stage(b, g, 2, out_proj)
                stage(b + 1, g, 1, turn_k)

            start_ahead(pe, "q_turned", "k_turned", "pv_done", "wo_done", "p_turned")
            program(pe, step)

        @block.vector
        def _(dve):
            def before(b):
                if type(b) is not int or b < B:
                    done(dve, "slot_hi", b)
                    nc.vector.tensor_tensor(xl[:, :, :], k.xn_t[:, :, cols(b, 0, P)], xh[:, :, :].bitcast(F32), ALU.subtract)
                    nc.vector.tensor_tensor(cl[:, :, :], k.ctx_t[:, :, cols(b, 0, P)], ch[:, :, :].bitcast(F32),
                                            ALU.subtract).then_inc(s["slot_lo"], 1)

            def masked_scores(b, g, n):
                done(dve, "scores_done", n)
                done(dve, "rnorm_done", n)
                freed(dve, "exp_done", n)
                for r in range(GH):
                    last = nc.vector.scalar_tensor_tensor(sc[:, r * P:(r + 1) * P], ps_s[:, r * P:(r + 1) * P],
                                                          rnorm[:, g, r:r + 1], k.mask[:, :], ALU.mult, ALU.add)
                last.then_inc(s["scores_read"], 1)
                done(dve, "scores_read", n)
                nc.vector.tensor_reduce(nmax[:, :], sc[:, :].rearrange("p (r e) -> p r e", r=GH), AX_X, ALU.max,
                                        negate=True).then_inc(s["nmax_done"], 1)

            def invert_sums(b, g, n):
                done(dve, "exp_done", n)
                freed(dve, "probn_done", n)
                nc.vector.reciprocal(rinv[:, :], rsum[:, :]).then_inc(s["rinv_done"], 1)

            def keep_probs(b, g, n):
                done(dve, "p_turned", n)
                freed(dve, "pv_done", n)
                nc.vector.tensor_copy(pt[:, :], ps_pt[:, :]).then_inc(s["pt_ready"], 1)

            def low_part_of_out(b, g, n):
                done(dve, "oh_ready", n)
                freed(dve, "wo_done", n)
                nc.vector.tensor_tensor(ol[:, :], ps_o[:, :], oh[:, :].bitcast(F32), ALU.subtract).then_inc(s["ol_ready"], 1)

            def add_out(b, g, n):
                if g == NKV0 - 1:
                    done(dve, "wo_done", n)
                    x_b = k.x_res[:, bass.ds(b, 1), :].rearrange("p o d -> p (o d)")
                    nc.vector.tensor_tensor(x_b, x_b, ps_y[:, 0:D], ALU.add).then_inc(s["y_added"], 1)

            def add_bias(b, g, n):
                done(dve, "proj_done", n)
                if type(b) is not int or n >= 2:
                    freed(dve, "q_turned", n - 1)
                    freed(dve, "kn_done", n - 1)
                    freed(dve, "v_ready", n - 1)
                bias = k.bias_a[:, g * 6 * P:(g + 1) * 6 * P]
                nc.vector.tensor_tensor(qkv[:, g % 2, 0:4 * P], ps_q[:, :], bias[:, 0:4 * P], ALU.add)
                nc.vector.tensor_tensor(qkv[:, g % 2, 4 * P:6 * P], ps_kv[:, 0:2 * P], bias[:, 4 * P:6 * P],
                                        ALU.add).then_inc(s["qkv_ready"], 1)

            def sum_squares(b, g, n):
                done(dve, "sq_done", n)
                freed(dve, "rnorm_done", n)
                nc.vector.tensor_reduce(ssum[:, :], sq[:, :].rearrange("p (r e) -> p r e", r=5), AX_X,
                                        ALU.add).then_inc(s["ssum_done"], 1)

            def step(b, g):
                stage(b, g, 0, masked_scores)
                stage(b, g, 1, keep_probs)
                stage(b + 1, g, 1, sum_squares)
                stage(b, g, 0, invert_sums)
                stage(b + 1, g, 0, add_bias)
                stage(b, g, 1, low_part_of_out)
                stage(b, g, 2, add_out)

            start_ahead(dve, "qkv_ready", "pt_ready", "ol_ready", "scores_read", "y_added", "ssum_done")
            program(dve, step, before)

        @block.scalar
        def _(act):
            def before(b):
                if type(b) is not int or 0 < b < B:
                    act.wait_ge(s["proj_done"], b * NKV0)
                if type(b) is not int or b < B:
                    nc.scalar.activation(xh[:, :, :], k.xn_t[:, :, cols(b, 0, P)], ACT.Copy)
                    nc.scalar.activation(ch[:, :, :], k.ctx_t[:, :, cols(b, 0, P)], ACT.Copy).then_inc(s["slot_hi"], 1)

            def exps(b, g, n):
                done(act, "nmax_done", n)
                freed(act, "probn_done", n)
                for r in range(GH):
                    last = nc.scalar.activation(prob[:, r * P:(r + 1) * P], sc[:, r * P:(r + 1) * P], ACT.Exp,
                                                bias=nmax[:, r:r + 1], accum_out=rsum[:, r:r + 1])
                last.then_inc(s["exp_done"], 1)

            def high_part_of_out(b, g, n):
                done(act, "pv_done", n)
                freed(act, "wo_done", n)
                nc.scalar.activation(oh[:, :], ps_o[:, :], ACT.Copy).then_inc(s["oh_ready"], 1)

            def squares(b, g, n):
                done(act, "qkv_ready", n)
                freed(act, "ssum_done", n)
                nc.scalar.activation(sq[:, :], qkv[:, g % 2, 0:5 * P], ACT.Square).then_inc(s["sq_done"], 1)

            def keep_q(b, g, n):
                done(act, "q_turned", n)
                nc.scalar.activation(qt[:, g, :], ps_qt[:, :], ACT.Copy).then_inc(s["qt_ready"], 1)

            def keep_k(b, g, n):
                done(act, "k_turned", n)
                nc.scalar.activation(kt[:, g, :], ps_kt[:, 0:P], ACT.Copy, scale=k.key_scale[:, 0:1]).then_inc(s["kt_ready"], 1)

            def keep_v(b, g, n):
                if type(b) is not int or b > 0:
                    done(act, "pv_done", n - NKV0)
                nc.scalar.activation(v[:, g, :], qkv[:, g % 2, 5 * P:6 * P], ACT.Copy).then_inc(s["v_ready"], 1)

            def step(b, g):
                stage(b + 1, g, 2, keep_k)
                stage(b + 1, g, 1, keep_q)
                stage(b, g, 0, exps)
                stage(b, g, 1, high_part_of_out)
                stage(b + 1, g, 1, keep_v)
                stage(b + 1, g, 0, squares)

            start_ahead(act, "exp_done", "sq_done", "qt_ready", "kt_ready", "v_ready")
            program(act, step, before)

        @block.gpsimd
        def _(pool):
            def inverse_norms(b, g, n):
                done(pool, "ssum_done", n)
                nc.gpsimd.tensor_tensor(sume[:, :], ssum[:, :], k.eps_a[:, :], ALU.add).then_inc(s["sume_done"], 1)
                done(pool, "sume_done", n)
                nc.gpsimd.tensor_tensor(rnorm[:, g, :], sume[:, :], k.neg_half[:, 0:5], ALU.pow).then_inc(s["rnorm_done"], 1)
                done(pool, "rnorm_done", n)
                freed(pool, "k_turned", n)
                nc.gpsimd.tensor_tensor(kn[:, :], qkv[:, g % 2, 4 * P:5 * P], rnorm[:, g, 4:5].broadcast_to([P, P]),
                                        ALU.mult).then_inc(s["kn_done"], 1)

            def normed_probs(b, g, n):
                done(pool, "rinv_done", n)
                freed(pool, "p_turned", n)
                nc.gpsimd.tensor_tensor(probn[:, :].rearrange("p (r e) -> p r e", r=GH),
                                        prob[:, :].rearrange("p (r e) -> p r e", r=GH),
                                        rinv[:, :].rearrange("p (r o) -> p r o", o=1).broadcast_to([P, GH, P]),
                                        ALU.mult).then_inc(s["probn_done"], 1)

            def step(b, g):
                stage(b + 1, g, 1, inverse_norms)
                stage(b, g, 0, normed_probs)

            start_ahead(pool, "probn_done", "kn_done", "rnorm_done")
            program(pool, step)


def router(nc, io, k):
    with ExitStack() as ctx:
        m = Mem(nc, ctx)
        bank = banks(k, 0, 5)
        ps_logit, ps_comb = bank[2], bank[3:5]
        stats = m.sb("c_stats", [P, B, 6])
        mv = m.sb("c_mv", [P, B, 2])
        vpe = m.sb("c_vpe", [P, B])
        rstd = m.sb("c_rstd", [P, B])
        xn = m.sb("c_xn", [P, 2, D])
        gw = m.sb("c_gw", [P, KC, NE])
        gw_hi = m.sb("c_gw_hi", [P, KC, NE], F32R)
        gw_lo = m.sb("c_gw_lo", [P, KC, NE], F32R)
        nmax = m.sb("c_nmax", [P, B])
        logit = m.sb("c_logit", [P, B, NE])
        ex = m.sb("c_ex", [P, B, NE])
        esum = m.sb("c_esum", [P, B])
        einv = m.sb("c_einv", [P, B])
        prob = m.sb("c_prob", [P, B, NE + TOPK])
        top = m.sb("c_top", [P, B, TOPK])
        tsum = m.sb("c_tsum", [P, 2, B])
        tinv = m.sb("c_tinv", [P, 2, B])
        cum = m.sb("c_cum", [P, B, TOPK])
        kept = m.sb("c_kept", [P, B, TOPK])
        left = m.sb("c_left", [P, B, TOPK])
        find = m.sb("c_find", [P, B, TOPK])
        rest = m.sb("c_rest", [P, B, NE + TOPK])
        sel = m.sb("c_sel", [P, B, NE])
        comb = m.sb("c_comb", [P, B, NE])
        comb_t = m.sb("c_comb_t", [NE, T])
        names = ("gw_loaded", "gw_hi", "gw_lo", "stats", "mv", "vpe", "rstd", "xn_ready", "x_turned", "x_hi", "x_lo",
                 "logits", "exps", "probs", "comb_ready", "comb_turned", "comb_kept", "comb_stored", "chain")
        s = {n: m.sem(f"c_{n}") for n in names}
        block = ctx.enter_context(nc.Block())

        @block.sync
        def _(sp):
            sp.dma_start(gw[:, :, :], io["gate_t"]).then_inc(s["gw_loaded"], 16)
            sp.wait_ge(s["comb_kept"], 2)
            sp.dma_start(k.comb_dram, comb_t[:, :]).then_inc(s["comb_stored"], 16)
            sp.wait_ge(s["comb_stored"], 16)

        @block.gpsimd
        def _(pool):
            pool.wait_ge(s["mv"], B)
            nc.gpsimd.tensor_scalar(vpe[:, :], mv[:, :, 1], 1e-5, None, ALU.add).then_inc(s["vpe"], 1)
            pool.wait_ge(s["vpe"], 1)
            nc.gpsimd.tensor_tensor(rstd[:, :], vpe[:, :], k.neg_half[:, 0:B], ALU.pow).then_inc(s["rstd"], 1)

        @block.vector
        def _(dve):
            for t in range(B):
                nc.vector.bn_stats(stats[:, t, :], k.x_res[:, t, :]).then_inc(s["stats"], 1)
            for t in range(B):
                dve.wait_ge(s["stats"], t + 1)
                nc.vector.bn_aggr(mv[:, t, :], stats[:, t, :]).then_inc(s["mv"], 1)
            nc.vector.memset(prob[:, :, NE:], -1.0)
            dve.wait_ge(s["gw_hi"], 1)
            nc.vector.tensor_tensor(gw_lo[:, :, :], gw[:, :, :], gw_hi[:, :, :].bitcast(F32), ALU.subtract).then_inc(s["gw_lo"], 1)
            dve.wait_ge(s["rstd"], 1)

            def low(t, j):
                dve.wait_ge(s["x_hi"], t + 1)
                at = k.xn_hi[:, :, cols(t, 0, P)]
                nc.vector.tensor_tensor(k.xn_lo[:, :, cols(t, 0, P)], bank[j][:, 0:D].rearrange("p (c n) -> p c n", c=KC),
                                        at.bitcast(F32), ALU.subtract).then_inc(s["x_lo"], 1)

            def norm(t, j):
                nc.vector.tensor_scalar(xn[:, j, :], k.x_res[:, bass.ds(t, 1), :].rearrange("p o d -> p (o d)"),
                                        mv[:, bass.ds(t, 1), 0], rstd[:, bass.ds(t, 1)],
                                        ALU.subtract, ALU.mult).then_inc(s["xn_ready"], 1)

            norm(0, 0)
            norm(1, 1)
            with dve.Fori(0, B // 2 - 1) as i:
                for j in range(2):
                    low(i * 2 + j, j)
                    norm(i * 2 + (j + 2), j)
            low(B - 2, 0)
            low(B - 1, 1)

            at = [0]

            def chained(ins):
                at[0] += 1
                ins.then_inc(s["chain"], 1)
                dve.wait_ge(s["chain"], at[0])

            wide = [P, B, NE]
            by_token = lambda a, n: a.rearrange("p (b o) -> p b o", o=1).broadcast_to([P, B, n])
            logits = ps_logit[:, 0:B * NE].rearrange("p (b e) -> p b e", b=B)
            dve.wait_ge(s["logits"], 1)
            chained(nc.vector.tensor_reduce(nmax[:, :], logits, AX_X, ALU.max, negate=True))
            nc.vector.tensor_tensor(logit[:, :, :], logits, by_token(nmax[:, :], NE), ALU.add).then_inc(s["probs"], 1)
            dve.wait_ge(s["exps"], 1)
            chained(nc.vector.tensor_reduce(esum[:, :], ex[:, :, :], AX_X, ALU.add))
            chained(nc.vector.reciprocal(einv[:, :], esum[:, :]))
            chained(nc.vector.tensor_tensor(prob[:, :, 0:NE], ex[:, :, :], by_token(einv[:, :], NE), ALU.mult))
            for t in range(B):
                last = nc.vector.max(top[:, t, :], prob[:, t, 0:NE])
            chained(last)
            chained(nc.vector.tensor_reduce(tsum[:, 0, :], top[:, :, :], AX_X, ALU.add))
            chained(nc.vector.tensor_scalar(tsum[:, 0, :], tsum[:, 0, :], 1e-12, None, ALU.max))
            chained(nc.vector.reciprocal(tinv[:, 0, :], tsum[:, 0, :]))
            chained(nc.vector.tensor_tensor(cum[:, :, :], top[:, :, :], by_token(tinv[:, 0, :], TOPK), ALU.mult))
            for j in range(1, TOPK):
                chained(nc.vector.tensor_tensor(cum[:, :, j], cum[:, :, j - 1], cum[:, :, j], ALU.add))
            nc.vector.tensor_copy(kept[:, :, 0], top[:, :, 0])
            nc.vector.tensor_copy(find[:, :, 0], top[:, :, 0])
            nc.vector.tensor_scalar(left[:, :, 1:], cum[:, :, 0:TOPK - 1], THRESHOLD, 1.0, ALU.is_lt, ALU.subtract)
            chained(nc.vector.scalar_tensor_tensor(kept[:, :, 1:], cum[:, :, 0:TOPK - 1], THRESHOLD, top[:, :, 1:],
                                                   ALU.is_lt, ALU.mult))
            nc.vector.tensor_tensor(find[:, :, 1:], kept[:, :, 1:], left[:, :, 1:], ALU.add)
            chained(nc.vector.tensor_reduce(tsum[:, 1, :], kept[:, :, :], AX_X, ALU.add))
            chained(nc.vector.tensor_scalar(tsum[:, 1, :], tsum[:, 1, :], 1e-12, None, ALU.max))
            chained(nc.vector.reciprocal(tinv[:, 1, :], tsum[:, 1, :]))
            for t in range(B):
                last = nc.vector.match_replace(rest[:, t, :], find[:, t, :], prob[:, t, :], -2.0)
            chained(last)
            chained(nc.vector.tensor_tensor(sel[:, :, :], rest[:, :, 0:NE], prob[:, :, 0:NE], ALU.not_equal))
            chained(nc.vector.tensor_tensor(sel[:, :, :], sel[:, :, :], prob[:, :, 0:NE], ALU.mult))
            nc.vector.tensor_tensor(comb[:, :, :], sel[:, :, :], by_token(tinv[:, 1, :], NE), ALU.mult).then_inc(s["comb_ready"], 1)
            dve.wait_ge(s["comb_turned"], 1)
            nc.vector.tensor_copy(comb_t[:, 0:T // 2], ps_comb[0][0:NE, :]).then_inc(s["comb_kept"], 1)

        @block.scalar
        def _(act):
            act.wait_ge(s["gw_loaded"], 16)
            nc.scalar.activation(gw_hi[:, :, :], gw[:, :, :], ACT.Copy).then_inc(s["gw_hi"], 1)
            with act.Fori(0, B // 2) as i:
                for j in range(2):
                    act.wait_ge(s["x_turned"], i * 2 + (j + 1))
                    nc.scalar.activation(k.xn_hi[:, :, cols(i * 2 + j, 0, P)], bank[j][:, 0:D].rearrange("p (c n) -> p c n", c=KC),
                                         ACT.Copy).then_inc(s["x_hi"], 1)
            act.wait_ge(s["probs"], 1)
            nc.scalar.activation(ex[:, :, :], logit[:, :, :], ACT.Exp).then_inc(s["exps"], 1)
            act.wait_ge(s["comb_turned"], 1)
            nc.scalar.activation(comb_t[:, T // 2:], ps_comb[1][0:NE, :], ACT.Copy).then_inc(s["comb_kept"], 1)

        @block.tensor
        def _(pe):
            def turn(t, j):
                pe.wait_ge(s["xn_ready"], t + 1)
                for c in range(KC):
                    last = nc.tensor.transpose(bank[j][:, c * P:(c + 1) * P], xn[:, j, c * P:(c + 1) * P], k.ident[:, :])
                last.then_inc(s["x_turned"], 1)

            turn(0, 0)
            turn(1, 1)
            with pe.Fori(1, B // 2) as i:
                for j in range(2):
                    pe.wait_ge(s["x_lo"], i * 2 + (j - 1))
                    turn(i * 2 + j, j)
            pe.wait_ge(s["gw_lo"], 1)
            pe.wait_ge(s["x_lo"], B)
            for t in range(B):
                out = ps_logit[:, t * NE:(t + 1) * NE]
                for c in range(KC):
                    x_hi, x_lo = k.xn_hi[:, c, t * P:(t + 1) * P], k.xn_lo[:, c, t * P:(t + 1) * P]
                    nc.tensor.matmul(out, x_hi, gw_hi[:, c, :], start=c == 0, stop=False)
                    nc.tensor.matmul(out, x_hi, gw_lo[:, c, :], start=False, stop=False)
                    last = nc.tensor.matmul(out, x_lo, gw_hi[:, c, :], start=False, stop=c == KC - 1)
            last.then_inc(s["logits"], 1)
            pe.wait_ge(s["comb_ready"], 1)
            for t in range(B):
                last = nc.tensor.transpose(ps_comb[t // 4][0:NE, t % 4 * P:(t % 4 + 1) * P], comb[:, t, :], k.ident[:, :])
            last.then_inc(s["comb_turned"], 1)


def experts(nc, io, k):
    with ExitStack() as ctx:
        m = Mem(nc, ctx)
        ps_g, ps_u = banks(k, 0, 2), banks(k, 2, 2)
        acc = banks(k, 4, 4)
        HALF = T // 2
        raw = m.sb("d_raw", [P, 3, WM])
        w_hi = m.sb("d_w_hi", [P, 3, WM], F32R)
        w_lo = m.sb("d_w_lo", [P, 3, WM], F32R)
        weight = m.sb("d_weight", [P, 3, T])
        silu = m.sb("d_silu", [P, 2, HALF])
        gu = m.sb("d_gu", [P, 2, HALF])
        h = m.sb("d_h", [P, 2, HALF])
        h_hi = m.sb("d_h_hi", [P, 2, HALF], F32R)
        h_lo = m.sb("d_h_lo", [P, 2, HALF], F32R)
        y_t = m.sb("d_y_t", [P, KC, T])
        ahead = ("gu_done", "h_done", "down_done", "lo_done", "h_lo_done")
        plain = ("gate_up_done", "silu_done", "h_hi_done", "hi_done", "acc_kept", "y_turned", "y_added")
        s = {n: m.sem(f"d_{n}") for n in ahead + plain}
        w_loaded = [m.sem(f"d_w_loaded{j}") for j in range(3)]
        weight_loaded = [m.sem(f"d_weight_loaded{j}") for j in range(3)]
        block = ctx.enter_context(nc.Block())
        SEGMENTS = [(j, max(q * INTER, j * P) - j * P, min((q + 1) * INTER, (j + 1) * P) - j * P, q)
                    for j in range(3) for q in range(4) if q * INTER < (j + 1) * P and (q + 1) * INTER > j * P]

        def done(eng, name, n):
            eng.wait_ge(s[name], n + (2 if name in ahead else 1))

        def freed(eng, name, n):
            if type(n) is not int or n >= 2:
                eng.wait_ge(s[name], n)

        def stage(i, u, lag, work):
            i, u = (i, u - lag) if u >= lag else (i - 1, u - lag + 6)
            if type(i) is not int or 0 <= i < MT // 3:
                work(i, u // 2, u % 2, i * 6 + u)

        def program(eng, step):
            for u in range(6):
                step(0, u)
            with eng.Fori(1, MT // 3 - 1) as i:
                for u in range(6):
                    step(i, u)
            for i, steps in ((MT // 3 - 1, 6), (MT // 3, 2)):
                for u in range(steps):
                    step(i, u)

        def next_tile(i, u, work):
            j = u // 2 + 1
            if u % 2 == 1 and not (type(i) is int and i * 3 + j >= MT):
                work(*((i, j) if j < 3 else (i + 1, 0)))

        @block.sync
        def _(sp):
            def load(i, j):
                if type(i) is not int:
                    sp.wait_ge(s["lo_done"], i * 3 + (j - 1))
                sp.dma_start(raw[:, j, :], io["wm"][bass.ds(i * 3 + j, 1)].rearrange("o p n -> p (o n)")
                             ).then_inc(w_loaded[j], 16)
                if type(i) is not int:
                    sp.wait_ge(s["h_done"], i * 6 + (2 * j - 3))
                for jj, a, b, q in SEGMENTS:
                    if jj == j:
                        sp.dma_start(weight[a:b, j, :], k.comb_dram[bass.ds(i * 4 + q, 1), :].broadcast_to([b - a, T])
                                     ).then_inc(weight_loaded[j], 16)

            for j in range(3):
                load(0, j)
            with sp.Fori(1, MT // 3) as i:
                for j in range(3):
                    load(i, j)

        @block.tensor
        def _(pe):
            def gate_up(i, j, half, n):
                if half == 0:
                    done(pe, "lo_done", i * 3 + j)
                freed(pe, "gu_done", n)
                for ps, at in ((ps_g[half], 0), (ps_u[half], KC * P)):
                    for c in range(KC):
                        hi, lo = (w[:, j, at + c * P:at + (c + 1) * P] for w in (w_hi, w_lo))
                        x_hi, x_lo = (x[:, c, half * HALF:(half + 1) * HALF] for x in (k.xn_hi, k.xn_lo))
                        nc.tensor.matmul(ps[:, :], hi, x_hi, start=c == 0, stop=False)
                        nc.tensor.matmul(ps[:, :], hi, x_lo, start=False, stop=False)
                        last = nc.tensor.matmul(ps[:, :], lo, x_hi, start=False, stop=c == KC - 1)
                last.then_inc(s["gate_up_done"], 1)

            def down(i, j, half, n):
                done(pe, "h_lo_done", n)
                first = type(i) is int and i == 0 and j == 0
                for c in range(KC):
                    hi, lo = (w[:, j, 2 * KC * P + c * P:2 * KC * P + (c + 1) * P] for w in (w_hi, w_lo))
                    out = acc[2 * c + half]
                    nc.tensor.matmul(out[:, :], hi, h_hi[:, half, :], start=first, stop=False, skip_group_check=True)
                    nc.tensor.matmul(out[:, :], hi, h_lo[:, half, :], start=False, stop=False, skip_group_check=True)
                    last = nc.tensor.matmul(out[:, :], lo, h_hi[:, half, :], start=False, stop=True, skip_group_check=True)
                last.then_inc(s["down_done"], 1)

            def step(i, u):
                stage(i, u, 0, gate_up)
                stage(i, u, 2, down)

            pe.sem_inc(s["down_done"], 1)
            program(pe, step)
            pe.wait_ge(s["acc_kept"], 4)
            for t in range(B):
                if t >= 4:
                    pe.wait_ge(s["y_added"], t - 3)
                ps = (ps_g + ps_u)[t % 4]
                for c in range(KC):
                    last = nc.tensor.transpose(ps[:, c * P:(c + 1) * P], y_t[:, c, t * P:(t + 1) * P], k.ident[:, :])
                last.then_inc(s["y_turned"], 1)

        @block.scalar
        def _(act):
            def hi_part(i, j):
                act.wait_ge(w_loaded[j], i * 16 + 16)
                if type(i) is not int or i > 0:
                    act.wait_ge(s["down_done"], i * 6 + (2 * j - 3))
                nc.scalar.activation(w_hi[:, j, :], raw[:, j, :], ACT.Copy).then_inc(s["hi_done"], 1)

            def silus(i, j, half, n):
                done(act, "gate_up_done", n)
                freed(act, "gu_done", n)
                nc.scalar.activation(silu[:, half, :], ps_g[half][:, :], ACT.Silu).then_inc(s["silu_done"], 1)

            def h_high(i, j, half, n):
                done(act, "h_done", n)
                freed(act, "down_done", n)
                nc.scalar.activation(h_hi[:, half, :], h[:, half, :], ACT.Copy).then_inc(s["h_hi_done"], 1)

            def step(i, u):
                stage(i, u, 0, silus)
                stage(i, u, 1, h_high)
                next_tile(i, u, hi_part)

            hi_part(0, 0)
            program(act, step)
            done(act, "down_done", 2 * MT - 1)
            for n in (2, 3):
                nc.scalar.activation(y_t[:, n // 2, n % 2 * HALF:(n % 2 + 1) * HALF], acc[n][:, :], ACT.Copy).then_inc(s["acc_kept"], 1)

        @block.vector
        def _(dve):
            def lo_part(i, j):
                dve.wait_ge(s["hi_done"], i * 3 + (j + 1))
                nc.vector.tensor_tensor(w_lo[:, j, :], raw[:, j, :], w_hi[:, j, :].bitcast(F32),
                                        ALU.subtract).then_inc(s["lo_done"], 1)

            def gate_times_up(i, j, half, n):
                done(dve, "silu_done", n)
                freed(dve, "h_done", n)
                nc.vector.tensor_tensor(gu[:, half, :], silu[:, half, :], ps_u[half][:, :], ALU.mult).then_inc(s["gu_done"], 1)

            def h_low(i, j, half, n):
                done(dve, "h_hi_done", n)
                nc.vector.tensor_tensor(h_lo[:, half, :], h[:, half, :], h_hi[:, half, :].bitcast(F32),
                                        ALU.subtract).then_inc(s["h_lo_done"], 1)

            def step(i, u):
                stage(i, u, 0, gate_times_up)
                stage(i, u, 1, h_low)
                next_tile(i, u, lo_part)

            dve.sem_inc(s["gu_done"], 1)
            dve.sem_inc(s["lo_done"], 1)
            dve.sem_inc(s["h_lo_done"], 1)
            lo_part(0, 0)
            program(dve, step)
            done(dve, "down_done", 2 * MT - 1)
            for n in (0, 1):
                nc.vector.tensor_copy(y_t[:, n // 2, n % 2 * HALF:(n % 2 + 1) * HALF], acc[n][:, :]).then_inc(s["acc_kept"], 1)
            for t in range(B):
                dve.wait_ge(s["y_turned"], t + 1)
                nc.vector.tensor_tensor(k.x_res[:, t, :], k.x_res[:, t, :], (ps_g + ps_u)[t % 4][:, 0:D],
                                        ALU.add).then_inc(s["y_added"], 1)

        @block.gpsimd
        def _(pool):
            def weigh(i, j, half, n):
                done(pool, "gu_done", n)
                if half == 0:
                    pool.wait_ge(weight_loaded[j], i * 32 + 32)
                freed(pool, "h_lo_done", n)
                nc.gpsimd.tensor_tensor(h[:, half, :], gu[:, half, :], weight[:, j, half * HALF:(half + 1) * HALF],
                                        ALU.mult).then_inc(s["h_done"], 1)

            pool.sem_inc(s["h_done"], 1)
            program(pool, lambda i, u: stage(i, u, 0, weigh))


def layer1_weights(nc, io, k):
    with ExitStack() as ctx:
        m = Mem(nc, ctx)
        bank = banks(k)
        wqp = m.sb("e_wqp", [P, 2 * KC, D])
        amax = m.sb("e_amax", [P, 2 * KC])
        scale = m.sb("e_scale", [P, 2 * KC])
        inv = m.sb("e_inv", [P, 2 * KC])
        rounded = m.sb("e_rounded", [P, 2 * KC, D])
        scale_cols = m.sb("e_scale_cols", [P, 2 * KC, P])
        wkv = m.sb("e_wkv", [P, KC, 2 * D])
        wkv_hi = m.sb("e_wkv_hi", [P, KC, 2 * D], F32R)
        wkv_lo = m.sb("e_wkv_lo", [P, KC, 2 * D], F32R)
        ctx_hi = m.sb("e_ctx_hi", [P, KC, T], F32R)
        ctx_lo = m.sb("e_ctx_lo", [P, KC, T], F32R)
        bk = m.sb("e_bk", [P, KC])
        bv = m.sb("e_bv", [P, D])
        wf = m.sb("e_wf", [P, 3, KC * HIDDEN])
        wr = m.sb("e_wr", [P, KC * HIDDEN])
        wsum = m.sb("e_wsum", [P, 3])
        ones = m.sb("e_ones", [P, P])
        ginv = m.sb("e_ginv", [P, 3])
        names = ("bk_loaded", "bv_loaded", "wqp_loaded", "wkv_loaded", "bias_loaded", "hi", "lo", "keys", "keys_kept",
                 "values", "values_kept", "chain", "rounded", "turned", "turned_kept", "scale_cols", "scales", "sums",
                 "gamma", "clipped", "ternary")
        s = {n: m.sem(f"e_{n}") for n in names}
        wf_loaded = [m.sem(f"e_wf_loaded{j}") for j in range(3)]
        block = ctx.enter_context(nc.Block())

        @block.sync
        def _(sp):
            sp.dma_start(wkv[:, :, :], io["wkv_t"]).then_inc(s["wkv_loaded"], 16)
            sp.dma_start(wqp[:, :, :], io["wqp"]).then_inc(s["wqp_loaded"], 16)
            sp.dma_start(bk[:, :], io["bk1"]).then_inc(s["bk_loaded"], 16)
            sp.dma_start(bv[:, :], io["bv1"].partition_broadcast(P)).then_inc(s["bv_loaded"], 16)
            for j in range(3):
                sp.dma_start(wf[:, j, :], io[("gate_w", "val_w", "out_w")[j]]).then_inc(wf_loaded[j], 16)
            sp.dma_start(k.bias1[:, :], io["bias1"].partition_broadcast(P)).then_inc(s["bias_loaded"], 16)
            sp.wait_ge(s["bias_loaded"], 16)

        @block.scalar
        def _(act):
            act.wait_ge(s["wkv_loaded"], 16)
            nc.scalar.activation(wkv_hi[:, :, :], wkv[:, :, :], ACT.Copy).then_inc(s["hi"], 1)
            nc.scalar.activation(ctx_hi[:, :, :], k.ctx_t[:, :, :], ACT.Copy).then_inc(s["hi"], 1)
            act.wait_ge(s["bk_loaded"], 16)
            for n in range(4):
                c, half = n // 2, n % 2
                act.wait_ge(s["keys"], n + 1)
                nc.scalar.activation(k.k1_t[:, c, half * 512:(half + 1) * 512], bank[n][:, :], ACT.Identity,
                                     bias=bk[:, c:c + 1]).then_inc(s["keys_kept"], 1)
            act.wait_ge(s["turned"], 1)
            for w in range(2):
                nc.scalar.activation(k.wqp_t[:, w, :, :], bank[2 + w][:, :].rearrange("p (c n) -> p c n", c=KC),
                                     ACT.Copy, bias=-RND).then_inc(s["turned_kept"], 1)
            act.wait_ge(s["scales"], 1)
            nc.scalar.activation(k.scale_qp[:, :], bank[4][:, :], ACT.Copy).then_inc(s["turned_kept"], 1)
            for j in range(3):
                act.wait_ge(s["clipped"], j + 1)
                nc.scalar.activation(k.w_ffn[:, j, :], wr[:, :], ACT.Copy, bias=-RND).then_inc(s["ternary"], 1)

        @block.tensor
        def _(pe):
            pe.wait_ge(s["lo"], 2)
            for n in range(4):
                c, half = n // 2, n % 2
                for kc in range(KC):
                    w_hi, w_lo = (w[:, kc, c * P:(c + 1) * P] for w in (wkv_hi, wkv_lo))
                    c_hi, c_lo = (a[:, kc, half * 512:(half + 1) * 512] for a in (ctx_hi, ctx_lo))
                    nc.tensor.matmul(bank[n][:, :], w_hi, c_hi, start=kc == 0, stop=False)
                    nc.tensor.matmul(bank[n][:, :], w_hi, c_lo, start=False, stop=False)
                    last = nc.tensor.matmul(bank[n][:, :], w_lo, c_hi, start=False, stop=kc == KC - 1)
                last.then_inc(s["keys"], 1)
            for b in range(B):
                if b >= 4:
                    pe.wait_ge(s["values_kept"], b - 3)
                ps = bank[4 + b % 4]
                for kc in range(KC):
                    w_hi, w_lo = (w[:, kc, D:2 * D] for w in (wkv_hi, wkv_lo))
                    c_hi, c_lo = (a[:, kc, b * P:(b + 1) * P] for a in (ctx_hi, ctx_lo))
                    nc.tensor.matmul(ps[:, 0:D], c_hi, w_hi, start=kc == 0, stop=False)
                    nc.tensor.matmul(ps[:, 0:D], c_hi, w_lo, start=False, stop=False)
                    last = nc.tensor.matmul(ps[:, 0:D], c_lo, w_hi, start=False, stop=kc == KC - 1)
                last.then_inc(s["values"], 1)
            pe.wait_ge(s["keys_kept"], 4)
            pe.wait_ge(s["rounded"], 1)
            for w in range(2):
                for r in range(KC):
                    for c in range(KC):
                        last = nc.tensor.transpose(bank[2 + w][:, c * D + r * P:c * D + (r + 1) * P],
                                                   rounded[:, w * KC + r, c * P:(c + 1) * P], k.ident[:, :])
            last.then_inc(s["turned"], 1)
            pe.wait_ge(s["scale_cols"], 1)
            pe.wait_ge(s["values_kept"], B)
            for r in range(2 * KC):
                last = nc.tensor.matmul(bank[4][:, r * P:(r + 1) * P], scale_cols[:, r, :], k.ident[:, :], start=True, stop=True)
            last.then_inc(s["scales"], 1)
            pe.wait_ge(s["sums"], 1)
            nc.tensor.matmul(bank[0][:, 0:3], ones[:, :], wsum[:, :], start=True, stop=True).then_inc(s["gamma"], 1)

        @block.vector
        def _(dve):
            at = [0]

            def chained(ins):
                at[0] += 1
                ins.then_inc(s["chain"], 1)
                dve.wait_ge(s["chain"], at[0])

            nc.vector.memset(ones[:, :], 1.0)
            nc.vector.memset(k.v1[:, :, :, HD1:], 1.0)
            dve.wait_ge(s["hi"], 1)
            nc.vector.tensor_tensor(wkv_lo[:, :, :], wkv[:, :, :], wkv_hi[:, :, :].bitcast(F32), ALU.subtract).then_inc(s["lo"], 1)
            dve.wait_ge(s["hi"], 2)
            nc.vector.tensor_tensor(ctx_lo[:, :, :], k.ctx_t[:, :, :], ctx_hi[:, :, :].bitcast(F32), ALU.subtract).then_inc(s["lo"], 1)
            dve.wait_ge(s["wqp_loaded"], 16)
            chained(nc.vector.tensor_reduce(amax[:, :], wqp[:, :, :], AX_X, ALU.max, apply_absolute_value=True))
            chained(nc.vector.tensor_scalar(scale[:, :], amax[:, :], 1.0 / 127.0, 1e-8, ALU.mult, ALU.max))
            nc.vector.tensor_copy(scale_cols[:, :, :], scale[:, :].rearrange("p (r o) -> p r o", o=1).broadcast_to(
                [P, 2 * KC, P])).then_inc(s["scale_cols"], 1)
            chained(nc.vector.reciprocal(inv[:, :], scale[:, :]))
            for r in range(2 * KC):
                last = nc.vector.tensor_scalar(wqp[:, r, :], wqp[:, r, :], inv[:, r:r + 1], RND, ALU.mult, ALU.add)
            chained(last)
            nc.vector.tensor_scalar(rounded[:, :, :], wqp[:, :, :], RND + 127.0, RND - 127.0, ALU.min, ALU.max
                                    ).then_inc(s["rounded"], 1)
            dve.wait_ge(s["bv_loaded"], 16)
            for b in range(B):
                dve.wait_ge(s["values"], b + 1)
                nc.vector.tensor_tensor(k.v1[:, b, :, 0:HD1], bank[4 + b % 4][:, 0:D].rearrange("p (h d) -> p h d", d=HD1),
                                        bv[:, :].rearrange("p (h d) -> p h d", d=HD1), ALU.add).then_inc(s["values_kept"], 1)
            for j in range(3):
                dve.wait_ge(wf_loaded[j], 16)
                last = nc.vector.tensor_reduce(wsum[:, j:j + 1], wf[:, j, :], AX_X, ALU.add, apply_absolute_value=True)
            last.then_inc(s["sums"], 1)
            dve.wait_ge(s["gamma"], 1)
            chained(nc.vector.tensor_scalar(k.gamma[:, :], bank[0][:, 0:3], 1.0 / (D * HIDDEN), 1e-5, ALU.mult, ALU.max))
            chained(nc.vector.reciprocal(ginv[:, :], k.gamma[:, :]))
            for j in range(3):
                chained(nc.vector.tensor_scalar(wf[:, j, :], wf[:, j, :], ginv[:, j:j + 1], RND, ALU.mult, ALU.add))
                if j >= 1:
                    dve.wait_ge(s["ternary"], j)
                nc.vector.tensor_scalar(wr[:, :], wf[:, j, :], RND + 1.0, RND - 1.0, ALU.min, ALU.max).then_inc(s["clipped"], 1)


def rounded_norm(nc, k, name, low, high, floor, as_gamma):
    with ExitStack() as ctx:
        m = Mem(nc, ctx)
        bank = banks(k, 0, 4)
        stats = m.sb(f"{name}_stats", [P, B, 6])
        mv = m.sb(f"{name}_mv", [P, B, 2])
        vpe = m.sb(f"{name}_vpe", [P, B])
        rstd = m.sb(f"{name}_rstd", [P, B])
        xn = m.sb(f"{name}_xn", [P, B, D])
        amax = m.sb(f"{name}_amax", [P, B])
        inv = m.sb(f"{name}_inv", [P, B])
        rnd = m.sb(f"{name}_rnd", [P, B, D])
        names = ("stats", "mv", "vpe", "rstd", "xn", "chain", "rounded", "turned", "kept")
        s = {n: m.sem(f"{name}_{n}") for n in names}
        block = ctx.enter_context(nc.Block())

        @block.gpsimd
        def _(pool):
            pool.wait_ge(s["mv"], B)
            nc.gpsimd.tensor_scalar(vpe[:, :], mv[:, :, 1], 1e-5, None, ALU.add).then_inc(s["vpe"], 1)
            pool.wait_ge(s["vpe"], 1)
            nc.gpsimd.tensor_tensor(rstd[:, :], vpe[:, :], k.neg_half[:, 0:B], ALU.pow).then_inc(s["rstd"], 1)

        @block.vector
        def _(dve):
            for t in range(B):
                nc.vector.bn_stats(stats[:, t, :], k.x_res[:, t, :]).then_inc(s["stats"], 1)
            for t in range(B):
                dve.wait_ge(s["stats"], t + 1)
                nc.vector.bn_aggr(mv[:, t, :], stats[:, t, :]).then_inc(s["mv"], 1)
            dve.wait_ge(s["rstd"], 1)
            for t in range(B):
                last = nc.vector.tensor_scalar(xn[:, t, :], k.x_res[:, t, :], mv[:, t, 0:1], rstd[:, t:t + 1],
                                               ALU.subtract, ALU.mult)
            last.then_inc(s["xn"], 1)
            dve.wait_ge(s["xn"], 1)
            nc.vector.tensor_reduce(amax[:, :], xn[:, :, :], AX_X, ALU.max, apply_absolute_value=True).then_inc(s["chain"], 1)
            dve.wait_ge(s["chain"], 1)
            if as_gamma:
                nc.vector.tensor_scalar(k.x_scale[:, :], amax[:, :], floor, 1.0 / 127.0, ALU.max, ALU.mult).then_inc(s["chain"], 1)
            else:
                nc.vector.tensor_scalar(k.x_scale[:, :], amax[:, :], 1.0 / 127.0, floor, ALU.mult, ALU.max).then_inc(s["chain"], 1)
            dve.wait_ge(s["chain"], 2)
            nc.vector.reciprocal(inv[:, :], k.x_scale[:, :]).then_inc(s["chain"], 1)
            dve.wait_ge(s["chain"], 3)
            for t in range(B):
                nc.vector.tensor_scalar(rnd[:, t, :], xn[:, t, :], inv[:, t:t + 1], RND, ALU.mult, ALU.add).then_inc(s["chain"], 1)
                dve.wait_ge(s["chain"], t + 4)
                nc.vector.tensor_scalar(rnd[:, t, :], rnd[:, t, :], RND + high, RND + low, ALU.min, ALU.max).then_inc(s["rounded"], 1)

        @block.tensor
        def _(pe):
            for t in range(B):
                pe.wait_ge(s["rounded"], t + 1)
                if t >= 4:
                    pe.wait_ge(s["kept"], t - 3)
                for c in range(KC):
                    last = nc.tensor.transpose(bank[t % 4][:, c * P:(c + 1) * P], rnd[:, t, c * P:(c + 1) * P], k.ident[:, :])
                last.then_inc(s["turned"], 1)

        @block.scalar
        def _(act):
            for t in range(B):
                act.wait_ge(s["turned"], t + 1)
                nc.scalar.activation(k.xi_t[:, :, t * P:(t + 1) * P], bank[t % 4][:, 0:D].rearrange("p (c n) -> p c n", c=KC),
                                     ACT.Copy, bias=-RND).then_inc(s["kept"], 1)


def layer1_attention(nc, io, k):
    with ExitStack() as ctx:
        m = Mem(nc, ctx)
        ps_s = banks(k, 0, KC, 2)
        ps_t0, ps_t1, ps_o, ps_m = banks(k, 4, 4)
        ps_t = (ps_t0, ps_t1)
        q0 = m.sb("f_q0", [P, D])
        q = m.sb("f_q", [P, D])
        q_t = m.sb("f_q_t", [P, KC, P])
        kd = m.sb("f_kd", [P, KC, HC, P])
        nmax = m.sb("f_nmax", [P, KC, HC])
        nbias = m.sb("f_nbias", [P, KC, HC])
        prob = m.sb("f_prob", [P, NH1, P])
        prob_t = m.sb("f_prob_t", [P, NH1, P])
        sinv = m.sb("f_sinv", [P, NH1])
        o = m.sb("f_o", [P, D])
        amax = m.sb("f_amax", [P, 1])
        o_scale = m.sb("f_o_scale", [P, 1])
        inv = m.sb("f_inv", [P, 1])
        o_rnd0 = m.sb("f_o_rnd0", [P, D])
        o_rnd = m.sb("f_o_rnd", [P, D])
        oi_t = m.sb("f_oi_t", [P, KC, P], BF16)
        y = m.sb("f_y", [P, D])
        yb = m.sb("f_yb", [P, D])
        names = ("q_proj", "q_read", "q_bias", "q_turned", "q_kept", "pv", "sinv", "o", "amax", "o_scale", "inv",
                 "o_rnd0", "o_rnd", "o_turned", "oi_kept", "out", "out_read", "y_bias", "added")
        s = {n: m.sem(f"f_{n}") for n in names}
        halves = ("keys", "scores", "nmax", "nbias", "exps")
        for c in range(KC):
            s.update({f"{n}{c}": m.sem(f"f_{n}{c}") for n in halves})
        for j in range(4):
            s.update({f"{n}{j}": m.sem(f"f_{n}{j}") for n in ("quarter", "quarter_kept")})
        block = ctx.enter_context(nc.Block())

        def done(eng, name, b):
            if type(b) is not int or 0 <= b < B:
                eng.wait_ge(s[name], b + 1)

        def stage(b, work, *args):
            if type(b) is not int or 0 <= b < B:
                work(b, *args)

        def program(eng, step):
            for b in range(-1, 2):
                step(b)
            with eng.Fori(2, B - 1) as b:
                step(b)
            for b in range(B - 1, B + 2):
                step(b)

        @block.tensor
        def _(pe):
            def q_proj(b):
                done(pe, "q_kept", b - 1)
                for c in range(KC):
                    last = nc.tensor.matmul(ps_m[:, 0:D], k.xi_t[:, c, cols(b, 0, P)], k.wqp_t[:, 0, c, :],
                                            start=c == 0, stop=c == KC - 1)
                last.then_inc(s["q_proj"], 1)

            def turn_o(b):
                done(pe, "o_rnd", b)
                done(pe, "q_read", b + 3)
                done(pe, "out_read", b - 1)
                for c in range(KC):
                    last = nc.tensor.transpose(ps_m[:, c * P:(c + 1) * P], o_rnd[:, c * P:(c + 1) * P], k.ident[:, :])
                last.then_inc(s["o_turned"], 1)

            def out_proj(b):
                done(pe, "oi_kept", b)
                for c in range(KC):
                    last = nc.tensor.matmul(ps_m[:, 0:D], oi_t[:, c, :], k.wqp_t[:, 1, c, :], start=c == 0, stop=c == KC - 1)
                last.then_inc(s["out"], 1)

            def turn_q(b):
                done(pe, "q_bias", b)
                done(pe, "out_read", b - 3)
                for c in range(KC):
                    last = nc.tensor.transpose(ps_m[:, c * P:(c + 1) * P], q[:, c * P:(c + 1) * P], k.ident[:, :])
                last.then_inc(s["q_turned"], 1)

            def scores(b, c):
                done(pe, "q_kept", b)
                done(pe, f"keys{c}", b)
                done(pe, f"exps{c}", b - 1)
                for j in range(HC // 4):
                    last = nc.tensor.matmul(ps_s[c][:, j * 512:(j + 1) * 512], q_t[:, c, :], kd[:, c, j * 4:(j + 1) * 4, :],
                                            start=True, stop=True)
                last.then_inc(s[f"scores{c}"], 1)

            def turn_probs(b, c):
                done(pe, f"exps{c}", b)
                for j in range(2 * c, 2 * c + 2):
                    if j < 2:
                        done(pe, f"quarter_kept{j + 2}", b - 1)
                    else:
                        done(pe, f"quarter_kept{j - 2}", b)
                    for r in range(4):
                        last = nc.tensor.transpose(ps_t[j % 2][:, r * P:(r + 1) * P], prob[:, 4 * j + r, :], k.ident[:, :])
                    last.then_inc(s[f"quarter{j}"], 1)

            def attend(b):
                done(pe, "o", b - 1)
                for h in range(NH1):
                    if h % 4 == 0:
                        done(pe, f"quarter_kept{h // 4}", b)
                    last = nc.tensor.matmul(ps_o[:, h * (HD1 + 1):(h + 1) * (HD1 + 1)], prob_t[:, h, :],
                                            k.v1[:, bass.ds(b, 1), h, :].rearrange("p o d -> p (o d)"), start=True, stop=True)
                last.then_inc(s["pv"], 1)

            def step(b):
                stage(b - 1, turn_probs, 0)
                stage(b + 1, q_proj)
                stage(b, scores, 0)
                stage(b - 2, turn_o)
                stage(b - 1, turn_probs, 1)
                stage(b, scores, 1)
                stage(b - 2, out_proj)
                stage(b - 1, attend)
                stage(b + 1, turn_q)

            program(pe, step)

        @block.vector
        def _(dve):
            def scale_q(b):
                done(dve, "q_proj", b)
                nc.vector.scalar_tensor_tensor(q0[:, :], ps_m[:, 0:D], k.x_scale[:, bass.ds(b, 1)], k.scale_qp[:, 0:D],
                                               ALU.mult, ALU.mult).then_inc(s["q_read"], 1)
                done(dve, "q_read", b)
                done(dve, "q_turned", b - 1)
                nc.vector.tensor_tensor(q[:, :], q0[:, :], k.bias1[:, BQ], ALU.add).then_inc(s["q_bias"], 1)

            def keep_q(b):
                done(dve, "q_turned", b)
                nc.vector.tensor_copy(q_t[:, :, :], ps_m[:, 0:D].rearrange("p (c n) -> p c n", c=KC)).then_inc(s["q_kept"], 1)

            def maxima(b, c):
                done(dve, f"scores{c}", b)
                nc.vector.tensor_reduce(nmax[:, c, :], ps_s[c][:, :].rearrange("p (h e) -> p h e", h=HC), AX_X, ALU.max,
                                        negate=True).then_inc(s[f"nmax{c}"], 1)
                done(dve, f"nmax{c}", b)
                done(dve, f"exps{c}", b - 1)
                nc.vector.tensor_scalar(nbias[:, c, :], nmax[:, c, :], float(HD1) ** -0.5, None, ALU.mult
                                        ).then_inc(s[f"nbias{c}"], 1)

            def keep_quarter(b, j):
                done(dve, f"quarter{j}", b)
                done(dve, "pv", b - 1)
                nc.vector.tensor_copy(prob_t[:, 4 * j:4 * j + 4, :], ps_t[j % 2][:, :].rearrange("p (r e) -> p r e", r=4)
                                      ).then_inc(s[f"quarter_kept{j}"], 1)

            def round_o(b):
                done(dve, "pv", b)
                heads = ps_o[:, 0:NH1 * (HD1 + 1)].rearrange("p (h d) -> p h d", h=NH1)
                nc.vector.reciprocal(sinv[:, :], heads[:, :, HD1]).then_inc(s["sinv"], 1)
                done(dve, "sinv", b)
                nc.vector.tensor_tensor(o[:, :].rearrange("p (h d) -> p h d", h=NH1), heads[:, :, 0:HD1],
                                        sinv[:, :].rearrange("p (h o) -> p h o", o=1).broadcast_to([P, NH1, HD1]),
                                        ALU.mult).then_inc(s["o"], 1)
                done(dve, "o", b)
                nc.vector.tensor_reduce(amax[:, :], o[:, :], AX_X, ALU.max, apply_absolute_value=True).then_inc(s["amax"], 1)
                done(dve, "amax", b)
                nc.vector.tensor_scalar(o_scale[:, :], amax[:, :], 1.0 / 127.0, 1e-8, ALU.mult, ALU.max).then_inc(s["o_scale"], 1)
                done(dve, "o_scale", b)
                nc.vector.reciprocal(inv[:, :], o_scale[:, :]).then_inc(s["inv"], 1)
                done(dve, "inv", b)
                nc.vector.tensor_scalar(o_rnd0[:, :], o[:, :], inv[:, 0:1], RND, ALU.mult, ALU.add).then_inc(s["o_rnd0"], 1)
                done(dve, "o_rnd0", b)
                done(dve, "o_turned", b - 1)
                nc.vector.tensor_scalar(o_rnd[:, :], o_rnd0[:, :], RND + 127.0, RND - 127.0, ALU.min, ALU.max
                                        ).then_inc(s["o_rnd"], 1)

            def scale_out(b):
                done(dve, "out", b)
                done(dve, "y_bias", b - 1)
                nc.vector.scalar_tensor_tensor(y[:, :], ps_m[:, 0:D], o_scale[:, :], k.scale_qp[:, D:2 * D],
                                               ALU.mult, ALU.mult).then_inc(s["out_read"], 1)

            def step(b):
                stage(b + 1, scale_q)
                stage(b - 1, keep_quarter, 0)
                stage(b, maxima, 0)
                stage(b - 1, keep_quarter, 2)
                stage(b, maxima, 1)
                stage(b - 2, scale_out)
                stage(b + 1, keep_q)
                stage(b - 1, round_o)

            program(dve, step)

        @block.scalar
        def _(act):
            def exps(b, c):
                done(act, f"nbias{c}", b)
                done(act, f"quarter{2 * c + 1}", b - 1)
                for h in range(HC):
                    last = nc.scalar.activation(prob[:, c * HC + h, :], ps_s[c][:, h * P:(h + 1) * P], ACT.Exp,
                                                bias=nbias[:, c, h:h + 1], scale=float(HD1) ** -0.5)
                last.then_inc(s[f"exps{c}"], 1)

            def keep_quarter(b, j):
                done(act, f"quarter{j}", b)
                done(act, "pv", b - 1)
                nc.scalar.activation(prob_t[:, 4 * j:4 * j + 4, :], ps_t[j % 2][:, :].rearrange("p (r e) -> p r e", r=4),
                                     ACT.Copy).then_inc(s[f"quarter_kept{j}"], 1)

            def keep_o(b):
                done(act, "o_turned", b)
                nc.scalar.activation(oi_t[:, :, :], ps_m[:, 0:D].rearrange("p (c n) -> p c n", c=KC), ACT.Copy,
                                     bias=-RND).then_inc(s["oi_kept"], 1)

            def step(b):
                stage(b - 1, keep_quarter, 1)
                stage(b, exps, 0)
                stage(b - 2, keep_o)
                stage(b - 1, keep_quarter, 3)
                stage(b, exps, 1)

            program(act, step)

        @block.gpsimd
        def _(pool):
            def spread_keys(b, c):
                done(pool, f"scores{c}", b - 1)
                keys = k.k1_t[:, c, cols(b, 0, P)].rearrange("p (o e) -> p o e", o=1).broadcast_to([P, HC, P])
                mask = k.head_mask[:, :].rearrange("p (h o) -> p h o", o=1).broadcast_to([P, HC, P])
                nc.gpsimd.tensor_tensor(kd[:, c, :, :], keys, mask, ALU.mult).then_inc(s[f"keys{c}"], 1)

            def add_out(b):
                done(pool, "out_read", b)
                done(pool, "added", b - 1)
                nc.gpsimd.tensor_tensor(yb[:, :], y[:, :], k.bias1[:, BP], ALU.add).then_inc(s["y_bias"], 1)
                done(pool, "y_bias", b)
                x_b = k.x_res[:, bass.ds(b, 1), :].rearrange("p o d -> p (o d)")
                nc.gpsimd.tensor_tensor(x_b, x_b, yb[:, :], ALU.add).then_inc(s["added"], 1)

            def step(b):
                stage(b + 1, spread_keys, 0)
                stage(b + 1, spread_keys, 1)
                stage(b - 2, add_out)

            program(pool, step)


def last_ffn(nc, io, k, out):
    with ExitStack() as ctx:
        m = Mem(nc, ctx)
        ps_g, ps_v, ps_t = banks(k, 0, 3, 2)
        (ps_y,) = banks(k, 6, 1)
        unit = m.sb("g_unit", [P, 2, B])
        gate = m.sb("g_gate_sb", [P, HIDDEN])
        silu = m.sb("g_silu", [P, HIDDEN])
        val = m.sb("g_val_sb", [P, HIDDEN])
        h = m.sb("g_h", [P, HIDDEN])
        amax = m.sb("g_amax", [P, 1])
        h_scale = m.sb("g_h_scale", [P, 1])
        h_unit = m.sb("g_h_unit", [P, 2, 1])
        inv = m.sb("g_inv", [P, 1])
        rnd0 = m.sb("g_rnd0", [P, HIDDEN])
        rnd1 = m.sb("g_rnd1", [P, HIDDEN])
        hi_t = m.sb("g_hi_t", [P, HIDDEN], BF16)
        y = m.sb("g_y", [P, 2, D])
        FC = HIDDEN // P
        names = ("units", "mm_gate", "mm_val", "gate", "val", "silu", "h", "amax", "h_scale", "h_unit", "inv", "rnd0",
                 "rnd1", "turned", "kept", "mm_out", "y", "x_done", "stored")
        s = {n: m.sem(f"g_{n}") for n in names}
        block = ctx.enter_context(nc.Block())

        def done(eng, name, t):
            eng.wait_ge(s[name], t + 2)

        def freed(eng, name, t):
            eng.wait_ge(s[name], t + 1)

        def start_ahead(eng, *names):
            for name in names:
                eng.sem_inc(s[name], 1)

        def stage(t, lag, work):
            if type(t) is not int or 0 <= t - lag < B:
                work(t - lag)

        def program(eng, step):
            step(0)
            with eng.Fori(1, B) as t:
                step(t)
            step(B)

        @block.tensor
        def _(pe):
            def gate_val(t):
                for name, ps, j, read in (("mm_gate", ps_g, 0, "gate"), ("mm_val", ps_v, 1, "val")):
                    freed(pe, read, t)
                    for half in range(2):
                        for c in range(KC):
                            at = c * HIDDEN + half * 512
                            last = nc.tensor.matmul(ps[:, half * 512:(half + 1) * 512], k.xi_t[:, c, cols(t, 0, P)],
                                                    k.w_ffn[:, j, at:at + 512], start=c == 0, stop=c == KC - 1)
                    last.then_inc(s[name], 1)

            def turn(t):
                done(pe, "rnd1", t)
                freed(pe, "kept", t)
                for c in range(FC):
                    last = nc.tensor.transpose(ps_t[:, c * P:(c + 1) * P], rnd1[:, c * P:(c + 1) * P], k.ident[:, :])
                last.then_inc(s["turned"], 1)

            def out_proj(t):
                done(pe, "kept", t)
                freed(pe, "y", t)
                for c in range(FC):
                    last = nc.tensor.matmul(ps_y[:, 0:D], hi_t[:, c * P:(c + 1) * P], k.w_ffn[:, 2, c * D:(c + 1) * D],
                                            start=c == 0, stop=c == FC - 1)
                last.then_inc(s["mm_out"], 1)

            def step(t):
                stage(t, 0, gate_val)
                stage(t, 1, turn)
                stage(t, 1, out_proj)

            start_ahead(pe, "mm_gate", "mm_val", "turned", "mm_out")
            program(pe, step)

        @block.vector
        def _(dve):
            def biased(t):
                done(dve, "mm_gate", t)
                freed(dve, "silu", t)
                nc.vector.scalar_tensor_tensor(gate[:, :], ps_g[:, :], unit[:, 0, bass.ds(t, 1)], k.bias1[:, BG],
                                               ALU.mult, ALU.add).then_inc(s["gate"], 1)
                done(dve, "mm_val", t)
                freed(dve, "h", t)
                nc.vector.scalar_tensor_tensor(val[:, :], ps_v[:, :], unit[:, 1, bass.ds(t, 1)], k.bias1[:, BV],
                                               ALU.mult, ALU.add).then_inc(s["val"], 1)

            def rounded(t):
                done(dve, "h", t)
                nc.vector.tensor_reduce(amax[:, :], h[:, :], AX_X, ALU.max, apply_absolute_value=True).then_inc(s["amax"], 1)
                done(dve, "amax", t)
                nc.vector.tensor_scalar(h_scale[:, :], amax[:, :], 1e-5, 1.0 / 127.0, ALU.max, ALU.mult).then_inc(s["h_scale"], 1)
                done(dve, "h_scale", t)
                nc.vector.reciprocal(inv[:, :], h_scale[:, :]).then_inc(s["inv"], 1)
                nc.vector.tensor_tensor(h_unit[:, 0, :], h_scale[:, :], k.gamma[:, 2:3], ALU.mult).then_inc(s["h_unit"], 1)
                done(dve, "inv", t)
                nc.vector.tensor_scalar(rnd0[:, :], h[:, :], inv[:, 0:1], RND, ALU.mult, ALU.add).then_inc(s["rnd0"], 1)
                done(dve, "rnd0", t)
                freed(dve, "turned", t)
                nc.vector.tensor_scalar(rnd1[:, :], rnd0[:, :], RND + 127.0, RND - 128.0, ALU.min, ALU.max).then_inc(s["rnd1"], 1)

            def add_out(t):
                done(dve, "mm_out", t)
                nc.vector.scalar_tensor_tensor(y[:, 0, :], ps_y[:, 0:D], h_unit[:, 0, :], k.bias1[:, BO],
                                               ALU.mult, ALU.add).then_inc(s["y"], 1)
                done(dve, "y", t)
                x_t = k.x_res[:, bass.ds(t, 1), :].rearrange("p o d -> p (o d)")
                nc.vector.tensor_tensor(x_t, x_t, y[:, 0, :], ALU.add).then_inc(s["x_done"], 1)

            def step(t):
                stage(t, 0, biased)
                stage(t, 1, add_out)
                stage(t, 0, rounded)

            start_ahead(dve, "gate", "val", "amax", "h_scale", "h_unit", "inv", "rnd0", "rnd1", "y", "x_done")
            nc.vector.tensor_scalar(unit[:, 0, :], k.x_scale[:, :], k.gamma[:, 0:1], None, ALU.mult)
            nc.vector.tensor_scalar(unit[:, 1, :], k.x_scale[:, :], k.gamma[:, 1:2], None, ALU.mult).then_inc(s["units"], 1)
            dve.wait_ge(s["units"], 1)
            program(dve, step)

        @block.scalar
        def _(act):
            def silus(t):
                done(act, "gate", t)
                freed(act, "h", t)
                nc.scalar.activation(silu[:, :], gate[:, :], ACT.Silu).then_inc(s["silu"], 1)

            def keep(t):
                done(act, "turned", t)
                freed(act, "mm_out", t)
                nc.scalar.activation(hi_t[:, :], ps_t[:, :], ACT.Copy, bias=-RND).then_inc(s["kept"], 1)

            def step(t):
                stage(t, 0, silus)
                stage(t, 1, keep)

            start_ahead(act, "silu", "kept")
            program(act, step)

        @block.gpsimd
        def _(pool):
            def times(t):
                done(pool, "silu", t)
                done(pool, "val", t)
                freed(pool, "rnd0", t)
                nc.gpsimd.tensor_tensor(h[:, :], silu[:, :], val[:, :], ALU.mult).then_inc(s["h"], 1)

            pool.sem_inc(s["h"], 1)
            program(pool, lambda t: stage(t, 0, times))

        @block.sync
        def _(sp):
            with sp.Fori(0, B) as t:
                done(sp, "x_done", t)
                sp.dma_start(out[bass.ds(t, 1)].rearrange("o p d -> p (o d)"),
                             k.x_res[:, bass.ds(t, 1), :].rearrange("p o d -> p (o d)")).then_inc(s["stored"], 16)
            sp.wait_ge(s["stored"], 16 * B)


class Kept:
    pass


def build(nc, io, out):
    with ExitStack() as ctx:
        Mem.held.clear()
        m = Mem(nc, ctx)
        k = Kept()
        k.psum = ctx.enter_context(nc.psum_tensor("psum", [P, 8 * BANK], F32))
        k.x_res = m.sb("x_res", [P, B, D])
        k.xn_t = m.sb("xn_t", [P, KC, T])
        k.ctx_t = m.sb("ctx_t", [P, KC, T])
        k.ident = m.sb("ident", [P, P])
        k.neg_half = m.sb("neg_half", [P, 16])
        k.head_mask = m.sb("head_mask", [P, HC])
        with ExitStack() as layer0:
            a = Mem(nc, layer0)
            k.wa_hi = a.sb("wa_hi", [P, NKV0, WA], F32R)
            k.wa_lo = a.sb("wa_lo", [P, NKV0, WA], F32R)
            k.mask = a.sb("mask", [P, S])
            k.bias_a = a.sb("bias_a", [P, NKV0 * 6 * P])
            k.eps_a = a.sb("eps_a", [P, 5])
            k.norm_w = a.sb("norm_w", [P, 2])
            k.key_scale = a.sb("key_scale", [P, 1])
            constants_and_first_norm(nc, io, k)
            layer0_attention(nc, io, k)
        k.comb_dram = nc.dram_tensor("expert_weights", (NE, T), F32, kind="Internal").ap()
        with ExitStack() as ffn0:
            a = Mem(nc, ffn0)
            k.xn_hi = a.sb("xn_hi", [P, KC, T], F32R)
            k.xn_lo = a.sb("xn_lo", [P, KC, T], F32R)
            router(nc, io, k)
            experts(nc, io, k)
        m.end_of_layer()
        k.k1_t = m.sb("k1_t", [P, KC, T])
        k.v1 = m.sb("v1", [P, B, NH1, HD1 + 1])
        k.wqp_t = m.sb("wqp_t", [P, 2, KC, D], BF16)
        k.scale_qp = m.sb("scale_qp", [P, 2 * D])
        k.bias1 = m.sb("bias1", [P, 3 * D + 2 * HIDDEN])
        k.w_ffn = m.sb("w_ffn", [P, 3, KC * HIDDEN], BF16)
        k.gamma = m.sb("gamma", [P, 3])
        k.xi_t = m.sb("xi_t", [P, KC, T], BF16)
        k.x_scale = m.sb("x_scale", [P, B])
        layer1_weights(nc, io, k)
        rounded_norm(nc, k, "n3", -127.0, 127.0, 1e-8, False)
        layer1_attention(nc, io, k)
        rounded_norm(nc, k, "n4", -128.0, 127.0, 1e-5, True)
        last_ffn(nc, io, k, out)


def lay_out(i):
    import numpy as np

    a = {n: np.asarray(v) for n, v in i.items()}

    def chunked(w):
        return w.reshape(-1, P, w.shape[1]).transpose(1, 0, 2)

    groups, biases = [], []
    for g in range(NKV0):
        q, kv = slice(g * GH * HD0, (g + 1) * GH * HD0), slice(g * HD0, (g + 1) * HD0)
        w_kv = np.concatenate([a["L0_xattn_Wk"][:, kv], a["L0_xattn_Wv"][:, kv]], axis=1)
        parts = (chunked(a["L0_xattn_Wq"][:, q]), chunked(w_kv), chunked(a["L0_xattn_Wo"][q]))
        groups.append(np.concatenate([p.reshape(P, -1) for p in parts], axis=1))
        biases += [a["L0_xattn_bq"][q], a["L0_xattn_bk"][kv], a["L0_xattn_bv"][kv]]
    gu, down = a["L0_ffn_gate_up_proj"], a["L0_ffn_down_proj"]
    inner = [w.reshape(MT, P, KC, P).transpose(0, 3, 2, 1).reshape(MT, P, KC * P) for w in (gu[:, :INTER], gu[:, INTER:])]
    inner.append(down.transpose(0, 2, 1).reshape(MT, P, D))
    return {
        "wkv_t": chunked(a["L1_xattn_wkv"].T),
        "wqp": np.concatenate([w.reshape(KC, P, D) for w in (a["L1_xattn_wq"], a["L1_xattn_wp"])]).transpose(1, 0, 2),
        "bk1": a["L1_xattn_bkv"][:D].reshape(KC, P).T,
        "bv1": a["L1_xattn_bkv"][D:],
        "bias1": np.concatenate([a[n] for n in ("L1_xattn_bq", "L1_xattn_bp", "L1_ffn_gate_b", "L1_ffn_val_b", "L1_ffn_out_b")]),
        "gate_w": chunked(a["L1_ffn_gate_w"].T).reshape(P, -1),
        "val_w": chunked(a["L1_ffn_val_w"].T).reshape(P, -1),
        "out_w": chunked(a["L1_ffn_out_w"].T).reshape(P, -1),
        "gate_t": chunked(a["L0_ffn_gate_weight"].T),
        "wm": np.concatenate(inner, axis=2),
        "x": a["x"],
        "ctx_t": chunked(a["ctx_2048"].reshape(T, D).T),
        "mask": a["mask_1xSxS2_ff0"],
        "wa": np.stack(groups),
        "bias_a": np.concatenate(biases),
        "norm_w": np.stack([a["L0_xattn_qn_w"], a["L0_xattn_kn_w"]], axis=1),
    }


def kernel(**inputs):
    import numpy as np
    import concourse.bacc as bacc
    from concourse.bass_utils import run_bass_kernel_spmd

    nc = bacc.Bacc("TRN2", target_bir_lowering=False, num_devices=1)
    arrays = {f"in_{n}": np.ascontiguousarray(v) for n, v in lay_out(inputs).items()}
    io = {n[3:]: nc.dram_tensor(n, v.shape, mybir.dt.from_np(v.dtype), kind="ExternalInput").ap() for n, v in arrays.items()}
    out = nc.dram_tensor("out", (B, S, D), F32, kind="ExternalOutput").ap()
    build(nc, io, out)
    r = run_bass_kernel_spmd(nc, [arrays], core_ids=[0])
    return r.results[0]["out"]
```

```python
from contextlib import ExitStack

import concourse.bass as bass
from concourse import mybir

P = 128
BANK = 512
F32 = mybir.dt.float32
F32R = mybir.dt.float32r
BF16 = mybir.dt.bfloat16
ALU = mybir.AluOpType
ACT = mybir.ActivationFunctionType
AX_X = mybir.AxisListType.X

B, S, D = 8, 128, 256
T = B * S
KC = D // P
NH0, NKV0, HD0 = 16, 4, 128
GH = NH0 // NKV0
NE, TOPK, INTER = 32, 8, 96
MT = NE * INTER // P
THRESHOLD = 0.8
NH1 = 16
HD1 = D // NH1
HC = P // HD1
HIDDEN = 4 * D
RND = 12582912.0
WA = KC * GH * HD0 + KC * 2 * HD0 + GH * D
WQ_AT, WKV_AT, WO_AT = 0, KC * GH * HD0, KC * GH * HD0 + KC * 2 * HD0
WA_SLOTS = NKV0 - 1
WM = 2 * KC * P + D
BQ, BP, BG, BV, BO = (slice(a, a + n) for a, n in (
    (0, D), (D, D), (2 * D, HIDDEN), (2 * D + HIDDEN, HIDDEN), (2 * D + 2 * HIDDEN, D)))


class Mem:

    held = []

    def __init__(self, nc, ctx):
        self.nc, self.ctx = nc, ctx

    def sb(self, name, shape, dt=F32):
        return self.ctx.enter_context(self.nc.sbuf_tensor(name, shape, dt))

    def sem(self, name):
        self.held.append(self.nc.alloc_semaphore(name=name))
        return self.held[-1]

    def end_of_layer(self):
        self.nc.clear_and_free_semaphores(self.held)
        self.held.clear()
        self.nc.all_engine_barrier()


def banks(k, first=0, n=8, width=1):
    return [k.psum[:, (first + i * width) * BANK:(first + (i + 1) * width) * BANK] for i in range(n)]


def cols(t, at, n):
    return bass.ds(t * n + at, n)


def constants_and_first_norm(nc, io, k):
    with ExitStack() as ctx:
        m = Mem(nc, ctx)
        bank = banks(k)
        stats = m.sb("a_stats", [P, B, 6])
        mv = m.sb("a_mv", [P, B, 2])
        rstd = m.sb("a_rstd", [P, B])
        vpe = m.sb("a_vpe", [P, B])
        xn = m.sb("a_xn", [P, B, D])
        s_x = m.sem("a_x")
        k.ctx_loaded, k.mask_loaded, k.bias_loaded, k.norm_w_loaded = (m.sem(f"a_{n}") for n in ("ctx", "mask", "bias", "norm_w"))
        k.wa_loaded = [m.sem(f"a_wa{j}") for j in range(WA_SLOTS)]
        zeroed, half, ident_done, hm_steps = (m.sem(f"a_{n}") for n in ("zeroed", "half", "ident", "hm"))
        stats_done, mv_done, vpe_done, rstd_done = (m.sem(f"a_{n}") for n in ("stats_d", "mv_d", "vpe_d", "rstd_d"))
        xn_done, xt_done = (m.sem(f"a_{n}") for n in ("xn_d", "xt_d"))
        block = ctx.enter_context(nc.Block())

        @block.sync
        def _(sp):
            sp.dma_start(k.x_res[:, :, :], io["x"].rearrange("b p d -> p b d")).then_inc(s_x, 16)
            for g in range(WA_SLOTS):
                sp.dma_start(k.wa_raw[:, g, :], io["wa"][g]).then_inc(k.wa_loaded[g], 16)

        @block.gpsimd
        def _(pool):
            nc.gpsimd.memset(k.ident[:, :], 0.0).then_inc(zeroed, 1)
            nc.gpsimd.memset(k.neg_half[:, :], -0.5).then_inc(half, 1)
            nc.gpsimd.memset(k.eps_a[:, :], HD0 * 1e-6)
            nc.gpsimd.memset(k.head_mask[:, :], float(HD1) ** -0.5).then_inc(hm_steps, 1)
            pool.wait_ge(zeroed, 1)
            nc.gpsimd.affine_select(out=k.ident[:, :], in_=k.ident[:, :], compare_op=ALU.not_equal, fill=1.0,
                                    base=0, pattern=[[-1, P]], channel_multiplier=1).then_inc(ident_done, 1)
            pool.wait_ge(hm_steps, 1)
            nc.gpsimd.affine_select(out=k.head_mask[:, :], in_=k.head_mask[:, :], compare_op=ALU.is_ge, fill=0.0,
                                    base=0, pattern=[[-HD1, HC]], channel_multiplier=1).then_inc(hm_steps, 1)
            pool.wait_ge(hm_steps, 2)
            nc.gpsimd.affine_select(out=k.head_mask[:, :], in_=k.head_mask[:, :], compare_op=ALU.is_ge, fill=0.0,
                                    base=HD1 - 1, pattern=[[HD1, HC]], channel_multiplier=-1).then_inc(hm_steps, 1)
            pool.wait_ge(mv_done, B)
            nc.gpsimd.tensor_scalar(vpe[:, :], mv[:, :, 1], 1e-5, None, ALU.add).then_inc(vpe_done, 1)
            pool.wait_ge(vpe_done, 1)
            pool.wait_ge(half, 1)
            nc.gpsimd.tensor_tensor(rstd[:, :], vpe[:, :], k.neg_half[:, 0:B], ALU.pow).then_inc(rstd_done, 1)

        @block.vector
        def _(dve):
            dve.wait_ge(s_x, 16)
            for t in range(B):
                nc.vector.bn_stats(stats[:, t, :], k.x_res[:, t, :]).then_inc(stats_done, 1)
            for t in range(B):
                dve.wait_ge(stats_done, t + 1)
                nc.vector.bn_aggr(mv[:, t, :], stats[:, t, :]).then_inc(mv_done, 1)
            dve.wait_ge(rstd_done, 1)
            for t in range(B):
                nc.vector.tensor_scalar(xn[:, t, :], k.x_res[:, t, :], mv[:, t, 0:1], rstd[:, t:t + 1],
                                        ALU.subtract, ALU.mult).then_inc(xn_done, 1)

        @block.tensor
        def _(pe):
            pe.wait_ge(ident_done, 1)
            for t in range(B):
                pe.wait_ge(xn_done, t + 1)
                for c in range(KC):
                    last = nc.tensor.transpose(bank[t][:, c * P:(c + 1) * P], xn[:, t, c * P:(c + 1) * P], k.ident[:, :])
                last.then_inc(xt_done, 1)

        @block.scalar
        def _(act):
            act.dma_start(k.norm_w[:, :], io["norm_w"]).then_inc(k.norm_w_loaded, 16)
            act.dma_start(k.mask[:, :], io["mask"][0]).then_inc(k.mask_loaded, 16)
            act.dma_start(k.ctx_t[:, :, :], io["ctx_t"]).then_inc(k.ctx_loaded, 16)
            act.dma_start(k.bias_a[:, :], io["bias_a"].partition_broadcast(P)).then_inc(k.bias_loaded, 16)
            for t in range(B):
                act.wait_ge(xt_done, t + 1)
                nc.scalar.activation(k.xn_t[:, :, t * P:(t + 1) * P], bank[t][:, 0:D].rearrange("p (c n) -> p c n", c=KC), ACT.Copy)


def layer0_attention(nc, io, k):
    with ExitStack() as ctx:
        m = Mem(nc, ctx)
        ps_s, ps_q, ps_kv, ps_pt, ps_qt, ps_kt, ps_o, ps_y = banks(k)
        xh, xl, ch, cl = (m.sb(f"b_{n}", [P, KC, P], F32R) for n in ("xh", "xl", "ch", "cl"))
        qkv = m.sb("b_qkv", [P, 2, 6 * P])
        sq = m.sb("b_sq", [P, 5 * P])
        ssum = m.sb("b_ssum", [P, 5])
        sume = m.sb("b_sume", [P, 5])
        rnorm = m.sb("b_rnorm", [P, NKV0, 5])
        kn = m.sb("b_kn", [P, P])
        qt = m.sb("b_qt", [P, NKV0, GH * P])
        kt = m.sb("b_kt", [P, NKV0, P])
        v = m.sb("b_v", [P, NKV0, P])
        sc = m.sb("b_sc", [P, GH * P])
        nmax = m.sb("b_nmax", [P, GH])
        prob = m.sb("b_prob", [P, GH * P])
        rsum = m.sb("b_rsum", [P, GH])
        rinv = m.sb("b_rinv", [P, GH])
        probn = m.sb("b_probn", [P, GH * P])
        pt = m.sb("b_pt", [P, GH * P])
        oh = m.sb("b_oh", [P, GH * P], F32R)
        ol = m.sb("b_ol", [P, GH * P], F32R)
        ahead = ("qkv_ready", "pt_ready", "ol_ready", "scores_read", "y_added", "exp_done", "sq_done", "qt_ready",
                 "kt_ready", "q_turned", "k_turned", "pv_done", "wo_done", "p_turned", "probn_done", "kn_done",
                 "v_ready", "ssum_done", "rnorm_done")
        plain = ("slot_hi", "slot_lo", "proj_done", "sume_done", "scores_done", "nmax_done", "rinv_done", "oh_ready")
        s = {n: m.sem(f"b_{n}") for n in ahead + plain}
        proj_hi, proj_lo, out_hi, out_lo = (m.sem(f"b_w_{n}") for n in ("proj_hi", "proj_lo", "out_hi", "out_lo"))
        scaled = m.sem("b_key_scale")
        PROJ, OUT = slice(0, WO_AT), slice(WO_AT, WA)
        block = ctx.enter_context(nc.Block())

        def done(eng, name, n):
            eng.wait_ge(s[name], n + (2 if name in ahead else 1))

        def freed(eng, name, n):
            eng.wait_ge(s[name], n + 1)

        def start_ahead(eng, *names):
            for name in names:
                eng.sem_inc(s[name], 1)

        def stage(b, g, lag, work):
            b, g = (b, g - lag) if g >= lag else (b - 1, g - lag + NKV0)
            if type(b) is not int or 0 <= b < B:
                work(b, g, b * NKV0 + g)

        def program(eng, step, before=None, split=None):
            for b in (-1, 0):
                if before:
                    before(b + 1)
                if split and b == -1:
                    split(0)
                for g in range(NKV0):
                    if split and b == -1 and g < NKV0 - 1:
                        split(g + 1)
                    step(b, g)
            with eng.Fori(1, B - 1) as b:
                if before:
                    before(b + 1)
                for g in range(NKV0):
                    step(b, g)
            for g in range(NKV0):
                step(B - 1, g)
            for g in range(2):
                step(B, g)

        @block.sync
        def _(sp):
            for g in range(WA_SLOTS, NKV0):
                for sem in (proj_hi, proj_lo, out_hi, out_lo):
                    sp.wait_ge(sem, g - WA_SLOTS + 1)
                sp.dma_start(k.wa_raw[:, g % WA_SLOTS, :], io["wa"][g]).then_inc(k.wa_loaded[g % WA_SLOTS], 16)

        @block.tensor
        def _(pe):
            def scores(b, g, n):
                done(pe, "qt_ready", n)
                done(pe, "kt_ready", n)
                freed(pe, "scores_read", n)
                for r in range(GH):
                    last = nc.tensor.matmul(ps_s[:, r * P:(r + 1) * P], qt[:, g, r * P:(r + 1) * P], kt[:, g, :],
                                            start=True, stop=True)
                last.then_inc(s["scores_done"], 1)

            def turn_probs(b, g, n):
                done(pe, "probn_done", n)
                freed(pe, "pt_ready", n)
                for r in range(GH):
                    last = nc.tensor.transpose(ps_pt[:, r * P:(r + 1) * P], probn[:, r * P:(r + 1) * P], k.ident[:, :])
                last.then_inc(s["p_turned"], 1)

            def attend(b, g, n):
                done(pe, "pt_ready", n)
                done(pe, "v_ready", n)
                freed(pe, "ol_ready", n)
                nc.tensor.matmul(ps_o[:, :], v[:, g, :], pt[:, :], start=True, stop=True).then_inc(s["pv_done"], 1)

            def out_proj(b, g, n):
                done(pe, "ol_ready", n)
                if type(b) is int and b == 0:
                    pe.wait_ge(out_hi, g + 1)
                    pe.wait_ge(out_lo, g + 1)
                if g == 0:
                    freed(pe, "y_added", b)
                for r in range(GH):
                    w_hi = k.wa_hi[:, g, WO_AT + r * D:WO_AT + (r + 1) * D]
                    w_lo = k.wa_lo[:, g, WO_AT + r * D:WO_AT + (r + 1) * D]
                    o_hi, o_lo = oh[:, r * P:(r + 1) * P], ol[:, r * P:(r + 1) * P]
                    nc.tensor.matmul(ps_y[:, 0:D], o_hi, w_hi, start=g == 0 and r == 0, stop=False)
                    nc.tensor.matmul(ps_y[:, 0:D], o_hi, w_lo, start=False, stop=False)
                    last = nc.tensor.matmul(ps_y[:, 0:D], o_lo, w_hi, start=False, stop=g == NKV0 - 1 and r == GH - 1)
                last.then_inc(s["wo_done"], 1)

            def project(b, g, n):
                if g == 0:
                    done(pe, "slot_hi", b)
                    done(pe, "slot_lo", b)
                if type(b) is int and b == 0:
                    pe.wait_ge(proj_hi, g + 1)
                    pe.wait_ge(proj_lo, g + 1)
                freed(pe, "qkv_ready", n)
                for ps, a_hi, a_lo, at, w in ((ps_q, xh, xl, WQ_AT, GH * HD0), (ps_kv, ch, cl, WKV_AT, 2 * HD0)):
                    for c in range(KC):
                        w_hi = k.wa_hi[:, g, at + c * w:at + (c + 1) * w]
                        w_lo = k.wa_lo[:, g, at + c * w:at + (c + 1) * w]
                        nc.tensor.matmul(ps[:, 0:w], a_hi[:, c, :], w_hi, start=c == 0, stop=False)
                        nc.tensor.matmul(ps[:, 0:w], a_hi[:, c, :], w_lo, start=False, stop=False)
                        last = nc.tensor.matmul(ps[:, 0:w], a_lo[:, c, :], w_hi, start=False, stop=c == KC - 1)
                last.then_inc(s["proj_done"], 1)

            def turn_q(b, g, n):
                done(pe, "qkv_ready", n)
                freed(pe, "qt_ready", n)
                for r in range(GH):
                    last = nc.tensor.transpose(ps_qt[:, r * P:(r + 1) * P], qkv[:, g % 2, r * P:(r + 1) * P], k.ident[:, :])
                last.then_inc(s["q_turned"], 1)

            def turn_k(b, g, n):
                done(pe, "kn_done", n)
                freed(pe, "kt_ready", n)
                nc.tensor.transpose(ps_kt[:, 0:P], kn[:, :], k.ident[:, :]).then_inc(s["k_turned"], 1)

            def step(b, g):
                stage(b, g, 0, scores)
                stage(b, g, 1, turn_probs)
                stage(b + 1, g, 1, turn_q)
                stage(b + 1, g, 0, project)
                stage(b, g, 1, attend)
                stage(b, g, 2, out_proj)
                stage(b + 1, g, 1, turn_k)

            start_ahead(pe, "q_turned", "k_turned", "pv_done", "wo_done", "p_turned")
            program(pe, step)

        @block.vector
        def _(dve):
            def before(b):
                if type(b) is not int or b < B:
                    done(dve, "slot_hi", b)
                    nc.vector.tensor_tensor(xl[:, :, :], k.xn_t[:, :, cols(b, 0, P)], xh[:, :, :].bitcast(F32), ALU.subtract)
                    nc.vector.tensor_tensor(cl[:, :, :], k.ctx_t[:, :, cols(b, 0, P)], ch[:, :, :].bitcast(F32),
                                            ALU.subtract).then_inc(s["slot_lo"], 1)

            def masked_scores(b, g, n):
                done(dve, "scores_done", n)
                done(dve, "rnorm_done", n)
                freed(dve, "exp_done", n)
                for r in range(GH):
                    last = nc.vector.scalar_tensor_tensor(sc[:, r * P:(r + 1) * P], ps_s[:, r * P:(r + 1) * P],
                                                          rnorm[:, g, r:r + 1], k.mask[:, :], ALU.mult, ALU.add)
                last.then_inc(s["scores_read"], 1)
                done(dve, "scores_read", n)
                nc.vector.tensor_reduce(nmax[:, :], sc[:, :].rearrange("p (r e) -> p r e", r=GH), AX_X, ALU.max,
                                        negate=True).then_inc(s["nmax_done"], 1)

            def invert_sums(b, g, n):
                done(dve, "exp_done", n)
                freed(dve, "probn_done", n)
                nc.vector.reciprocal(rinv[:, :], rsum[:, :]).then_inc(s["rinv_done"], 1)

            def keep_probs(b, g, n):
                done(dve, "p_turned", n)
                freed(dve, "pv_done", n)
                nc.vector.tensor_copy(pt[:, :], ps_pt[:, :]).then_inc(s["pt_ready"], 1)

            def low_part_of_out(b, g, n):
                done(dve, "oh_ready", n)
                freed(dve, "wo_done", n)
                nc.vector.tensor_tensor(ol[:, :], ps_o[:, :], oh[:, :].bitcast(F32), ALU.subtract).then_inc(s["ol_ready"], 1)

            def add_out(b, g, n):
                if g == NKV0 - 1:
                    done(dve, "wo_done", n)
                    x_b = k.x_res[:, bass.ds(b, 1), :].rearrange("p o d -> p (o d)")
                    nc.vector.tensor_tensor(x_b, x_b, ps_y[:, 0:D], ALU.add).then_inc(s["y_added"], 1)

            def add_bias(b, g, n):
                done(dve, "proj_done", n)
                if type(b) is not int or n >= 2:
                    freed(dve, "q_turned", n - 1)
                    freed(dve, "kn_done", n - 1)
                    freed(dve, "v_ready", n - 1)
                bias = k.bias_a[:, g * 6 * P:(g + 1) * 6 * P]
                nc.vector.tensor_tensor(qkv[:, g % 2, 0:4 * P], ps_q[:, :], bias[:, 0:4 * P], ALU.add)
                nc.vector.tensor_tensor(qkv[:, g % 2, 4 * P:6 * P], ps_kv[:, 0:2 * P], bias[:, 4 * P:6 * P],
                                        ALU.add).then_inc(s["qkv_ready"], 1)

            def sum_squares(b, g, n):
                done(dve, "sq_done", n)
                freed(dve, "rnorm_done", n)
                nc.vector.tensor_reduce(ssum[:, :], sq[:, :].rearrange("p (r e) -> p r e", r=5), AX_X,
                                        ALU.add).then_inc(s["ssum_done"], 1)

            def step(b, g):
                stage(b, g, 0, masked_scores)
                stage(b, g, 1, keep_probs)
                stage(b + 1, g, 1, sum_squares)
                stage(b, g, 0, invert_sums)
                stage(b + 1, g, 0, add_bias)
                stage(b, g, 1, low_part_of_out)
                stage(b, g, 2, add_out)

            def split(g):
                dve.wait_ge(proj_hi, g + 1)
                nc.vector.tensor_tensor(k.wa_lo[:, g, PROJ], k.wa_raw[:, g % WA_SLOTS, PROJ],
                                        k.wa_hi[:, g, PROJ].bitcast(F32), ALU.subtract).then_inc(proj_lo, 1)

            start_ahead(dve, "qkv_ready", "pt_ready", "ol_ready", "scores_read", "y_added", "ssum_done")
            dve.wait_ge(k.norm_w_loaded, 16)
            nc.vector.scalar_tensor_tensor(k.key_scale[:, :], k.norm_w[:, 0:1], float(HD0) ** 0.5, k.norm_w[:, 1:2],
                                           ALU.mult, ALU.mult).then_inc(scaled, 1)
            dve.wait_ge(k.mask_loaded, 16)
            dve.wait_ge(k.bias_loaded, 16)
            program(dve, step, before, split)

        @block.scalar
        def _(act):
            def before(b):
                if type(b) is not int or 0 < b < B:
                    act.wait_ge(s["proj_done"], b * NKV0)
                if type(b) is not int or b < B:
                    nc.scalar.activation(xh[:, :, :], k.xn_t[:, :, cols(b, 0, P)], ACT.Copy)
                    nc.scalar.activation(ch[:, :, :], k.ctx_t[:, :, cols(b, 0, P)], ACT.Copy).then_inc(s["slot_hi"], 1)

            def exps(b, g, n):
                done(act, "nmax_done", n)
                freed(act, "probn_done", n)
                for r in range(GH):
                    last = nc.scalar.activation(prob[:, r * P:(r + 1) * P], sc[:, r * P:(r + 1) * P], ACT.Exp,
                                                bias=nmax[:, r:r + 1], accum_out=rsum[:, r:r + 1])
                last.then_inc(s["exp_done"], 1)

            def high_part_of_out(b, g, n):
                done(act, "pv_done", n)
                freed(act, "wo_done", n)
                nc.scalar.activation(oh[:, :], ps_o[:, :], ACT.Copy).then_inc(s["oh_ready"], 1)

            def squares(b, g, n):
                done(act, "qkv_ready", n)
                freed(act, "ssum_done", n)
                nc.scalar.activation(sq[:, :], qkv[:, g % 2, 0:5 * P], ACT.Square).then_inc(s["sq_done"], 1)

            def keep_q(b, g, n):
                done(act, "q_turned", n)
                nc.scalar.activation(qt[:, g, :], ps_qt[:, :], ACT.Copy).then_inc(s["qt_ready"], 1)

            def keep_k(b, g, n):
                done(act, "k_turned", n)
                nc.scalar.activation(kt[:, g, :], ps_kt[:, 0:P], ACT.Copy, scale=k.key_scale[:, 0:1]).then_inc(s["kt_ready"], 1)

            def keep_v(b, g, n):
                if type(b) is not int or b > 0:
                    done(act, "pv_done", n - NKV0)
                nc.scalar.activation(v[:, g, :], qkv[:, g % 2, 5 * P:6 * P], ACT.Copy).then_inc(s["v_ready"], 1)

            def step(b, g):
                stage(b + 1, g, 2, keep_k)
                stage(b + 1, g, 1, keep_q)
                stage(b, g, 0, exps)
                stage(b, g, 1, high_part_of_out)
                stage(b + 1, g, 1, keep_v)
                stage(b + 1, g, 0, squares)

            def split(g):
                act.wait_ge(k.wa_loaded[g % WA_SLOTS], 16 * (g // WA_SLOTS + 1))
                for part, sem in ((PROJ, proj_hi), (OUT, out_hi)):
                    nc.scalar.activation(k.wa_hi[:, g, part], k.wa_raw[:, g % WA_SLOTS, part], ACT.Copy).then_inc(sem, 1)

            start_ahead(act, "exp_done", "sq_done", "qt_ready", "kt_ready", "v_ready")
            act.wait_ge(k.ctx_loaded, 16)
            act.wait_ge(scaled, 1)
            program(act, step, before, split)

        @block.gpsimd
        def _(pool):
            def inverse_norms(b, g, n):
                done(pool, "ssum_done", n)
                nc.gpsimd.tensor_tensor(sume[:, :], ssum[:, :], k.eps_a[:, :], ALU.add).then_inc(s["sume_done"], 1)
                done(pool, "sume_done", n)
                nc.gpsimd.tensor_tensor(rnorm[:, g, :], sume[:, :], k.neg_half[:, 0:5], ALU.pow).then_inc(s["rnorm_done"], 1)
                done(pool, "rnorm_done", n)
                freed(pool, "k_turned", n)
                nc.gpsimd.tensor_tensor(kn[:, :], qkv[:, g % 2, 4 * P:5 * P], rnorm[:, g, 4:5].broadcast_to([P, P]),
                                        ALU.mult).then_inc(s["kn_done"], 1)

            def normed_probs(b, g, n):
                done(pool, "rinv_done", n)
                freed(pool, "p_turned", n)
                nc.gpsimd.tensor_tensor(probn[:, :].rearrange("p (r e) -> p r e", r=GH),
                                        prob[:, :].rearrange("p (r e) -> p r e", r=GH),
                                        rinv[:, :].rearrange("p (r o) -> p r o", o=1).broadcast_to([P, GH, P]),
                                        ALU.mult).then_inc(s["probn_done"], 1)

            def step(b, g):
                stage(b + 1, g, 1, inverse_norms)
                stage(b, g, 0, normed_probs)

            def split(g):
                pool.wait_ge(out_hi, g + 1)
                nc.gpsimd.tensor_tensor(k.wa_lo[:, g, OUT], k.wa_raw[:, g % WA_SLOTS, OUT],
                                        k.wa_hi[:, g, OUT].bitcast(F32), ALU.subtract).then_inc(out_lo, 1)

            start_ahead(pool, "probn_done", "kn_done", "rnorm_done")
            program(pool, step, split=split)


def router_and_layer1_keys(nc, io, k):
    with ExitStack() as ctx:
        m = Mem(nc, ctx)
        bank = banks(k)
        ps_logit_t, ps_logit, ps_comb = bank[0:2], bank[2], bank[3:5]
        side = banks(k, 5, 3)
        wqp = m.sb("e_wqp", [P, 2 * KC, D])
        amax = m.sb("e_amax", [P, 2 * KC])
        scale = m.sb("e_scale", [P, 2 * KC])
        inv = m.sb("e_inv", [P, 2 * KC])
        rounded = m.sb("e_rounded", [P, 2 * KC, D])
        scale_cols = m.sb("e_scale_cols", [P, 2 * KC, P])
        wkv = m.sb("e_wkv", [P, KC, 2 * D])
        wkv_hi = m.sb("e_wkv_hi", [P, KC, 2 * D], F32R)
        wkv_lo = m.sb("e_wkv_lo", [P, KC, 2 * D], F32R)
        ctx_hi = m.sb("e_ctx_hi", [P, KC, T], F32R)
        ctx_lo = m.sb("e_ctx_lo", [P, KC, T], F32R)
        bk = m.sb("e_bk", [P, KC])
        wsum = m.sb("e_wsum", [P, 3])
        ones = m.sb("e_ones", [P, P])
        stats = m.sb("c_stats", [P, B, 6])
        mv = m.sb("c_mv", [P, B, 2])
        vpe = m.sb("c_vpe", [P, B])
        rstd = m.sb("c_rstd", [P, B])
        xn = m.sb("c_xn", [P, B, D])
        logit_t = m.sb("c_logit_t", [NE, T])
        gw = m.sb("c_gw", [P, KC, NE])
        gw_hi = m.sb("c_gw_hi", [P, KC, NE], F32R)
        gw_lo = m.sb("c_gw_lo", [P, KC, NE], F32R)
        nmax = m.sb("c_nmax", [P, B])
        logit = m.sb("c_logit", [P, B, NE])
        ex = m.sb("c_ex", [P, B, NE])
        esum = m.sb("c_esum", [P, B])
        einv = m.sb("c_einv", [P, B])
        prob = m.sb("c_prob", [P, B, NE + TOPK])
        top = m.sb("c_top", [P, B, TOPK])
        tsum = m.sb("c_tsum", [P, 2, B])
        tinv = m.sb("c_tinv", [P, 2, B])
        cum = m.sb("c_cum", [P, B, TOPK])
        kept = m.sb("c_kept", [P, B, TOPK])
        left = m.sb("c_left", [P, B, TOPK])
        find = m.sb("c_find", [P, B, TOPK])
        rest = m.sb("c_rest", [P, B, NE + TOPK])
        sel = m.sb("c_sel", [P, B, NE])
        comb = m.sb("c_comb", [P, B, NE])
        comb_t = m.sb("c_comb_t", [NE, T])
        names = ("gw_loaded", "gw_hi", "gw_lo", "stats", "mv", "vpe", "rstd", "xn_ready", "x_turned", "x_hi", "x_lo",
                 "logits_t", "logits_t_kept",
                 "logits", "exps", "probs", "comb_ready", "comb_turned", "comb_kept", "comb_stored", "chain",
                 "wkv_loaded", "wqp_loaded", "w_hi", "bk_loaded", "small_loaded", "kv_hi", "kv_lo", "side_made", "side_kept",
                 "row_scales", "scale_cols", "row_rounded", "clipped", "ones_set", "sums", "gamma_made")
        s = {n: m.sem(f"c_{n}") for n in names}
        wf_loaded = [m.sem(f"c_wf_loaded{j}") for j in range(3)]
        k.w_loaded = [m.sem(f"d_w_loaded{j}") for j in range(3)]
        block = ctx.enter_context(nc.Block())

        @block.sync
        def _(sp):
            sp.dma_start(gw[:, :, :], io["gate_t"]).then_inc(s["gw_loaded"], 16)
            sp.dma_start(wqp[:, :, :], io["wqp"]).then_inc(s["wqp_loaded"], 16)
            sp.dma_start(wkv[:, :, :], io["wkv_t"]).then_inc(s["wkv_loaded"], 16)
            sp.dma_start(bk[:, :], io["bk1"]).then_inc(s["bk_loaded"], 16)
            for j in range(3):
                sp.dma_start(k.raw[:, j, :], io["wm"][j]).then_inc(k.w_loaded[j], 16)
            for j in range(3):
                sp.dma_start(k.wf[:, j, :], io[("gate_w", "val_w", "out_w")[j]]).then_inc(wf_loaded[j], 16)
            sp.dma_start(k.bq[:, :], io["bq1"]).then_inc(s["small_loaded"], 16)
            sp.dma_start(k.bv[:, :], io["bv1"].partition_broadcast(P)).then_inc(s["small_loaded"], 16)
            sp.dma_start(k.bias1[:, :], io["bias1"].partition_broadcast(P)).then_inc(s["small_loaded"], 16)
            sp.wait_ge(s["small_loaded"], 48)
            sp.wait_ge(s["comb_kept"], 2)
            sp.dma_start(k.comb_dram, comb_t[:, :]).then_inc(s["comb_stored"], 16)
            sp.wait_ge(s["comb_stored"], 16)

        @block.gpsimd
        def _(pool):
            pool.wait_ge(s["mv"], B)
            nc.gpsimd.tensor_scalar(vpe[:, :], mv[:, :, 1], 1e-5, None, ALU.add).then_inc(s["vpe"], 1)
            pool.wait_ge(s["vpe"], 1)
            nc.gpsimd.tensor_tensor(rstd[:, :], vpe[:, :], k.neg_half[:, 0:B], ALU.pow).then_inc(s["rstd"], 1)
            nc.gpsimd.memset(ones[:, :], 1.0).then_inc(s["ones_set"], 1)
            pool.wait_ge(s["kv_hi"], 1)
            nc.gpsimd.tensor_tensor(ctx_lo[:, :, :], k.ctx_t[:, :, :], ctx_hi[:, :, :].bitcast(F32), ALU.subtract).then_inc(s["kv_lo"], 1)
            pool.wait_ge(s["kv_hi"], 2)
            nc.gpsimd.tensor_tensor(wkv_lo[:, :, :], wkv[:, :, :], wkv_hi[:, :, :].bitcast(F32), ALU.subtract).then_inc(s["kv_lo"], 1)
            pool.wait_ge(s["w_hi"], 1)
            nc.gpsimd.tensor_tensor(k.w_lo[:, 0, :], k.raw[:, 0, :], k.w_hi[:, 0, :].bitcast(F32), ALU.subtract)
            pool.wait_ge(s["row_rounded"], 1)
            nc.gpsimd.tensor_scalar(rounded[:, :, :], wqp[:, :, :], RND + 127.0, RND - 127.0, ALU.min, ALU.max
                                    ).then_inc(s["clipped"], 1)

        @block.vector
        def _(dve):
            for t in range(B):
                nc.vector.bn_stats(stats[:, t, :], k.x_res[:, t, :]).then_inc(s["stats"], 1)
            for t in range(B):
                dve.wait_ge(s["stats"], t + 1)
                nc.vector.bn_aggr(mv[:, t, :], stats[:, t, :]).then_inc(s["mv"], 1)
            dve.wait_ge(s["wqp_loaded"], 16)
            nc.vector.tensor_reduce(amax[:, :], wqp[:, :, :], AX_X, ALU.max, apply_absolute_value=True).then_inc(s["row_scales"], 1)
            nc.vector.memset(prob[:, :, NE:], -1.0)
            dve.wait_ge(s["gw_hi"], 1)
            nc.vector.tensor_tensor(gw_lo[:, :, :], gw[:, :, :], gw_hi[:, :, :].bitcast(F32), ALU.subtract).then_inc(s["gw_lo"], 1)
            dve.wait_ge(s["row_scales"], 1)
            nc.vector.tensor_scalar(scale[:, :], amax[:, :], 1.0 / 127.0, 1e-8, ALU.mult, ALU.max).then_inc(s["row_scales"], 1)
            dve.wait_ge(s["rstd"], 1)

            for t in range(B):
                nc.vector.tensor_scalar(xn[:, t, :], k.x_res[:, t, :], mv[:, t, 0:1], rstd[:, t:t + 1],
                                        ALU.subtract, ALU.mult).then_inc(s["xn_ready"], 1)
            dve.wait_ge(s["row_scales"], 2)
            nc.vector.reciprocal(inv[:, :], scale[:, :]).then_inc(s["row_scales"], 1)
            nc.vector.tensor_copy(k.wq_scale[:, :], scale[:, 0:KC])
            nc.vector.tensor_copy(scale_cols[:, :, :], scale[:, :].rearrange("p (r o) -> p r o", o=1).broadcast_to(
                [P, 2 * KC, P])).then_inc(s["scale_cols"], 1)
            for t in range(B):
                dve.wait_ge(s["x_hi"], t + 1)
                x_hi = k.xn_hi[:, :, t * P:(t + 1) * P]
                nc.vector.tensor_tensor(k.xn_lo[:, :, t * P:(t + 1) * P], bank[t][:, 0:D].rearrange("p (c n) -> p c n", c=KC),
                                        x_hi.bitcast(F32), ALU.subtract).then_inc(s["x_lo"], 1)
            dve.wait_ge(s["logits_t"], 1)
            nc.vector.tensor_copy(logit_t[:, 0:T // 2], ps_logit_t[0][0:NE, :]).then_inc(s["logits_t_kept"], 1)

            at = [0]

            def chained(ins):
                at[0] += 1
                ins.then_inc(s["chain"], 1)
                dve.wait_ge(s["chain"], at[0])

            wide = [P, B, NE]
            by_token = lambda a, n: a.rearrange("p (b o) -> p b o", o=1).broadcast_to([P, B, n])
            logits = ps_logit[:, 0:B * NE].rearrange("p (b e) -> p b e", b=B)
            dve.wait_ge(s["logits"], 1)
            chained(nc.vector.tensor_reduce(nmax[:, :], logits, AX_X, ALU.max, negate=True))
            nc.vector.tensor_tensor(logit[:, :, :], logits, by_token(nmax[:, :], NE), ALU.add).then_inc(s["probs"], 1)
            dve.wait_ge(s["exps"], 1)
            chained(nc.vector.tensor_reduce(esum[:, :], ex[:, :, :], AX_X, ALU.add))
            chained(nc.vector.reciprocal(einv[:, :], esum[:, :]))
            chained(nc.vector.tensor_tensor(prob[:, :, 0:NE], ex[:, :, :], by_token(einv[:, :], NE), ALU.mult))
            for t in range(B):
                last = nc.vector.max(top[:, t, :], prob[:, t, 0:NE])
            chained(last)
            chained(nc.vector.tensor_reduce(tsum[:, 0, :], top[:, :, :], AX_X, ALU.add))
            chained(nc.vector.tensor_scalar(tsum[:, 0, :], tsum[:, 0, :], 1e-12, None, ALU.max))
            chained(nc.vector.reciprocal(tinv[:, 0, :], tsum[:, 0, :]))
            chained(nc.vector.tensor_tensor(cum[:, :, :], top[:, :, :], by_token(tinv[:, 0, :], TOPK), ALU.mult))
            for j in range(1, TOPK):
                chained(nc.vector.tensor_tensor(cum[:, :, j], cum[:, :, j - 1], cum[:, :, j], ALU.add))
            nc.vector.tensor_copy(kept[:, :, 0], top[:, :, 0])
            nc.vector.tensor_copy(find[:, :, 0], top[:, :, 0])
            nc.vector.tensor_scalar(left[:, :, 1:], cum[:, :, 0:TOPK - 1], THRESHOLD, 1.0, ALU.is_lt, ALU.subtract)
            chained(nc.vector.scalar_tensor_tensor(kept[:, :, 1:], cum[:, :, 0:TOPK - 1], THRESHOLD, top[:, :, 1:],
                                                   ALU.is_lt, ALU.mult))
            nc.vector.tensor_tensor(find[:, :, 1:], kept[:, :, 1:], left[:, :, 1:], ALU.add)
            chained(nc.vector.tensor_reduce(tsum[:, 1, :], kept[:, :, :], AX_X, ALU.add))
            chained(nc.vector.tensor_scalar(tsum[:, 1, :], tsum[:, 1, :], 1e-12, None, ALU.max))
            chained(nc.vector.reciprocal(tinv[:, 1, :], tsum[:, 1, :]))
            for t in range(B):
                last = nc.vector.match_replace(rest[:, t, :], find[:, t, :], prob[:, t, :], -2.0)
            chained(last)
            chained(nc.vector.tensor_tensor(sel[:, :, :], rest[:, :, 0:NE], prob[:, :, 0:NE], ALU.not_equal))
            chained(nc.vector.tensor_tensor(sel[:, :, :], sel[:, :, :], prob[:, :, 0:NE], ALU.mult))
            nc.vector.tensor_tensor(comb[:, :, :], sel[:, :, :], by_token(tinv[:, 1, :], NE), ALU.mult).then_inc(s["comb_ready"], 1)
            dve.wait_ge(s["comb_turned"], 1)
            nc.vector.tensor_copy(comb_t[:, 0:T // 2], ps_comb[0][0:NE, :]).then_inc(s["comb_kept"], 1)
            for j in range(1, 3):
                dve.wait_ge(wf_loaded[j], 16)
                last = nc.vector.tensor_reduce(wsum[:, j:j + 1], k.wf[:, j, :], AX_X, ALU.add, apply_absolute_value=True)
            last.then_inc(s["sums"], 1)
            dve.wait_ge(s["gamma_made"], 1)
            chained(nc.vector.tensor_scalar(k.gamma[:, :], side[0][:, 0:3], 1.0 / (D * HIDDEN), 1e-5, ALU.mult, ALU.max))
            nc.vector.reciprocal(k.ginv[:, :], k.gamma[:, :])

        @block.scalar
        def _(act):
            act.wait_ge(s["gw_loaded"], 16)
            nc.scalar.activation(gw_hi[:, :, :], gw[:, :, :], ACT.Copy).then_inc(s["gw_hi"], 1)
            nc.scalar.activation(ctx_hi[:, :, :], k.ctx_t[:, :, :], ACT.Copy).then_inc(s["kv_hi"], 1)
            act.wait_ge(s["wkv_loaded"], 16)
            nc.scalar.activation(wkv_hi[:, :, :], wkv[:, :, :], ACT.Copy).then_inc(s["kv_hi"], 1)
            for t in range(B):
                act.wait_ge(s["x_turned"], t + 1)
                nc.scalar.activation(k.xn_hi[:, :, t * P:(t + 1) * P], bank[t][:, 0:D].rearrange("p (c n) -> p c n", c=KC),
                                     ACT.Copy).then_inc(s["x_hi"], 1)
            act.wait_ge(s["logits_t"], 2)
            nc.scalar.activation(logit_t[:, T // 2:], ps_logit_t[1][0:NE, :], ACT.Copy).then_inc(s["logits_t_kept"], 1)
            act.wait_ge(k.w_loaded[0], 16)
            nc.scalar.activation(k.w_hi[:, 0, :], k.raw[:, 0, :], ACT.Copy).then_inc(s["w_hi"], 1)
            act.wait_ge(s["probs"], 1)
            nc.scalar.activation(ex[:, :, :], logit[:, :, :], ACT.Exp).then_inc(s["exps"], 1)
            act.wait_ge(s["row_scales"], 3)
            for r in range(2 * KC):
                last = nc.scalar.activation(wqp[:, r, :], wqp[:, r, :], ACT.Copy, bias=RND, scale=inv[:, r:r + 1])
            last.then_inc(s["row_rounded"], 1)
            act.wait_ge(s["bk_loaded"], 16)
            for n in range(4):
                c, half = n // 2, n % 2
                act.wait_ge(s["side_made"], n + 1)
                nc.scalar.activation(k.k1_t[:, c, half * 512:(half + 1) * 512], side[n % 3][:, :], ACT.Identity,
                                     bias=bk[:, c:c + 1]).then_inc(s["side_kept"], 1)
            for n in range(4, 8):
                act.wait_ge(s["side_made"], n + 1)
                nc.scalar.activation(k.v1[:, 2 * (n - 4):2 * (n - 3), :], side[n % 3][:, :].rearrange("p (b d) -> p b d", b=2),
                                     ACT.Copy).then_inc(s["side_kept"], 1)
            act.wait_ge(s["comb_turned"], 1)
            nc.scalar.activation(comb_t[:, T // 2:], ps_comb[1][0:NE, :], ACT.Copy).then_inc(s["comb_kept"], 1)
            for n in range(8, 10):
                act.wait_ge(s["side_made"], n + 1)
                nc.scalar.activation(k.wqp_t[:, n - 8, :, :], side[n % 3][:, :].rearrange("p (c n) -> p c n", c=KC),
                                     ACT.Copy, bias=-RND).then_inc(s["side_kept"], 1)
            act.wait_ge(s["side_made"], 11)
            nc.scalar.activation(k.scale_qp[:, :], side[10 % 3][:, :], ACT.Copy).then_inc(s["side_kept"], 1)
            act.wait_ge(wf_loaded[0], 16)
            nc.scalar.activation(k.w_ffn[:, 0, :], k.wf[:, 0, :], ACT.Abs, accum_out=wsum[:, 0:1]).then_inc(s["sums"], 1)

        @block.tensor
        def _(pe):
            for t in range(B):
                pe.wait_ge(s["xn_ready"], t + 1)
                for c in range(KC):
                    last = nc.tensor.transpose(bank[t][:, c * P:(c + 1) * P], xn[:, t, c * P:(c + 1) * P], k.ident[:, :])
                last.then_inc(s["x_turned"], 1)
            pe.wait_ge(s["gw_lo"], 1)
            pe.wait_ge(s["x_lo"], B)
            for half in range(2):
                for c in range(KC):
                    x_hi, x_lo = (x[:, c, half * T // 2:(half + 1) * T // 2] for x in (k.xn_hi, k.xn_lo))
                    out = ps_logit_t[half][0:NE, :]
                    nc.tensor.matmul(out, gw_hi[:, c, :], x_hi, start=c == 0, stop=False)
                    nc.tensor.matmul(out, gw_lo[:, c, :], x_hi, start=False, stop=False)
                    last = nc.tensor.matmul(out, gw_hi[:, c, :], x_lo, start=False, stop=c == KC - 1)
                last.then_inc(s["logits_t"], 1)
            pe.wait_ge(s["logits_t_kept"], 2)
            for t in range(B):
                last = nc.tensor.transpose(ps_logit[:, t * NE:(t + 1) * NE], logit_t[:, t * P:(t + 1) * P], k.ident[0:NE, 0:NE])
            last.then_inc(s["logits"], 1)

            def side_free(n):
                if n >= 3:
                    pe.wait_ge(s["side_kept"], n - 2)
                return side[n % 3]

            pe.wait_ge(s["kv_lo"], 2)
            for n in range(4):
                c, half = n // 2, n % 2
                ps = side_free(n)
                for kc in range(KC):
                    w_hi, w_lo = (w[:, kc, c * P:(c + 1) * P] for w in (wkv_hi, wkv_lo))
                    c_hi, c_lo = (a[:, kc, half * 512:(half + 1) * 512] for a in (ctx_hi, ctx_lo))
                    nc.tensor.matmul(ps[:, :], w_hi, c_hi, start=kc == 0, stop=False)
                    nc.tensor.matmul(ps[:, :], w_hi, c_lo, start=False, stop=False)
                    last = nc.tensor.matmul(ps[:, :], w_lo, c_hi, start=False, stop=kc == KC - 1)
                last.then_inc(s["side_made"], 1)
            for n in range(4, 8):
                ps = side_free(n)
                for b in (2 * (n - 4), 2 * (n - 4) + 1):
                    out = ps[:, b % 2 * D:(b % 2 + 1) * D]
                    for kc in range(KC):
                        w_hi, w_lo = (w[:, kc, D:2 * D] for w in (wkv_hi, wkv_lo))
                        c_hi, c_lo = (a[:, kc, b * P:(b + 1) * P] for a in (ctx_hi, ctx_lo))
                        nc.tensor.matmul(out, c_hi, w_hi, start=kc == 0, stop=False)
                        nc.tensor.matmul(out, c_hi, w_lo, start=False, stop=False)
                        last = nc.tensor.matmul(out, c_lo, w_hi, start=False, stop=kc == KC - 1)
                last.then_inc(s["side_made"], 1)
            pe.wait_ge(s["comb_ready"], 1)
            for t in range(B):
                last = nc.tensor.transpose(ps_comb[t // 4][0:NE, t % 4 * P:(t % 4 + 1) * P], comb[:, t, :], k.ident[:, :])
            last.then_inc(s["comb_turned"], 1)
            pe.wait_ge(s["clipped"], 1)
            for n in range(8, 10):
                ps = side_free(n)
                for r in range(KC):
                    for c in range(KC):
                        last = nc.tensor.transpose(ps[:, c * D + r * P:c * D + (r + 1) * P],
                                                   rounded[:, (n - 8) * KC + r, c * P:(c + 1) * P], k.ident[:, :])
                last.then_inc(s["side_made"], 1)
            ps = side_free(10)
            pe.wait_ge(s["scale_cols"], 1)
            for r in range(2 * KC):
                last = nc.tensor.matmul(ps[:, r * P:(r + 1) * P], scale_cols[:, r, :], k.ident[:, :], start=True, stop=True)
            last.then_inc(s["side_made"], 1)
            pe.wait_ge(s["ones_set"], 1)
            pe.wait_ge(s["sums"], 2)
            pe.wait_ge(s["side_kept"], 10)
            nc.tensor.matmul(side[0][:, 0:3], ones[:, :], wsum[:, :], start=True, stop=True).then_inc(s["gamma_made"], 1)


def experts(nc, io, k):
    with ExitStack() as ctx:
        m = Mem(nc, ctx)
        ps_g, ps_u = banks(k, 0, 2), banks(k, 2, 2)
        acc = banks(k, 4, 4)
        HALF = T // 2
        raw, w_hi, w_lo, w_loaded = k.raw, k.w_hi, k.w_lo, k.w_loaded
        weight = m.sb("d_weight", [P, 3, T])
        silu = m.sb("d_silu", [P, 2, HALF])
        gu = m.sb("d_gu", [P, 2, HALF])
        h = m.sb("d_h", [P, 2, HALF])
        h_hi = m.sb("d_h_hi", [P, 2, HALF], F32R)
        h_lo = m.sb("d_h_lo", [P, 2, HALF], F32R)
        y_t = m.sb("d_y_t", [P, KC, T])
        ahead = ("gu_done", "h_done", "down_done", "lo_done", "h_lo_done")
        plain = ("gate_up_done", "silu_done", "h_hi_done", "hi_done", "acc_kept", "y_turned", "y_added",
                 "piece_rounded", "piece_clipped")
        s = {n: m.sem(f"d_{n}") for n in ahead + plain}
        weight_loaded = [m.sem(f"d_weight_loaded{j}") for j in range(3)]
        block = ctx.enter_context(nc.Block())
        SEGMENTS = [(j, max(q * INTER, j * P) - j * P, min((q + 1) * INTER, (j + 1) * P) - j * P, q)
                    for j in range(3) for q in range(4) if q * INTER < (j + 1) * P and (q + 1) * INTER > j * P]

        def done(eng, name, n):
            eng.wait_ge(s[name], n + (2 if name in ahead else 1))

        def freed(eng, name, n):
            if type(n) is not int or n >= 2:
                eng.wait_ge(s[name], n)

        def stage(i, u, lag, work):
            i, u = (i, u - lag) if u >= lag else (i - 1, u - lag + 6)
            if type(i) is not int or 0 <= i < MT // 3:
                work(i, u // 2, u % 2, i * 6 + u)

        def program(eng, step):
            for u in range(6):
                step(0, u)
            with eng.Fori(1, MT // 3 - 1) as i:
                for u in range(6):
                    step(i, u)
            for i, steps in ((MT // 3 - 1, 6), (MT // 3, 2)):
                for u in range(steps):
                    step(i, u)

        def next_tile(i, u, work):
            j = u // 2 + 1
            if u % 2 == 0 and not (type(i) is int and i * 3 + j >= MT):
                work(*((i, j) if j < 3 else (i + 1, 0)))

        def piece(a, n):
            return a[:, n // 2, n % 2 * HIDDEN:(n % 2 + 1) * HIDDEN]

        @block.sync
        def _(sp):
            def load(i, j):
                if type(i) is not int:
                    sp.wait_ge(s["lo_done"], i * 3 + (j - 1))
                    sp.dma_start(raw[:, j, :], io["wm"][bass.ds(i * 3 + j, 1)].rearrange("o p n -> p (o n)")
                                 ).then_inc(w_loaded[j], 16)
                    sp.wait_ge(s["h_done"], i * 6 + (2 * j - 3))
                for jj, a, b, q in SEGMENTS:
                    if jj == j:
                        sp.dma_start(weight[a:b, j, :], k.comb_dram[bass.ds(i * 4 + q, 1), :].broadcast_to([b - a, T])
                                     ).then_inc(weight_loaded[j], 16)

            for j in range(3):
                load(0, j)
            with sp.Fori(1, MT // 3) as i:
                for j in range(3):
                    load(i, j)

        @block.tensor
        def _(pe):
            def gate_up(i, j, half, n):
                if half == 0:
                    done(pe, "lo_done", i * 3 + j)
                freed(pe, "gu_done", n)
                for ps, at in ((ps_g[half], 0), (ps_u[half], KC * P)):
                    for c in range(KC):
                        hi, lo = (w[:, j, at + c * P:at + (c + 1) * P] for w in (w_hi, w_lo))
                        x_hi, x_lo = (x[:, c, half * HALF:(half + 1) * HALF] for x in (k.xn_hi, k.xn_lo))
                        nc.tensor.matmul(ps[:, :], hi, x_hi, start=c == 0, stop=False)
                        nc.tensor.matmul(ps[:, :], hi, x_lo, start=False, stop=False)
                        last = nc.tensor.matmul(ps[:, :], lo, x_hi, start=False, stop=c == KC - 1)
                last.then_inc(s["gate_up_done"], 1)

            def down(i, j, half, n):
                done(pe, "h_lo_done", n)
                first = type(i) is int and i == 0 and j == 0
                for c in range(KC):
                    hi, lo = (w[:, j, 2 * KC * P + c * P:2 * KC * P + (c + 1) * P] for w in (w_hi, w_lo))
                    out = acc[2 * c + half]
                    nc.tensor.matmul(out[:, :], hi, h_hi[:, half, :], start=first, stop=False, skip_group_check=True)
                    nc.tensor.matmul(out[:, :], hi, h_lo[:, half, :], start=False, stop=False, skip_group_check=True)
                    last = nc.tensor.matmul(out[:, :], lo, h_hi[:, half, :], start=False, stop=True, skip_group_check=True)
                last.then_inc(s["down_done"], 1)

            def step(i, u):
                stage(i, u, 0, gate_up)
                stage(i, u, 2, down)

            pe.sem_inc(s["down_done"], 1)
            program(pe, step)
            pe.wait_ge(s["acc_kept"], 4)
            for t in range(B):
                if t >= 4:
                    pe.wait_ge(s["y_added"], t - 3)
                ps = (ps_g + ps_u)[t % 4]
                for c in range(KC):
                    last = nc.tensor.transpose(ps[:, c * P:(c + 1) * P], y_t[:, c, t * P:(t + 1) * P], k.ident[:, :])
                last.then_inc(s["y_turned"], 1)

        @block.scalar
        def _(act):
            def hi_part(i, j):
                act.wait_ge(w_loaded[j], i * 16 + 16)
                if type(i) is not int or i > 0:
                    act.wait_ge(s["down_done"], i * 6 + (2 * j - 3))
                nc.scalar.activation(w_hi[:, j, :], raw[:, j, :], ACT.Copy).then_inc(s["hi_done"], 1)

            def silus(i, j, half, n):
                done(act, "gate_up_done", n)
                freed(act, "gu_done", n)
                nc.scalar.activation(silu[:, half, :], ps_g[half][:, :], ACT.Silu).then_inc(s["silu_done"], 1)

            def h_high(i, j, half, n):
                done(act, "h_done", n)
                freed(act, "down_done", n)
                nc.scalar.activation(h_hi[:, half, :], h[:, half, :], ACT.Copy).then_inc(s["h_hi_done"], 1)

            def step(i, u):
                stage(i, u, 0, silus)
                stage(i, u, 1, h_high)
                next_tile(i, u, hi_part)
                if type(i) is int and i == 0:
                    nc.scalar.activation(piece(k.wf, u), piece(k.wf, u), ACT.Copy, bias=RND, scale=k.ginv[:, u // 2:u // 2 + 1]
                                         ).then_inc(s["piece_rounded"], 1)
                    if u >= 1:
                        integers(u - 1)

            def integers(n):
                act.wait_ge(s["piece_clipped"], n + 1)
                nc.scalar.activation(piece(k.w_ffn, n), piece(k.wf, n), ACT.Copy, bias=-RND)

            act.sem_inc(s["hi_done"], 1)
            program(act, step)
            integers(5)
            done(act, "down_done", 2 * MT - 1)
            for n in (2, 3):
                nc.scalar.activation(y_t[:, n // 2, n % 2 * HALF:(n % 2 + 1) * HALF], acc[n][:, :], ACT.Copy).then_inc(s["acc_kept"], 1)

        @block.vector
        def _(dve):
            def lo_part(i, j):
                dve.wait_ge(s["hi_done"], i * 3 + (j + 1))
                nc.vector.tensor_tensor(w_lo[:, j, :], raw[:, j, :], w_hi[:, j, :].bitcast(F32),
                                        ALU.subtract).then_inc(s["lo_done"], 1)

            def gate_times_up(i, j, half, n):
                done(dve, "silu_done", n)
                freed(dve, "h_done", n)
                nc.vector.tensor_tensor(gu[:, half, :], silu[:, half, :], ps_u[half][:, :], ALU.mult).then_inc(s["gu_done"], 1)

            def h_low(i, j, half, n):
                done(dve, "h_hi_done", n)
                nc.vector.tensor_tensor(h_lo[:, half, :], h[:, half, :], h_hi[:, half, :].bitcast(F32),
                                        ALU.subtract).then_inc(s["h_lo_done"], 1)

            def step(i, u):
                stage(i, u, 0, gate_times_up)
                stage(i, u, 1, h_low)
                next_tile(i, u, lo_part)
                if type(i) is int and i == 0:
                    dve.wait_ge(s["piece_rounded"], u + 1)
                    nc.vector.tensor_scalar(piece(k.wf, u), piece(k.wf, u), RND + 1.0, RND - 1.0, ALU.min, ALU.max
                                            ).then_inc(s["piece_clipped"], 1)

            dve.sem_inc(s["gu_done"], 1)
            dve.sem_inc(s["lo_done"], 2)
            dve.sem_inc(s["h_lo_done"], 1)
            program(dve, step)
            done(dve, "down_done", 2 * MT - 1)
            for n in (0, 1):
                nc.vector.tensor_copy(y_t[:, n // 2, n % 2 * HALF:(n % 2 + 1) * HALF], acc[n][:, :]).then_inc(s["acc_kept"], 1)
            for t in range(B):
                dve.wait_ge(s["y_turned"], t + 1)
                nc.vector.tensor_tensor(k.x_res[:, t, :], k.x_res[:, t, :], (ps_g + ps_u)[t % 4][:, 0:D],
                                        ALU.add).then_inc(s["y_added"], 1)

        @block.gpsimd
        def _(pool):
            def weigh(i, j, half, n):
                done(pool, "gu_done", n)
                if half == 0:
                    pool.wait_ge(weight_loaded[j], i * 32 + 32)
                freed(pool, "h_lo_done", n)
                nc.gpsimd.tensor_tensor(h[:, half, :], gu[:, half, :], weight[:, j, half * HALF:(half + 1) * HALF],
                                        ALU.mult).then_inc(s["h_done"], 1)

            pool.sem_inc(s["h_done"], 1)
            program(pool, lambda i, u: stage(i, u, 0, weigh))


def layer1(nc, io, k, out):
    with ExitStack() as ctx:
        m = Mem(nc, ctx)
        QH = NH1 // 4
        VW = P // QH
        FH = HIDDEN // 2
        ps_s = banks(k, 0, 2)
        (ps_t,) = banks(k, 2, 1)
        (ps_turn,) = banks(k, 3, 1)
        ps_g, ps_v, ps_m, ps_o = banks(k, 4, 4)
        ps_m = ps_m[:, 0:D]
        q0 = m.sb("f_q0", [P, D])
        q_t = m.sb("f_q_t", [P, KC, P])
        v_now = m.sb("f_v_now", [P, NH1, VW])
        o_t = m.sb("f_o_t", [P, QH * P])
        kd = m.sb("f_kd", [P, KC, HC, P])
        nmax = m.sb("f_nmax", [P, NH1])
        prob = m.sb("f_prob", [P, NH1, P])
        prob_t = m.sb("f_prob_t", [P, NH1, P])
        sinv = m.sb("f_sinv", [P, NH1])
        o = m.sb("f_o", [P, D])
        o_rnd = m.sb("f_o_rnd", [P, D])
        oi_t = m.sb("f_oi_t", [P, KC, P], BF16)
        y = m.sb("f_y", [P, D])
        stats = m.sb("f_stats", [P, B, 6])
        mv3 = m.sb("f_mv3", [P, B, 2])
        stats4 = m.sb("f_stats4", [P, 6])
        mv4 = m.sb("f_mv4", [P, 2])
        vpe = m.sb("f_vpe", [P, B])
        rstd3 = m.sb("f_rstd3", [P, B])
        vpe4 = m.sb("f_vpe4", [P, 1])
        rstd4 = m.sb("f_rstd4", [P, 1])
        eps = m.sb("f_eps", [P, B])
        scale3 = m.sb("f_scale3", [P, B])
        scale_now = m.sb("f_scale_now", [P, 1])
        xs = m.sb("f_xs", [P, D])
        stats4_seen = m.sb("f_stats4_seen", [P, 6])
        scale4 = m.sb("f_scale4", [P, 1])
        unit = m.sb("f_unit", [P, 2, B])
        gamma = m.sb("f_gamma", [P, 2])
        norm = {n: m.sb(f"f_xn{n}", [P, D]) for n in (3, 4)}
        rnd = {n: m.sb(f"f_rnd{n}", [P, D]) for n in (3, 4)}
        amax = {n: m.sb(f"f_amax_{n}", [P, 1]) for n in (3, 4, "o", "h")}
        inv = {n: m.sb(f"f_inv_{n}", [P, 1]) for n in (3, 4, "o", "h")}
        raw_rnd = {n: m.sb(f"f_raw_rnd_{n}", [P, D]) for n in (3, 4, "o")}
        o_scale = m.sb("f_o_scale", [P, 1])
        x3_t = m.sb("f_x3_t", [P, KC, T], BF16)
        x4_t = m.sb("f_x4_t", [P, KC, T], BF16)
        gate = m.sb("f_gate", [P, HIDDEN])
        tanh = m.sb("f_tanh", [P, HIDDEN])
        product = m.sb("f_gate_val", [P, HIDDEN])
        half_bv = m.sb("f_half_bv", [P, HIDDEN])
        val = m.sb("f_val", [P, HIDDEN])
        h = m.sb("f_h", [P, HIDDEN])
        h_scale = m.sb("f_h_scale", [P, 1])
        h_unit = m.sb("f_h_unit", [P, 1])
        h_rnd0 = m.sb("f_h_rnd0", [P, HIDDEN])
        h_rnd = m.sb("f_h_rnd", [P, HIDDEN])
        hi_t = m.sb("f_hi_t", [P, HIDDEN], BF16)
        names = ["halved", "all_stats", "all_mv", "eps_set", "all_vpe", "all_rstd",
                 "q_proj", "q_scaled", "q_turned", "q_kept", "v_now", "o_t_kept", "o_back", "sinv", "o", "o_amax", "o_scale", "o_inv", "o_raw", "o_rnd",
                 "o_turned", "o_kept", "out", "out_read", "added", "x_kept",
                 "xn3", "amax3", "scale3", "inv3", "raw3", "rnd3", "scale3_kept", "x3_turned", "x3_kept", "bias3",
                 "stats4", "mv4", "vpe4", "rstd4", "xn4", "amax4", "scale4", "inv4", "raw4", "rnd4", "x4_turned", "x4_kept",
                 "bias4", "units", "h_amax", "h_scale", "h_inv", "h_unit", "h_rnd0", "h_rnd", "ffn_out", "x_done", "stored"]
        for n, count in (("scores", 4), ("nmax", 4), ("exps", 4), ("quarter", 4), ("quarter_kept", 4), ("pv", 4), ("keys", 2),
                         ("mm_gate", 2), ("mm_val", 2), ("gate", 2), ("val", 2), ("tanh", 2), ("product", 2), ("h", 2), ("h_turned", 2),
                         ("h_kept", 2)):
            names += [f"{n}{j}" for j in range(count)]
        s = {n: m.sem(f"f_{n}") for n in names}
        block = ctx.enter_context(nc.Block())

        ahead = ("h_kept1", "x_done", "h_turned1", "ffn_out")

        def done(eng, name, b):
            if type(b) is not int or 0 <= b < B:
                eng.wait_ge(s[name], b + (2 if name in ahead else 1))

        def stage(b, work, *args):
            if type(b) is not int or 0 <= b < B:
                work(b, *args)

        def program(eng, step):
            for b in range(-2, 4):
                step(b)
            with eng.Fori(4, B - 2) as b:
                step(b)
            for b in range(B - 2, B + 4):
                step(b)

        def x_of(b):
            return k.x_res[:, bass.ds(b, 1), :].rearrange("p o d -> p (o d)")

        def turn(src, n):
            for c in range(n):
                last = nc.tensor.transpose(ps_turn[:, c * P:(c + 1) * P], src[:, c * P:(c + 1) * P], k.ident[:, :])
            return last

        @block.tensor
        def _(pe):
            def bank_free(*uses):
                for name, b in uses:
                    done(pe, name, b)

            def scores(b, j):
                c = j // 2
                done(pe, "q_kept", b)
                done(pe, f"keys{c}", b)
                done(pe, f"exps{(j + 2) % 4}", b if j >= 2 else b - 1)
                nc.tensor.matmul(ps_s[j % 2][:, :], q_t[:, c, :], kd[:, c, j % 2 * QH:(j % 2 + 1) * QH, :],
                                 start=True, stop=True).then_inc(s[f"scores{j}"], 1)

            def turn_probs(b, j):
                done(pe, f"exps{j}", b)
                done(pe, f"quarter_kept{(j + 3) % 4}", b if j >= 1 else b - 1)
                for r in range(QH):
                    last = nc.tensor.transpose(ps_t[:, r * P:(r + 1) * P], prob[:, QH * j + r, :], k.ident[:, :])
                last.then_inc(s[f"quarter{j}"], 1)

            def attend(b, j):
                if j == 0:
                    done(pe, "o", b - 1)
                    done(pe, "v_now", b)
                done(pe, f"quarter_kept{j}", b)
                for r in range(QH):
                    last = nc.tensor.matmul(ps_o[r * VW:(r + 1) * VW, j * P:(j + 1) * P], v_now[:, QH * j + r, :],
                                            prob_t[:, QH * j + r, :], start=True, stop=True, tile_position=(0, r * VW))
                last.then_inc(s[f"pv{j}"], 1)

            def turn_back(b):
                done(pe, "o_t_kept", b)
                for j in range(4):
                    last = nc.tensor.transpose(ps_o[:, j * P:(j + 1) * P], o_t[:, j * P:(j + 1) * P], k.ident[:, :])
                last.then_inc(s["o_back"], 1)

            def turn_x3(b):
                done(pe, "rnd3", b)
                bank_free(("x3_kept", b - 1), ("o_kept", b - 4))
                turn(rnd[3], KC).then_inc(s["x3_turned"], 1)

            def q_proj(b):
                done(pe, "x3_kept", b)
                bank_free(("q_kept", b - 1), ("out_read", b - 3))
                for c in range(KC):
                    last = nc.tensor.matmul(ps_m, x3_t[:, c, cols(b, 0, P)], k.wqp_t[:, 0, c, :], start=c == 0, stop=c == KC - 1)
                last.then_inc(s["q_proj"], 1)

            def turn_q(b):
                done(pe, "q_scaled", b)
                for c in range(KC):
                    last = nc.tensor.transpose(ps_m[:, c * P:(c + 1) * P], q0[:, c * P:(c + 1) * P], k.ident[:, :])
                last.then_inc(s["q_turned"], 1)

            def turn_o(b):
                done(pe, "o_rnd", b)
                bank_free(("o_kept", b - 1), ("x3_kept", b + 3), ("x4_kept", b - 1), ("h_kept1", b - 3))
                turn(o_rnd, KC).then_inc(s["o_turned"], 1)

            def out_proj(b):
                done(pe, "o_kept", b)
                bank_free(("out_read", b - 1), ("q_kept", b + 2), ("x_done", b - 3))
                for c in range(KC):
                    last = nc.tensor.matmul(ps_m, oi_t[:, c, :], k.wqp_t[:, 1, c, :], start=c == 0, stop=c == KC - 1)
                last.then_inc(s["out"], 1)

            def turn_x4(b):
                done(pe, "rnd4", b)
                bank_free(("o_kept", b), ("x3_kept", b + 4), ("h_kept0", b - 2))
                turn(rnd[4], KC).then_inc(s["x4_turned"], 1)

            def gate_val(b, half):
                done(pe, "x4_kept", b)
                for name, ps, j in (("gate", ps_g, 0), ("val", ps_v, 1)):
                    done(pe, f"{name}{1 - half}", b if half else b - 1)
                    for c in range(KC):
                        at = c * HIDDEN + half * FH
                        last = nc.tensor.matmul(ps[:, :], x4_t[:, c, cols(b, 0, P)], k.w_ffn[:, j, at:at + FH],
                                                start=c == 0, stop=c == KC - 1)
                    last.then_inc(s[f"mm_{name}{half}"], 1)

            def turn_h(b, j):
                done(pe, "h_rnd", b)
                if j == 0:
                    bank_free(("h_kept1", b - 1), ("o_kept", b + 2), ("x3_kept", b + 6))
                else:
                    bank_free(("h_kept0", b), ("x4_kept", b + 2))
                turn(h_rnd[:, j * FH:(j + 1) * FH], FH // P).then_inc(s[f"h_turned{j}"], 1)

            def ffn_out(b):
                for j in range(2):
                    done(pe, f"h_kept{j}", b)
                bank_free(("x_done", b - 1), ("out_read", b + 2), ("q_kept", b + 5))
                for c in range(HIDDEN // P):
                    last = nc.tensor.matmul(ps_m, hi_t[:, c * P:(c + 1) * P], k.w_ffn[:, 2, c * D:(c + 1) * D],
                                            start=c == 0, stop=c == HIDDEN // P - 1)
                last.then_inc(s["ffn_out"], 1)

            def step(b):
                stage(b, scores, 0)
                stage(b - 1, turn_probs, 2)
                stage(b - 2, out_proj)
                stage(b - 3, gate_val, 0)
                stage(b - 1, attend, 1)

                stage(b, scores, 1)
                stage(b - 1, turn_probs, 3)
                stage(b + 1, q_proj)
                stage(b + 2, turn_x3)
                stage(b - 1, attend, 2)

                stage(b, scores, 2)
                stage(b, turn_probs, 0)
                stage(b - 1, attend, 3)
                stage(b - 4, turn_h, 0)
                stage(b - 3, gate_val, 1)

                stage(b, scores, 3)
                stage(b - 1, turn_back)
                stage(b - 2, turn_x4)
                stage(b + 1, turn_q)
                stage(b, turn_probs, 1)
                stage(b - 4, turn_h, 1)
                stage(b, attend, 0)
                stage(b - 1, turn_o)
                stage(b - 4, ffn_out)

            pe.sem_inc(s["h_turned1"], 1)
            pe.sem_inc(s["ffn_out"], 1)
            program(pe, step)

        @block.vector
        def _(dve):
            def maxima(b, j):
                done(dve, f"scores{j}", b)
                done(dve, f"exps{j}", b - 1)
                nc.vector.tensor_reduce(nmax[:, QH * j:QH * (j + 1)], ps_s[j % 2][:, :].rearrange("p (h e) -> p h e", h=QH),
                                        AX_X, ALU.max, negate=True).then_inc(s[f"nmax{j}"], 1)

            def rounded(b, n, src, scale, low, high, sems, turned):
                done(dve, sems[0], b)
                nc.vector.reciprocal(inv[n][:, :], scale).then_inc(s[sems[1]], 1)
                done(dve, sems[1], b)
                raw, to = (h_rnd0, h_rnd) if n == "h" else (raw_rnd[n], o_rnd if n == "o" else rnd[n])
                nc.vector.tensor_scalar(raw[:, :], src, inv[n][:, 0:1], RND, ALU.mult, ALU.add).then_inc(s[sems[2]], 1)
                done(dve, sems[2], b)
                done(dve, turned, b - 1)
                nc.vector.tensor_scalar(to[:, :], raw[:, :], RND + high, RND + low, ALU.min, ALU.max).then_inc(s[sems[3]], 1)

            def largest(b, n, src, sem):
                nc.vector.tensor_reduce(amax[n][:, :], src, AX_X, ALU.max, apply_absolute_value=True).then_inc(s[sem], 1)
                done(dve, sem, b)

            def round_x3(b):
                nc.vector.tensor_scalar(norm[3][:, :], x_of(b), mv3[:, bass.ds(b, 1), 0], rstd3[:, bass.ds(b, 1)],
                                        ALU.subtract, ALU.mult).then_inc(s["xn3"], 1)
                done(dve, "xn3", b)
                largest(b, 3, norm[3][:, :], "amax3")
                scale = scale_now[:, :]
                nc.vector.tensor_scalar(scale, amax[3][:, :], 1.0 / 127.0, 1e-8, ALU.mult, ALU.max).then_inc(s["scale3"], 1)
                nc.vector.tensor_scalar(scale3[:, bass.ds(b, 1)], amax[3][:, :], 1.0 / 127.0, 1e-8, ALU.mult, ALU.max
                                        ).then_inc(s["scale3_kept"], 1)
                rounded(b, 3, norm[3][:, :], scale, -127.0, 127.0, ("scale3", "inv3", "raw3", "rnd3"), "x3_turned")

            def normed_o(b):
                done(dve, "o_back", b)
                heads = ps_o[:, :].rearrange("p (h d) -> p h d", h=NH1)
                nc.vector.reciprocal(sinv[:, :], heads[:, :, HD1]).then_inc(s["sinv"], 1)
                done(dve, "sinv", b)
                nc.vector.tensor_tensor(o[:, :].rearrange("p (h d) -> p h d", h=NH1), heads[:, :, 0:HD1],
                                        sinv[:, :].rearrange("p (h o) -> p h o", o=1).broadcast_to([P, NH1, HD1]),
                                        ALU.mult).then_inc(s["o"], 1)

            def round_o(b):
                done(dve, "o", b)
                largest(b, "o", o[:, :], "o_amax")
                nc.vector.tensor_scalar(o_scale[:, :], amax["o"][:, :], 1.0 / 127.0, 1e-8, ALU.mult, ALU.max).then_inc(s["o_scale"], 1)
                rounded(b, "o", o[:, :], o_scale[:, :], -127.0, 127.0, ("o_scale", "o_inv", "o_raw", "o_rnd"), "o_turned")

            def add_out(b):
                done(dve, "out", b)
                nc.vector.scalar_tensor_tensor(y[:, :], ps_m, o_scale[:, :], k.scale_qp[:, D:2 * D],
                                               ALU.mult, ALU.mult).then_inc(s["out_read"], 1)
                done(dve, "out_read", b)
                done(dve, "bias3", b)
                nc.vector.tensor_tensor(xs[:, :], x_of(b), y[:, :], ALU.add).then_inc(s["added"], 1)
                done(dve, "added", b)
                nc.vector.tensor_tensor(x_of(b), x_of(b), y[:, :], ALU.add).then_inc(s["x_kept"], 1)
                nc.vector.bn_stats(stats4[:, :], xs[:, :]).then_inc(s["stats4"], 1)
                done(dve, "stats4", b)
                nc.vector.tensor_copy(stats4_seen[:, :], stats4[:, :])
                nc.vector.bn_aggr(mv4[:, :], stats4[:, :]).then_inc(s["mv4"], 1)

            def round_x4(b):
                done(dve, "rstd4", b)
                nc.vector.tensor_scalar(norm[4][:, :], xs[:, :], mv4[:, 0:1], rstd4[:, 0:1],
                                        ALU.subtract, ALU.mult).then_inc(s["xn4"], 1)
                done(dve, "xn4", b)
                largest(b, 4, norm[4][:, :], "amax4")
                nc.vector.tensor_scalar(scale4[:, :], amax[4][:, :], 1e-5, 1.0 / 127.0, ALU.max, ALU.mult).then_inc(s["scale4"], 1)
                rounded(b, 4, norm[4][:, :], scale4[:, :], -128.0, 127.0, ("scale4", "inv4", "raw4", "rnd4"), "x4_turned")
                for j in range(2):
                    last = nc.vector.tensor_tensor(unit[:, j, bass.ds(b, 1)], scale4[:, :], gamma[:, j:j + 1], ALU.mult)
                last.then_inc(s["units"], 1)

            def biased(b, name, half):
                done(dve, f"mm_{name}{half}", b)
                done(dve, "units", b)
                done(dve, f"product{half}", b - 1)
                if name == "gate":
                    done(dve, f"tanh{half}", b - 1)
                j, to, ps, bias = (0, gate, ps_g, k.bias1[:, BG]) if name == "gate" else (1, val, ps_v, half_bv)
                nc.vector.scalar_tensor_tensor(to[:, half * FH:(half + 1) * FH], ps[:, :], unit[:, j, bass.ds(b, 1)],
                                               bias[:, half * FH:(half + 1) * FH],
                                               ALU.mult, ALU.add).then_inc(s[f"{name}{half}"], 1)

            def hidden(b, half):
                done(dve, f"tanh{half}", b)
                done(dve, f"product{half}", b)
                at = slice(half * FH, (half + 1) * FH)
                nc.vector.scalar_tensor_tensor(h[:, at], tanh[:, at], 1.0, product[:, at], ALU.add, ALU.mult
                                               ).then_inc(s[f"h{half}"], 1)

            def round_h(b):
                done(dve, "h0", b)
                done(dve, "h1", b)
                largest(b, "h", h[:, :], "h_amax")
                nc.vector.tensor_scalar(h_scale[:, :], amax["h"][:, :], 1e-5, 1.0 / 127.0, ALU.max, ALU.mult).then_inc(s["h_scale"], 1)
                rounded(b, "h", h[:, :], h_scale[:, :], -128.0, 127.0, ("h_scale", "h_inv", "h_rnd0", "h_rnd"), "h_turned1")
                nc.vector.tensor_tensor(h_unit[:, :], h_scale[:, :], k.gamma[:, 2:3], ALU.mult).then_inc(s["h_unit"], 1)

            def finish(b):
                done(dve, "ffn_out", b)
                done(dve, "bias4", b)
                done(dve, "h_unit", b)
                nc.vector.scalar_tensor_tensor(x_of(b), ps_m, h_unit[:, 0:1], x_of(b), ALU.mult, ALU.add).then_inc(s["x_done"], 1)

            def step(b):
                stage(b, maxima, 0)
                stage(b - 2, add_out)
                stage(b - 3, biased, "gate", 0)
                stage(b - 3, biased, "val", 0)

                stage(b, maxima, 1)
                stage(b - 4, hidden, 1)
                stage(b + 2, round_x3)
                stage(b - 4, round_h)

                stage(b, maxima, 2)
                stage(b - 2, round_x4)
                stage(b - 3, hidden, 0)
                stage(b - 3, biased, "gate", 1)

                stage(b, maxima, 3)
                stage(b - 1, normed_o)
                stage(b - 1, round_o)
                stage(b - 3, biased, "val", 1)
                stage(b - 4, finish)

            nc.vector.tensor_scalar(half_bv[:, :], k.bias1[:, BV], 0.5, None, ALU.mult)
            nc.vector.tensor_copy(gamma[:, 0:1], k.gamma[:, 0:1])
            nc.vector.tensor_scalar(gamma[:, 1:2], k.gamma[:, 1:2], 0.5, None, ALU.mult).then_inc(s["halved"], 1)
            dve.wait_ge(s["halved"], 1)
            for t in range(B):
                nc.vector.bn_stats(stats[:, t, :], k.x_res[:, t, :]).then_inc(s["all_stats"], 1)
            for t in range(B):
                dve.wait_ge(s["all_stats"], t + 1)
                nc.vector.bn_aggr(mv3[:, t, :], stats[:, t, :]).then_inc(s["all_mv"], 1)
            dve.wait_ge(s["all_rstd"], 1)
            dve.sem_inc(s["x_done"], 1)
            program(dve, step)

        @block.scalar
        def _(act):
            def exps(b, j):
                done(act, f"nmax{j}", b)
                done(act, f"quarter{j}", b - 1)
                for r in range(QH):
                    i = QH * j + r
                    last = nc.scalar.activation(prob[:, i, :], ps_s[j % 2][:, r * P:(r + 1) * P], ACT.Exp, bias=nmax[:, i:i + 1])
                last.then_inc(s[f"exps{j}"], 1)

            def keep_quarter(b, j):
                done(act, f"quarter{j}", b)
                done(act, f"pv{j}", b - 1)
                nc.scalar.activation(prob_t[:, QH * j:QH * (j + 1), :], ps_t[:, :].rearrange("p (r e) -> p r e", r=QH),
                                     ACT.Copy).then_inc(s[f"quarter_kept{j}"], 1)

            def scale_q(b):
                done(act, "q_proj", b)
                done(act, "q_turned", b - 1)
                done(act, "scale3_kept", b)
                nc.scalar.activation(q0[:, :], ps_m, ACT.Copy, scale=scale3[:, bass.ds(b, 1)]).then_inc(s["q_scaled"], 1)

            def keep_q(b):
                done(act, "q_turned", b)
                done(act, "scores3", b - 1)
                for c in range(KC):
                    last = nc.scalar.activation(q_t[:, c, :], ps_m[:, c * P:(c + 1) * P], ACT.Identity,
                                                bias=k.bq[:, c:c + 1], scale=k.wq_scale[:, c:c + 1])
                last.then_inc(s["q_kept"], 1)

            def keep_o_t(b):
                done(act, "pv3", b)
                done(act, "o_back", b - 1)
                nc.scalar.activation(o_t[:, :], ps_o[:, :], ACT.Copy).then_inc(s["o_t_kept"], 1)

            def keep_x(b, name, to):
                done(act, f"{name}_turned", b)
                nc.scalar.activation(to[:, :, cols(b, 0, P)], ps_turn[:, 0:D].rearrange("p (c n) -> p c n", c=KC), ACT.Copy,
                                     bias=-RND).then_inc(s[f"{name}_kept"], 1)

            def keep_o(b):
                done(act, "o_turned", b)
                done(act, "out", b - 1)
                nc.scalar.activation(oi_t[:, :, :], ps_turn[:, 0:D].rearrange("p (c n) -> p c n", c=KC), ACT.Copy,
                                     bias=-RND).then_inc(s["o_kept"], 1)

            def keep_h(b, j):
                done(act, f"h_turned{j}", b)
                done(act, "ffn_out", b - 1)
                nc.scalar.activation(hi_t[:, j * FH:(j + 1) * FH], ps_turn[:, :], ACT.Copy,
                                     bias=-RND).then_inc(s[f"h_kept{j}"], 1)

            def tanhs(b, half):
                done(act, f"gate{half}", b)
                done(act, f"h{half}", b - 1)
                at = slice(half * FH, (half + 1) * FH)
                nc.scalar.activation(tanh[:, at], gate[:, at], ACT.Tanh, scale=0.5).then_inc(s[f"tanh{half}"], 1)

            def step(b):
                stage(b - 1, keep_quarter, 2)
                stage(b, exps, 0)
                stage(b - 3, tanhs, 0)

                stage(b - 1, keep_quarter, 3)
                stage(b + 1, scale_q)
                stage(b + 2, keep_x, "x3", x3_t)
                stage(b, exps, 1)

                stage(b, keep_quarter, 0)
                stage(b - 1, keep_o_t)
                stage(b - 4, keep_h, 0)
                stage(b, exps, 2)

                stage(b - 2, keep_x, "x4", x4_t)
                stage(b + 1, keep_q)
                stage(b, keep_quarter, 1)
                stage(b - 4, keep_h, 1)
                stage(b - 3, tanhs, 1)
                stage(b, exps, 3)
                stage(b - 1, keep_o)

            act.sem_inc(s["h_kept1"], 1)
            program(act, step)

        @block.gpsimd
        def _(pool):
            def spread_keys(b, c):
                done(pool, f"scores{2 * c + 1}", b - 1)
                keys = k.k1_t[:, c, cols(b, 0, P)].rearrange("p (o e) -> p o e", o=1).broadcast_to([P, HC, P])
                mask = k.head_mask[:, :].rearrange("p (h o) -> p h o", o=1).broadcast_to([P, HC, P])
                nc.gpsimd.tensor_tensor(kd[:, c, :, :], keys, mask, ALU.mult).then_inc(s[f"keys{c}"], 1)

            def spread_values(b):
                done(pool, "pv3", b - 1)
                heads = lambda a: a.rearrange("p (h d) -> p h d", h=NH1)
                v_b = k.v1[:, bass.ds(b, 1), :].rearrange("p o (h d) -> p (o h) d", h=NH1)
                nc.gpsimd.tensor_tensor(v_now[:, :, 0:HD1], v_b, heads(k.bv[:, :]), ALU.add).then_inc(s["v_now"], 1)

            def add_bias(b, after, bias, sem):
                done(pool, after, b)
                nc.gpsimd.tensor_tensor(x_of(b), x_of(b), k.bias1[:, bias], ALU.add).then_inc(s[sem], 1)

            def invert_std(b):
                done(pool, "mv4", b)
                nc.gpsimd.tensor_tensor(vpe4[:, :], mv4[:, 1:2], eps[:, 0:1], ALU.add).then_inc(s["vpe4"], 1)
                done(pool, "vpe4", b)
                nc.gpsimd.tensor_tensor(rstd4[:, :], vpe4[:, :], k.neg_half[:, 0:1], ALU.pow).then_inc(s["rstd4"], 1)

            def times(b, half):
                done(pool, f"gate{half}", b)
                done(pool, f"val{half}", b)
                done(pool, f"h{half}", b - 1)
                at = slice(half * FH, (half + 1) * FH)
                nc.gpsimd.tensor_tensor(product[:, at], gate[:, at], val[:, at], ALU.mult).then_inc(s[f"product{half}"], 1)

            def step(b):
                stage(b, spread_keys, 1)
                stage(b - 2, invert_std)
                stage(b - 3, times, 0)
                stage(b + 1, add_bias, "xn3", BP, "bias3")
                stage(b + 1, spread_keys, 0)
                stage(b, spread_values)
                stage(b - 2, add_bias, "x_kept", BO, "bias4")
                stage(b - 3, times, 1)

            nc.gpsimd.memset(eps[:, :], 1e-5).then_inc(s["eps_set"], 1)
            nc.gpsimd.memset(v_now[:, :, HD1 + 1:], 0.0)
            nc.gpsimd.memset(v_now[:, :, HD1:HD1 + 1], 1.0)
            pool.wait_ge(s["all_mv"], B)
            pool.wait_ge(s["eps_set"], 1)
            nc.gpsimd.tensor_tensor(vpe[:, :], mv3[:, :, 1], eps[:, :], ALU.add).then_inc(s["all_vpe"], 1)
            pool.wait_ge(s["all_vpe"], 1)
            nc.gpsimd.tensor_tensor(rstd3[:, :], vpe[:, :], k.neg_half[:, 0:B], ALU.pow).then_inc(s["all_rstd"], 1)
            program(pool, step)

        @block.sync
        def _(sp):
            with sp.Fori(0, B) as b:
                done(sp, "x_done", b)
                sp.dma_start(out[bass.ds(b, 1)].rearrange("o p d -> p (o d)"), x_of(b)).then_inc(s["stored"], 16)
            sp.wait_ge(s["stored"], 16 * B)


class Kept:
    pass


def build(nc, io, out):
    with ExitStack() as ctx:
        Mem.held.clear()
        m = Mem(nc, ctx)
        k = Kept()
        k.psum = ctx.enter_context(nc.psum_tensor("psum", [P, 8 * BANK], F32))
        k.x_res = m.sb("x_res", [P, B, D])
        k.xn_t = m.sb("xn_t", [P, KC, T])
        k.ctx_t = m.sb("ctx_t", [P, KC, T])
        k.ident = m.sb("ident", [P, P])
        k.neg_half = m.sb("neg_half", [P, 16])
        k.head_mask = m.sb("head_mask", [P, HC])
        with ExitStack() as layer0:
            a = Mem(nc, layer0)
            k.wa_hi = a.sb("wa_hi", [P, NKV0, WA], F32R)
            k.wa_lo = a.sb("wa_lo", [P, NKV0, WA], F32R)
            k.wa_raw = a.sb("wa_raw", [P, WA_SLOTS, WA])
            k.mask = a.sb("mask", [P, S])
            k.bias_a = a.sb("bias_a", [P, NKV0 * 6 * P])
            k.eps_a = a.sb("eps_a", [P, 5])
            k.norm_w = a.sb("norm_w", [P, 2])
            k.key_scale = a.sb("key_scale", [P, 1])
            constants_and_first_norm(nc, io, k)
            layer0_attention(nc, io, k)
        k.comb_dram = nc.dram_tensor("expert_weights", (NE, T), F32, kind="Internal").ap()
        k.k1_t = m.sb("k1_t", [P, KC, T])
        k.v1 = m.sb("v1", [P, B, D])
        k.bv = m.sb("bv", [P, D])
        k.wqp_t = m.sb("wqp_t", [P, 2, KC, D], BF16)
        k.scale_qp = m.sb("scale_qp", [P, 2 * D])
        k.bias1 = m.sb("bias1", [P, 3 * D + 2 * HIDDEN])
        k.w_ffn = m.sb("w_ffn", [P, 3, KC * HIDDEN], BF16)
        k.gamma = m.sb("gamma", [P, 3])
        k.bq = m.sb("bq", [P, KC])
        k.wq_scale = m.sb("wq_scale", [P, KC])
        with ExitStack() as ffn0:
            a = Mem(nc, ffn0)
            k.wf = a.sb("wf", [P, 3, KC * HIDDEN])
            k.ginv = a.sb("ginv", [P, 3])
            k.raw = a.sb("wm_raw", [P, 3, WM])
            k.w_hi = a.sb("wm_hi", [P, 3, WM], F32R)
            k.w_lo = a.sb("wm_lo", [P, 3, WM], F32R)
            k.xn_hi = a.sb("xn_hi", [P, KC, T], F32R)
            k.xn_lo = a.sb("xn_lo", [P, KC, T], F32R)
            router_and_layer1_keys(nc, io, k)
            experts(nc, io, k)
        m.end_of_layer()
        layer1(nc, io, k, out)


def lay_out(i):
    import numpy as np

    a = {n: np.asarray(v) for n, v in i.items()}

    def chunked(w):
        return w.reshape(-1, P, w.shape[1]).transpose(1, 0, 2)

    groups, biases = [], []
    for g in range(NKV0):
        q, kv = slice(g * GH * HD0, (g + 1) * GH * HD0), slice(g * HD0, (g + 1) * HD0)
        w_kv = np.concatenate([a["L0_xattn_Wk"][:, kv], a["L0_xattn_Wv"][:, kv]], axis=1)
        parts = (chunked(a["L0_xattn_Wq"][:, q]), chunked(w_kv), chunked(a["L0_xattn_Wo"][q]))
        groups.append(np.concatenate([p.reshape(P, -1) for p in parts], axis=1))
        biases += [a["L0_xattn_bq"][q], a["L0_xattn_bk"][kv], a["L0_xattn_bv"][kv]]
    gu, down = a["L0_ffn_gate_up_proj"], a["L0_ffn_down_proj"]
    inner = [w.reshape(MT, P, KC, P).transpose(0, 3, 2, 1).reshape(MT, P, KC * P) for w in (gu[:, :INTER], gu[:, INTER:])]
    inner.append(down.transpose(0, 2, 1).reshape(MT, P, D))
    return {
        "wkv_t": chunked(a["L1_xattn_wkv"].T),
        "wqp": np.concatenate([w.reshape(KC, P, D) for w in (a["L1_xattn_wq"], a["L1_xattn_wp"])]).transpose(1, 0, 2),
        "bk1": a["L1_xattn_bkv"][:D].reshape(KC, P).T,
        "bq1": a["L1_xattn_bq"].reshape(KC, P).T,
        "bv1": a["L1_xattn_bkv"][D:],
        "bias1": np.concatenate([a[n] for n in ("L1_xattn_bq", "L1_xattn_bp", "L1_ffn_gate_b", "L1_ffn_val_b", "L1_ffn_out_b")]),
        "gate_w": chunked(a["L1_ffn_gate_w"].T).reshape(P, -1),
        "val_w": chunked(a["L1_ffn_val_w"].T).reshape(P, -1),
        "out_w": chunked(a["L1_ffn_out_w"].T).reshape(P, -1),
        "gate_t": chunked(a["L0_ffn_gate_weight"].T),
        "wm": np.concatenate(inner, axis=2),
        "x": a["x"],
        "ctx_t": chunked(a["ctx_2048"].reshape(T, D).T),
        "mask": a["mask_1xSxS2_ff0"],
        "wa": np.stack(groups),
        "bias_a": np.concatenate(biases),
        "norm_w": np.stack([a["L0_xattn_qn_w"], a["L0_xattn_kn_w"]], axis=1),
    }


def kernel(**inputs):
    import numpy as np
    import concourse.bacc as bacc
    from concourse.bass_utils import run_bass_kernel_spmd

    nc = bacc.Bacc("TRN2", target_bir_lowering=False, num_devices=1)
    arrays = {f"in_{n}": np.ascontiguousarray(v) for n, v in lay_out(inputs).items()}
    io = {n[3:]: nc.dram_tensor(n, v.shape, mybir.dt.from_np(v.dtype), kind="ExternalInput").ap() for n, v in arrays.items()}
    out = nc.dram_tensor("out", (B, S, D), F32, kind="ExternalOutput").ap()
    build(nc, io, out)
    r = run_bass_kernel_spmd(nc, [arrays], core_ids=[0])
    return r.results[0]["out"]
```

```python
from contextlib import ExitStack

import concourse.bass as bass
from concourse import mybir

P = 128
BANK = 512
F32 = mybir.dt.float32
F32R = mybir.dt.float32r
BF16 = mybir.dt.bfloat16
ALU = mybir.AluOpType
ACT = mybir.ActivationFunctionType
AX_X = mybir.AxisListType.X

B, S, D = 8, 128, 256
T = B * S
KC = D // P
NH0, NKV0, HD0 = 16, 4, 128
GH = NH0 // NKV0
NE, TOPK, INTER = 32, 8, 96
MT = NE * INTER // P
THRESHOLD = 0.8
NH1 = 16
HD1 = D // NH1
HC = P // HD1
HIDDEN = 4 * D
FIRST = 2
RND = 12582912.0
WA = KC * GH * HD0 + KC * 2 * HD0 + GH * D
WQ_AT, WKV_AT, WO_AT = 0, KC * GH * HD0, KC * GH * HD0 + KC * 2 * HD0
PROJ, OUT = slice(0, WO_AT), slice(WO_AT, WA)
OUT_STEP = 3
WM = 2 * KC * P + D
BQ, BP, BG, BV, BO = (slice(a, a + n) for a, n in (
    (0, D), (D, D), (2 * D, HIDDEN), (2 * D + HIDDEN, HIDDEN), (2 * D + 2 * HIDDEN, D)))


class Mem:

    held = []

    def __init__(self, nc, ctx):
        self.nc, self.ctx = nc, ctx

    def sb(self, name, shape, dt=F32):
        return self.ctx.enter_context(self.nc.sbuf_tensor(name, shape, dt))

    def sem(self, name):
        self.held.append(self.nc.alloc_semaphore(name=name))
        return self.held[-1]

    def end_of_layer(self):
        self.nc.clear_and_free_semaphores(self.held)
        self.held.clear()
        self.nc.all_engine_barrier()


def banks(k, first=0, n=8, width=1):
    return [k.psum[:, (first + i * width) * BANK:(first + (i + 1) * width) * BANK] for i in range(n)]


def cols(t, at, n):
    return bass.ds(t * n + at, n)


def constants_and_first_norm(nc, io, k):
    with ExitStack() as ctx:
        m = Mem(nc, ctx)
        bank = banks(k)
        stats = m.sb("a_stats", [P, B, 6])
        mv = m.sb("a_mv", [P, B, 2])
        rstd = m.sb("a_rstd", [P, B])
        vpe = m.sb("a_vpe", [P, B])
        xn = m.sb("a_xn", [P, B, D])
        x_loaded = [m.sem(f"a_x{half}") for half in range(2)]
        k.ctx_loaded = [m.sem(f"a_ctx{j}") for j in range(2)]
        k.mask_loaded, k.norm_w_loaded = (m.sem(f"a_{n}") for n in ("mask", "norm_w"))
        k.bias_loaded = [m.sem(f"a_bias{j}") for j in range(NKV0 - 1)]
        k.wa_loaded = [m.sem(f"a_wa{j}") for j in range(NKV0)]
        zeroed, neg_half_set, ident_done, hm_steps = (m.sem(f"a_{n}") for n in ("zeroed", "half", "ident", "hm"))
        stats_done, mv_done, vpe_done, rstd_done = (m.sem(f"a_{n}") for n in ("stats_d", "mv_d", "vpe_d", "rstd_d"))
        xn_done, xt_done, wa0_hi = (m.sem(f"a_{n}") for n in ("xn_d", "xt_d", "wa0_hi"))
        block = ctx.enter_context(nc.Block())

        @block.sync
        def _(sp):
            for half in range(2):
                at = slice(half * B // 2, (half + 1) * B // 2)
                sp.dma_start(k.x_res[:, at, :], io["x"][at].rearrange("b p d -> p b d")).then_inc(x_loaded[half], 16)
            sp.dma_start(k.ctx_t[:, :, 0:P], io["ctx_t"][:, :, 0:P]).then_inc(k.ctx_loaded[0], 16)
            for g in range(NKV0):
                sp.dma_start(k.wa_raw[:, g, :], io["wa"][g]).then_inc(k.wa_loaded[g], 16)
                if g >= 1:
                    at = slice((g - 1) * 6 * P, (g if g < NKV0 - 1 else NKV0) * 6 * P)
                    sp.dma_start(k.bias_a[:, at], io["bias_a"][at].partition_broadcast(P)).then_inc(k.bias_loaded[g - 1], 16)
            sp.dma_start(k.ctx_t[:, :, P:], io["ctx_t"][:, :, P:]).then_inc(k.ctx_loaded[1], 16)

        @block.gpsimd
        def _(pool):
            nc.gpsimd.memset(k.ident[:, :], 0.0).then_inc(zeroed, 1)
            nc.gpsimd.memset(k.neg_half[:, :], -0.5).then_inc(neg_half_set, 1)
            nc.gpsimd.memset(k.eps_a[:, :], HD0 * 1e-6)
            nc.gpsimd.memset(k.eps[:, :], 1e-5)
            nc.gpsimd.memset(k.minus_one[:, :], -1.0)
            nc.gpsimd.memset(k.head_mask[:, :], float(HD1) ** -0.5).then_inc(hm_steps, 1)
            pool.wait_ge(zeroed, 1)
            nc.gpsimd.affine_select(out=k.ident[:, :], in_=k.ident[:, :], compare_op=ALU.not_equal, fill=1.0,
                                    base=0, pattern=[[-1, P]], channel_multiplier=1).then_inc(ident_done, 1)
            pool.wait_ge(hm_steps, 1)
            nc.gpsimd.affine_select(out=k.head_mask[:, :], in_=k.head_mask[:, :], compare_op=ALU.is_ge, fill=0.0,
                                    base=0, pattern=[[-HD1, HC]], channel_multiplier=1).then_inc(hm_steps, 1)
            pool.wait_ge(hm_steps, 2)
            nc.gpsimd.affine_select(out=k.head_mask[:, :], in_=k.head_mask[:, :], compare_op=ALU.is_ge, fill=0.0,
                                    base=HD1 - 1, pattern=[[HD1, HC]], channel_multiplier=-1).then_inc(hm_steps, 1)
            pool.wait_ge(neg_half_set, 1)
            for half in range(2):
                at = slice(half * B // 2, (half + 1) * B // 2)
                pool.wait_ge(mv_done, (half + 1) * B // 2)
                nc.gpsimd.tensor_scalar(vpe[:, at], mv[:, at, 1], 1e-5, None, ALU.add).then_inc(vpe_done, 1)
                pool.wait_ge(vpe_done, half + 1)
                nc.gpsimd.tensor_tensor(rstd[:, at], vpe[:, at], k.neg_half[:, at], ALU.pow).then_inc(rstd_done, 1)

        @block.vector
        def _(dve):
            for half in range(2):
                tiles = range(half * B // 2, (half + 1) * B // 2)
                dve.wait_ge(x_loaded[half], 16)
                for t in tiles:
                    nc.vector.bn_stats(stats[:, t, :], k.x_res[:, t, :]).then_inc(stats_done, 1)
                for t in tiles:
                    dve.wait_ge(stats_done, t + 1)
                    nc.vector.bn_aggr(mv[:, t, :], stats[:, t, :]).then_inc(mv_done, 1)
            for t in range(B):
                dve.wait_ge(rstd_done, 1 + t // (B // 2))
                nc.vector.tensor_scalar(xn[:, t, :], k.x_res[:, t, :], mv[:, t, 0:1], rstd[:, t:t + 1],
                                        ALU.subtract, ALU.mult).then_inc(xn_done, 1)
            dve.wait_ge(wa0_hi, 1)
            nc.vector.tensor_tensor(k.wa_lo[:, 0, PROJ], k.wa_raw[:, 0, PROJ], k.wa_hi[:, 0, PROJ].bitcast(F32), ALU.subtract)

        @block.tensor
        def _(pe):
            pe.wait_ge(ident_done, 1)
            for t in range(B):
                pe.wait_ge(xn_done, t + 1)
                for c in range(KC):
                    last = nc.tensor.transpose(bank[t][:, c * P:(c + 1) * P], xn[:, t, c * P:(c + 1) * P], k.ident[:, :])
                last.then_inc(xt_done, 1)

        @block.scalar
        def _(act):
            act.dma_start(k.norm_w[:, :], io["norm_w"]).then_inc(k.norm_w_loaded, 16)
            act.dma_start(k.mask[:, :], io["mask"][0]).then_inc(k.mask_loaded, 16)
            act.wait_ge(k.wa_loaded[0], 16)
            nc.scalar.activation(k.wa_hi[:, 0, PROJ], k.wa_raw[:, 0, PROJ], ACT.Copy).then_inc(wa0_hi, 1)
            for t in range(B):
                act.wait_ge(xt_done, t + 1)
                nc.scalar.activation(k.xn_t[:, :, t * P:(t + 1) * P], bank[t][:, 0:D].rearrange("p (c n) -> p c n", c=KC), ACT.Copy)


def layer0_attention(nc, io, k):
    with ExitStack() as ctx:
        m = Mem(nc, ctx)
        ps_s, ps_q, ps_kv, ps_pt, ps_qt, ps_kt, ps_o, ps_y = banks(k)
        xh, xl, ch, cl = (m.sb(f"b_{n}", [P, KC, P], F32R) for n in ("xh", "xl", "ch", "cl"))
        qkv = m.sb("b_qkv", [P, 2, 6 * P])
        sq = m.sb("b_sq", [P, 5 * P])
        ssum = m.sb("b_ssum", [P, 5])
        sume = m.sb("b_sume", [P, 5])
        stats = m.sb("b_stats", [P, B - 1, 6])
        rnorm = m.sb("b_rnorm", [P, NKV0, 5])
        kn = m.sb("b_kn", [P, P])
        qt = m.sb("b_qt", [P, NKV0, GH * P])
        kt = m.sb("b_kt", [P, NKV0, P])
        vh = m.sb("b_vh", [P, NKV0, P], F32R)
        vl = m.sb("b_vl", [P, NKV0, P], F32R)
        sc = m.sb("b_sc", [P, GH * P])
        nmax = m.sb("b_nmax", [P, GH])
        prob = m.sb("b_prob", [P, GH * P])
        rsum = m.sb("b_rsum", [P, GH])
        rinv = m.sb("b_rinv", [P, GH])
        probn = m.sb("b_probn", [P, GH * P])
        pth = m.sb("b_pth", [P, GH * P], F32R)
        ptl = m.sb("b_ptl", [P, GH * P], F32R)
        oh = m.sb("b_oh", [P, 2, GH * P], F32R)
        ol = m.sb("b_ol", [P, 2, GH * P], F32R)
        ahead = ("qkv_ready", "pt_ready", "ol_ready", "scores_read", "y_added", "exp_done", "sq_done", "qt_ready",
                 "kt_ready", "q_turned", "k_turned", "pv_done", "wo_done", "p_turned", "probn_done", "kn_done",
                 "v_ready", "ssum_done", "rnorm_done")
        plain = ("pt_high", "v_high", "slot_hi", "slot_lo", "proj_done", "sume_done", "scores_done", "nmax_done", "rinv_done", "oh_ready")
        s = {n: m.sem(f"b_{n}") for n in ahead + plain}
        proj_hi, proj_lo, out_hi, out_lo = (m.sem(f"b_w_{n}") for n in ("proj_hi", "proj_lo", "out_hi", "out_lo"))
        scaled = m.sem("b_key_scale")
        next_stats, next_mv, next_vpe = (m.sem(f"b_next_{n}") for n in ("stats", "mv", "vpe"))
        block = ctx.enter_context(nc.Block())

        def done(eng, name, n):
            eng.wait_ge(s[name], n + (2 if name in ahead else 1))

        def freed(eng, name, n):
            eng.wait_ge(s[name], n + 1)

        def start_ahead(eng, *names):
            for name in names:
                eng.sem_inc(s[name], 1)

        def stage(b, g, lag, work):
            b, g = (b, g - lag) if g >= lag else (b - 1, g - lag + NKV0)
            if type(b) is not int or 0 <= b < B:
                work(b, g, b * NKV0 + g)

        def program(eng, step, before=None, split=None, split_out=None, lead=1, late=None):
            if before:
                before(0)
            for n in range(2 * NKV0):
                for g in range(n + lead if n else 1, n + lead + 1):
                    if split and g < NKV0:
                        split(g)
                step(n // NKV0 - 1, n % NKV0)
                if split_out and 0 <= n - OUT_STEP < NKV0:
                    split_out(n - OUT_STEP)
            with eng.Fori(1, B - 2) as b:
                for g in range(NKV0):
                    step(b, g)
            for b, steps in ((B - 2, NKV0), (B - 1, NKV0), (B, 2)):
                for g in range(steps):
                    step(b, g)
                    if late and b == B - 1:
                        late(g)

        @block.tensor
        def _(pe):
            def scores(b, g, n):
                done(pe, "qt_ready", n)
                done(pe, "kt_ready", n)
                freed(pe, "scores_read", n)
                for r in range(GH):
                    last = nc.tensor.matmul(ps_s[:, r * P:(r + 1) * P], qt[:, g, r * P:(r + 1) * P], kt[:, g, :],
                                            start=True, stop=True)
                last.then_inc(s["scores_done"], 1)

            def turn_probs(b, g, n):
                done(pe, "probn_done", n)
                freed(pe, "pt_ready", n)
                for r in range(GH):
                    last = nc.tensor.transpose(ps_pt[:, r * P:(r + 1) * P], probn[:, r * P:(r + 1) * P], k.ident[:, :])
                last.then_inc(s["p_turned"], 1)

            def attend(b, g, n):
                done(pe, "pt_ready", n)
                done(pe, "v_ready", n)
                freed(pe, "ol_ready", n)
                nc.tensor.matmul(ps_o[:, :], vh[:, g, :], pth[:, :], start=True, stop=False)
                nc.tensor.matmul(ps_o[:, :], vl[:, g, :], pth[:, :], start=False, stop=False)
                nc.tensor.matmul(ps_o[:, :], vh[:, g, :], ptl[:, :], start=False, stop=True).then_inc(s["pv_done"], 1)

            def out_proj(b, g, n):
                done(pe, "ol_ready", n)
                if type(b) is int and b == 0:
                    pe.wait_ge(out_hi, g + 1)
                    pe.wait_ge(out_lo, g + 1)
                if g == 0:
                    freed(pe, "y_added", b)
                for r in range(GH):
                    w_hi = k.wa_hi[:, g, WO_AT + r * D:WO_AT + (r + 1) * D]
                    w_lo = k.wa_lo[:, g, WO_AT + r * D:WO_AT + (r + 1) * D]
                    o_hi, o_lo = oh[:, g % 2, r * P:(r + 1) * P], ol[:, g % 2, r * P:(r + 1) * P]
                    nc.tensor.matmul(ps_y[:, 0:D], o_hi, w_hi, start=g == 0 and r == 0, stop=False)
                    nc.tensor.matmul(ps_y[:, 0:D], o_hi, w_lo, start=False, stop=False)
                    last = nc.tensor.matmul(ps_y[:, 0:D], o_lo, w_hi, start=False, stop=g == NKV0 - 1 and r == GH - 1)
                last.then_inc(s["wo_done"], 1)

            def project(b, g, n):
                if g == 0:
                    done(pe, "slot_hi", b)
                    done(pe, "slot_lo", b)
                if type(b) is int and b == 0 and g >= 1:
                    pe.wait_ge(proj_hi, g)
                    pe.wait_ge(proj_lo, g)
                freed(pe, "qkv_ready", n)
                for ps, a_hi, a_lo, at, w in ((ps_q, xh, xl, WQ_AT, GH * HD0), (ps_kv, ch, cl, WKV_AT, 2 * HD0)):
                    for c in range(KC):
                        w_hi = k.wa_hi[:, g, at + c * w:at + (c + 1) * w]
                        w_lo = k.wa_lo[:, g, at + c * w:at + (c + 1) * w]
                        nc.tensor.matmul(ps[:, 0:w], a_hi[:, c, :], w_hi, start=c == 0, stop=False)
                        nc.tensor.matmul(ps[:, 0:w], a_hi[:, c, :], w_lo, start=False, stop=False)
                        last = nc.tensor.matmul(ps[:, 0:w], a_lo[:, c, :], w_hi, start=False, stop=c == KC - 1)
                last.then_inc(s["proj_done"], 1)

            def turn_q(b, g, n):
                done(pe, "qkv_ready", n)
                freed(pe, "qt_ready", n)
                for r in range(GH):
                    last = nc.tensor.transpose(ps_qt[:, r * P:(r + 1) * P], qkv[:, g % 2, r * P:(r + 1) * P], k.ident[:, :])
                last.then_inc(s["q_turned"], 1)

            def turn_k(b, g, n):
                done(pe, "kn_done", n)
                freed(pe, "kt_ready", n)
                nc.tensor.transpose(ps_kt[:, 0:P], kn[:, :], k.ident[:, :]).then_inc(s["k_turned"], 1)

            def step(b, g):
                if type(b) is not int or b < B - 1 or g == 0:
                    stage(b, g, 0, scores)
                stage(b, g, 1, turn_probs)
                stage(b + 1, g, 1, turn_q)
                stage(b + 1, g, 0, project)
                stage(b + 1, g, 2, turn_k)
                if type(b) is int and b == B - 1 and g < NKV0 - 1:
                    scores(b, g + 1, b * NKV0 + g + 1)
                stage(b, g, 1, attend)
                stage(b, g, 2, out_proj)

            start_ahead(pe, "q_turned", "k_turned", "pv_done", "wo_done", "p_turned")
            program(pe, step)

        @block.vector
        def _(dve):
            def low_parts(b):
                if type(b) is not int or b < B:
                    done(dve, "slot_hi", b)
                    nc.vector.tensor_tensor(xl[:, :, :], k.xn_t[:, :, cols(b, 0, P)], xh[:, :, :].bitcast(F32), ALU.subtract)
                    nc.vector.tensor_tensor(cl[:, :, :], k.ctx_t[:, :, cols(b, 0, P)], ch[:, :, :].bitcast(F32),
                                            ALU.subtract).then_inc(s["slot_lo"], 1)

            def masked_scores(b, g, n):
                done(dve, "scores_done", n)
                done(dve, "rnorm_done", n)
                freed(dve, "exp_done", n)
                for r in range(GH):
                    last = nc.vector.scalar_tensor_tensor(sc[:, r * P:(r + 1) * P], ps_s[:, r * P:(r + 1) * P],
                                                          rnorm[:, g, r:r + 1], k.mask[:, :], ALU.mult, ALU.add)
                last.then_inc(s["scores_read"], 1)
                done(dve, "scores_read", n)
                nc.vector.tensor_reduce(nmax[:, :], sc[:, :].rearrange("p (r e) -> p r e", r=GH), AX_X, ALU.max,
                                        negate=True).then_inc(s["nmax_done"], 1)

            def invert_sums(b, g, n):
                done(dve, "exp_done", n)
                freed(dve, "probn_done", n)
                nc.vector.reciprocal(rinv[:, :], rsum[:, :]).then_inc(s["rinv_done"], 1)

            def low_part_of_probs(b, g, n):
                done(dve, "pt_high", n)
                freed(dve, "pv_done", n)
                nc.vector.tensor_tensor(ptl[:, :], ps_pt[:, :], pth[:, :].bitcast(F32), ALU.subtract).then_inc(s["pt_ready"], 1)

            def low_part_of_v(b, g, n):
                done(dve, "v_high", n)
                if type(b) is not int or b > 0:
                    done(dve, "pv_done", n - NKV0)
                nc.vector.tensor_tensor(vl[:, g, :], qkv[:, g % 2, 5 * P:6 * P], vh[:, g, :].bitcast(F32),
                                        ALU.subtract).then_inc(s["v_ready"], 1)

            def low_part_of_out(b, g, n):
                done(dve, "oh_ready", n)
                if type(n) is not int or n >= 1:
                    freed(dve, "wo_done", n - 1)
                nc.vector.tensor_tensor(ol[:, g % 2, :], ps_o[:, :], oh[:, g % 2, :].bitcast(F32), ALU.subtract).then_inc(s["ol_ready"], 1)

            def add_out(b, g, n):
                if g == NKV0 - 1:
                    done(dve, "wo_done", n)
                    x_b = k.x_res[:, bass.ds(b, 1), :].rearrange("p o d -> p (o d)")
                    nc.vector.tensor_tensor(x_b, x_b, ps_y[:, 0:D], ALU.add).then_inc(s["y_added"], 1)

            def add_bias(b, g, n):
                done(dve, "proj_done", n)
                if type(b) is int and n < NKV0 - 1:
                    dve.wait_ge(k.bias_loaded[n], 16)
                if type(b) is not int or n >= 2:
                    freed(dve, "q_turned", n - 1)
                    freed(dve, "kn_done", n - 1)
                    freed(dve, "v_ready", n - 1)
                bias = k.bias_a[:, g * 6 * P:(g + 1) * 6 * P]
                nc.vector.tensor_tensor(qkv[:, g % 2, 0:4 * P], ps_q[:, :], bias[:, 0:4 * P], ALU.add)
                nc.vector.tensor_tensor(qkv[:, g % 2, 4 * P:6 * P], ps_kv[:, 0:2 * P], bias[:, 4 * P:6 * P],
                                        ALU.add).then_inc(s["qkv_ready"], 1)

            def sum_squares(b, g, n):
                done(dve, "sq_done", n)
                freed(dve, "rnorm_done", n)
                nc.vector.tensor_reduce(ssum[:, :], sq[:, :].rearrange("p (r e) -> p r e", r=5), AX_X,
                                        ALU.add).then_inc(s["ssum_done"], 1)

            def step(b, g):
                at_end = type(b) is int and b == B - 1
                if not at_end or g == 0:
                    stage(b, g, 0, masked_scores)
                stage(b, g, 1, low_part_of_probs)
                if type(b) is int and b == -1:
                    stage(b + 1, g, 0, add_bias)
                    stage(b + 1, g, 1, sum_squares)
                else:
                    stage(b + 1, g, 1, sum_squares)
                    stage(b, g, 0, invert_sums)
                    if at_end and g < NKV0 - 1:
                        masked_scores(b, g + 1, b * NKV0 + g + 1)
                    stage(b + 1, g, 0, add_bias)
                if g == NKV0 - 1:
                    low_parts(b + 2)
                stage(b, g, 1, low_part_of_out)
                stage(b + 1, g, 1, low_part_of_v)
                stage(b, g, 2, add_out)

            def split(g):
                dve.wait_ge(proj_hi, g)
                nc.vector.tensor_tensor(k.wa_lo[:, g, PROJ], k.wa_raw[:, g, PROJ],
                                        k.wa_hi[:, g, PROJ].bitcast(F32), ALU.subtract).then_inc(proj_lo, 1)

            start_ahead(dve, "v_ready", "qkv_ready", "pt_ready", "ol_ready", "scores_read", "y_added", "ssum_done")
            dve.wait_ge(k.norm_w_loaded, 16)
            nc.vector.scalar_tensor_tensor(k.key_scale[:, :], k.norm_w[:, 0:1], float(HD0) ** 0.5, k.norm_w[:, 1:2],
                                           ALU.mult, ALU.mult).then_inc(scaled, 1)
            dve.wait_ge(k.mask_loaded, 16)
            def next_norm(g):
                first, last = {0: (0, B // 2), 1: (B // 2, B - 2), 2: (B - 2, B - 1)}.get(g, (0, 0))
                for t in range(first, last):
                    done(dve, "y_added", t)
                    nc.vector.bn_stats(stats[:, t, :], k.x_res[:, t, :]).then_inc(next_stats, 1)
                for t in range(first, last):
                    dve.wait_ge(next_stats, t + 1)
                    nc.vector.bn_aggr(k.mv[:, t, :], stats[:, t, :]).then_inc(next_mv, 1)

            program(dve, step, low_parts, split, late=next_norm)

        @block.scalar
        def _(act):
            def high_parts(b):
                if type(b) is not int or 0 < b < B:
                    act.wait_ge(s["proj_done"], b * NKV0)
                if type(b) is int and b == 1:
                    act.wait_ge(k.ctx_loaded[1], 16)
                if type(b) is not int or b < B:
                    nc.scalar.activation(xh[:, :, :], k.xn_t[:, :, cols(b, 0, P)], ACT.Copy)
                    nc.scalar.activation(ch[:, :, :], k.ctx_t[:, :, cols(b, 0, P)], ACT.Copy).then_inc(s["slot_hi"], 1)

            def high_part_of_probs(b, g, n):
                done(act, "p_turned", n)
                freed(act, "pv_done", n)
                nc.scalar.activation(pth[:, :], ps_pt[:, :], ACT.Copy).then_inc(s["pt_high"], 1)

            def exps(b, g, n):
                done(act, "nmax_done", n)
                freed(act, "probn_done", n)
                for r in range(GH):
                    last = nc.scalar.activation(prob[:, r * P:(r + 1) * P], sc[:, r * P:(r + 1) * P], ACT.Exp,
                                                bias=nmax[:, r:r + 1], accum_out=rsum[:, r:r + 1])
                last.then_inc(s["exp_done"], 1)

            def high_part_of_out(b, g, n):
                done(act, "pv_done", n)
                if type(n) is not int or n >= 1:
                    freed(act, "wo_done", n - 1)
                nc.scalar.activation(oh[:, g % 2, :], ps_o[:, :], ACT.Copy).then_inc(s["oh_ready"], 1)

            def squares(b, g, n):
                done(act, "qkv_ready", n)
                freed(act, "ssum_done", n)
                nc.scalar.activation(sq[:, :], qkv[:, g % 2, 0:5 * P], ACT.Square).then_inc(s["sq_done"], 1)

            def keep_q(b, g, n):
                done(act, "q_turned", n)
                nc.scalar.activation(qt[:, g, :], ps_qt[:, :], ACT.Copy).then_inc(s["qt_ready"], 1)

            def keep_k(b, g, n):
                done(act, "k_turned", n)
                nc.scalar.activation(kt[:, g, :], ps_kt[:, 0:P], ACT.Copy, scale=k.key_scale[:, 0:1]).then_inc(s["kt_ready"], 1)

            def keep_v(b, g, n):
                if type(b) is not int or b > 0:
                    done(act, "pv_done", n - NKV0)
                nc.scalar.activation(vh[:, g, :], qkv[:, g % 2, 5 * P:6 * P], ACT.Copy).then_inc(s["v_high"], 1)

            def step(b, g):
                stage(b, g, 1, high_part_of_probs)
                stage(b + 1, g, 1, keep_q)
                stage(b, g, 0, exps)
                if g == NKV0 - 1:
                    high_parts(b + 2)
                stage(b, g, 1, high_part_of_out)
                stage(b + 1, g, 2, keep_k)
                stage(b + 1, g, 1, keep_v)
                stage(b + 1, g, 0, squares)

            def split(g):
                act.wait_ge(k.wa_loaded[g], 16)
                nc.scalar.activation(k.wa_hi[:, g, PROJ], k.wa_raw[:, g, PROJ], ACT.Copy).then_inc(proj_hi, 1)

            def split_out(g):
                nc.scalar.activation(k.wa_hi[:, g, OUT], k.wa_raw[:, g, OUT], ACT.Copy).then_inc(out_hi, 1)

            start_ahead(act, "exp_done", "sq_done", "qt_ready", "kt_ready")
            act.wait_ge(k.ctx_loaded[0], 16)
            act.wait_ge(scaled, 1)
            program(act, step, high_parts, split, split_out, lead=2)

        @block.gpsimd
        def _(pool):
            def inverse_norms(b, g, n):
                done(pool, "ssum_done", n)
                nc.gpsimd.tensor_tensor(sume[:, :], ssum[:, :], k.eps_a[:, :], ALU.add).then_inc(s["sume_done"], 1)
                done(pool, "sume_done", n)
                nc.gpsimd.tensor_tensor(rnorm[:, g, :], sume[:, :], k.neg_half[:, 0:5], ALU.pow).then_inc(s["rnorm_done"], 1)
                done(pool, "rnorm_done", n)
                freed(pool, "k_turned", n)
                nc.gpsimd.tensor_tensor(kn[:, :], qkv[:, g % 2, 4 * P:5 * P], rnorm[:, g, 4:5].broadcast_to([P, P]),
                                        ALU.mult).then_inc(s["kn_done"], 1)

            def normed_probs(b, g, n):
                done(pool, "rinv_done", n)
                freed(pool, "p_turned", n)
                nc.gpsimd.tensor_tensor(probn[:, :].rearrange("p (r e) -> p r e", r=GH),
                                        prob[:, :].rearrange("p (r e) -> p r e", r=GH),
                                        rinv[:, :].rearrange("p (r o) -> p r o", o=1).broadcast_to([P, GH, P]),
                                        ALU.mult).then_inc(s["probn_done"], 1)

            def step(b, g):
                stage(b, g, 0, normed_probs)
                stage(b + 1, g, 1, inverse_norms)

            def split_out(g):
                pool.wait_ge(out_hi, g + 1)
                nc.gpsimd.tensor_tensor(k.wa_lo[:, g, OUT], k.wa_raw[:, g, OUT],
                                        k.wa_hi[:, g, OUT].bitcast(F32), ALU.subtract).then_inc(out_lo, 1)

            start_ahead(pool, "probn_done", "kn_done", "rnorm_done")
            def next_norm(g):
                if g == NKV0 - 1:
                    pool.wait_ge(next_mv, B - 1)
                    nc.gpsimd.tensor_tensor(k.vpe[:, 0:B - 1], k.mv[:, 0:B - 1, 1], k.eps[:, 0:B - 1], ALU.add).then_inc(next_vpe, 1)
                    pool.wait_ge(next_vpe, 1)
                    nc.gpsimd.tensor_tensor(k.rstd[:, 0:B - 1], k.vpe[:, 0:B - 1], k.neg_half[:, 0:B - 1], ALU.pow)

            program(pool, step, split_out=split_out, late=next_norm)


def router_and_layer1_keys(nc, io, k):
    with ExitStack() as ctx:
        m = Mem(nc, ctx)
        bank = banks(k)
        ps_logit_t, ps_logit, ps_comb = bank[0:2], bank[2], bank[3:5]
        side = banks(k, 5, 3)
        wqp = m.sb("e_wqp", [P, 2 * KC, D])
        amax = m.sb("e_amax", [P, 2 * KC])
        scale = m.sb("e_scale", [P, 2 * KC])
        inv = m.sb("e_inv", [P, 2 * KC])
        rounded = m.sb("e_rounded", [P, 2 * KC, D])
        scale_cols = m.sb("e_scale_cols", [P, 2 * KC, P])
        wkv = m.sb("e_wkv", [P, KC, 2 * D])
        wkv_hi = m.sb("e_wkv_hi", [P, KC, 2 * D], F32R)
        wkv_lo = m.sb("e_wkv_lo", [P, KC, 2 * D], F32R)
        ctx_hi = m.sb("e_ctx_hi", [P, KC, T], F32R)
        ctx_lo = m.sb("e_ctx_lo", [P, KC, T], F32R)
        bk = m.sb("e_bk", [P, KC])
        wsum = m.sb("e_wsum", [P, 3])
        ones = m.sb("e_ones", [P, P])
        stats = m.sb("c_stats", [P, 6])
        xn = m.sb("c_xn", [P, B, D])
        logit_t = m.sb("c_logit_t", [NE, T])
        gw = m.sb("c_gw", [P, KC, NE])
        gw_hi = m.sb("c_gw_hi", [P, KC, NE], F32R)
        gw_lo = m.sb("c_gw_lo", [P, KC, NE], F32R)
        nmax = m.sb("c_nmax", [P, B])
        logit = m.sb("c_logit", [P, B, NE])
        ex = m.sb("c_ex", [P, B, NE])
        esum = m.sb("c_esum", [P, B])
        einv = m.sb("c_einv", [P, B])
        prob = m.sb("c_prob", [P, B, NE + TOPK])
        top = m.sb("c_top", [P, B, TOPK])
        tsum = m.sb("c_tsum", [P, 2, B])
        tinv = m.sb("c_tinv", [P, 2, B])
        cum = m.sb("c_cum", [P, B, TOPK])
        kept = m.sb("c_kept", [P, B, TOPK])
        left = m.sb("c_left", [P, B, TOPK])
        find = m.sb("c_find", [P, B, TOPK])
        rest = m.sb("c_rest", [P, B, NE + TOPK])
        sel = m.sb("c_sel", [P, B, NE])
        comb = m.sb("c_comb", [P, B, NE])
        comb_t = k.comb_t
        names = ("gw_loaded", "gw_hi", "gw_lo", "stats", "mv", "vpe", "rstd", "xn_ready", "x_turned", "x_hi", "x_lo",
                 "logits_t", "logits_t_kept",
                 "logits", "exps", "probs", "comb_ready", "comb_turned", "comb_kept", "chain",
                 "wkv_loaded", "wqp_loaded", "w_hi", "bk_loaded", "small_loaded", "kv_hi", "ctx_lo", "wkv_lo", "side_made", "side_kept",
                 "row_scales", "scale_cols", "row_rounded", "clipped", "ones_set", "sums", "gamma_made")
        s = {n: m.sem(f"c_{n}") for n in names}
        wf_loaded = [m.sem(f"c_wf_loaded{j}") for j in range(3)]
        k.comb_stored = m.sem("c_comb_stored")
        k.w_loaded = [m.sem(f"d_w_loaded{j}") for j in range(3)]
        block = ctx.enter_context(nc.Block())

        @block.sync
        def _(sp):
            sp.dma_start(gw[:, :, :], io["gate_t"]).then_inc(s["gw_loaded"], 16)
            sp.dma_start(wqp[:, :, :], io["wqp"]).then_inc(s["wqp_loaded"], 16)
            sp.dma_start(wkv[:, :, :], io["wkv_t"]).then_inc(s["wkv_loaded"], 16)
            sp.dma_start(bk[:, :], io["bk1"]).then_inc(s["bk_loaded"], 16)
            for j in range(3):
                sp.dma_start(k.wf[:, j, :], io[("gate_w", "val_w", "out_w")[j]]).then_inc(wf_loaded[j], 16)
            for j in range(3):
                sp.dma_start(k.raw[:, j, :], io["wm"][j]).then_inc(k.w_loaded[j], 16)
            sp.dma_start(k.bq[:, :], io["bq1"]).then_inc(s["small_loaded"], 16)
            sp.dma_start(k.bv[:, :], io["bv1"].partition_broadcast(P)).then_inc(s["small_loaded"], 16)
            sp.dma_start(k.bias1[:, :], io["bias1"].partition_broadcast(P)).then_inc(s["small_loaded"], 16)
            sp.wait_ge(s["small_loaded"], 48)
            sp.wait_ge(s["comb_kept"], 2)
            sp.dma_start(k.comb_dram, comb_t[:, :]).then_inc(k.comb_stored, 16)

        @block.gpsimd
        def _(pool):
            pool.wait_ge(s["mv"], 1)
            nc.gpsimd.tensor_tensor(k.vpe[:, B - 1:B], k.mv[:, B - 1:B, 1], k.eps[:, 0:1], ALU.add).then_inc(s["vpe"], 1)
            pool.wait_ge(s["vpe"], 1)
            nc.gpsimd.tensor_tensor(k.rstd[:, B - 1:B], k.vpe[:, B - 1:B], k.neg_half[:, 0:1], ALU.pow).then_inc(s["rstd"], 1)
            nc.gpsimd.memset(ones[:, :], 1.0).then_inc(s["ones_set"], 1)
            pool.wait_ge(s["kv_hi"], 2)
            nc.gpsimd.tensor_tensor(wkv_lo[:, :, :], wkv[:, :, :], wkv_hi[:, :, :].bitcast(F32), ALU.subtract).then_inc(s["wkv_lo"], 1)
            pool.wait_ge(s["row_rounded"], 1)
            nc.gpsimd.tensor_scalar(rounded[:, :, :], wqp[:, :, :], RND + 127.0, RND - 127.0, ALU.min, ALU.max
                                    ).then_inc(s["clipped"], 1)
            pool.wait_ge(s["w_hi"], 1)
            nc.gpsimd.tensor_tensor(k.w_lo[:, 0, :], k.raw[:, 0, :], k.w_hi[:, 0, :].bitcast(F32), ALU.subtract)

        @block.vector
        def _(dve):
            nc.vector.bn_stats(stats[:, :], k.x_res[:, B - 1, :]).then_inc(s["stats"], 1)
            for t in range(B):
                if t == 1:
                    dve.wait_ge(s["stats"], 1)
                    nc.vector.bn_aggr(k.mv[:, B - 1, :], stats[:, :]).then_inc(s["mv"], 1)
                if t == B - 1:
                    dve.wait_ge(s["rstd"], 1)
                nc.vector.tensor_scalar(xn[:, t, :], k.x_res[:, t, :], k.mv[:, t, 0:1], k.rstd[:, t:t + 1],
                                        ALU.subtract, ALU.mult).then_inc(s["xn_ready"], 1)
            nc.vector.memset(prob[:, :, NE:], -1.0)
            dve.wait_ge(s["gw_hi"], 1)
            nc.vector.tensor_tensor(gw_lo[:, :, :], gw[:, :, :], gw_hi[:, :, :].bitcast(F32), ALU.subtract).then_inc(s["gw_lo"], 1)
            for t in range(B):
                dve.wait_ge(s["x_hi"], t + 1)
                x_hi = k.xn_hi[:, :, t * P:(t + 1) * P]
                nc.vector.tensor_tensor(k.xn_lo[:, :, t * P:(t + 1) * P], bank[t][:, 0:D].rearrange("p (c n) -> p c n", c=KC),
                                        x_hi.bitcast(F32), ALU.subtract).then_inc(s["x_lo"], 1)
            dve.wait_ge(s["wqp_loaded"], 16)
            nc.vector.tensor_reduce(amax[:, :], wqp[:, :, :], AX_X, ALU.max, apply_absolute_value=True).then_inc(s["row_scales"], 1)
            dve.wait_ge(s["row_scales"], 1)
            nc.vector.tensor_scalar(scale[:, :], amax[:, :], 1.0 / 127.0, 1e-8, ALU.mult, ALU.max).then_inc(s["row_scales"], 1)
            dve.wait_ge(s["row_scales"], 2)
            nc.vector.reciprocal(inv[:, :], scale[:, :]).then_inc(s["row_scales"], 1)
            nc.vector.tensor_copy(k.wq_scale[:, :], scale[:, 0:KC])
            nc.vector.tensor_copy(scale_cols[:, :, :], scale[:, :].rearrange("p (r o) -> p r o", o=1).broadcast_to(
                [P, 2 * KC, P])).then_inc(s["scale_cols"], 1)
            dve.wait_ge(s["kv_hi"], 1)
            nc.vector.tensor_tensor(ctx_lo[:, :, :], k.ctx_t[:, :, :], ctx_hi[:, :, :].bitcast(F32), ALU.subtract).then_inc(s["ctx_lo"], 1)
            dve.wait_ge(s["logits_t"], 1)
            nc.vector.tensor_copy(logit_t[:, 0:T // 2], ps_logit_t[0][0:NE, :]).then_inc(s["logits_t_kept"], 1)

            at = [0]

            def chained(ins):
                at[0] += 1
                ins.then_inc(s["chain"], 1)
                dve.wait_ge(s["chain"], at[0])

            wide = [P, B, NE]
            by_token = lambda a, n: a.rearrange("p (b o) -> p b o", o=1).broadcast_to([P, B, n])
            logits = ps_logit[:, 0:B * NE].rearrange("p (b e) -> p b e", b=B)
            dve.wait_ge(s["logits"], 1)
            chained(nc.vector.tensor_reduce(nmax[:, :], logits, AX_X, ALU.max, negate=True))
            nc.vector.tensor_tensor(logit[:, :, :], logits, by_token(nmax[:, :], NE), ALU.add).then_inc(s["probs"], 1)
            dve.wait_ge(s["exps"], 1)
            chained(nc.vector.tensor_reduce(esum[:, :], ex[:, :, :], AX_X, ALU.add))
            chained(nc.vector.reciprocal(einv[:, :], esum[:, :]))
            chained(nc.vector.tensor_tensor(prob[:, :, 0:NE], ex[:, :, :], by_token(einv[:, :], NE), ALU.mult))
            for t in range(B):
                last = nc.vector.max(top[:, t, :], prob[:, t, 0:NE])
            chained(last)
            chained(nc.vector.tensor_reduce(tsum[:, 0, :], top[:, :, :], AX_X, ALU.add))
            chained(nc.vector.tensor_scalar(tsum[:, 0, :], tsum[:, 0, :], 1e-12, None, ALU.max))
            chained(nc.vector.reciprocal(tinv[:, 0, :], tsum[:, 0, :]))
            chained(nc.vector.tensor_tensor(cum[:, :, :], top[:, :, :], by_token(tinv[:, 0, :], TOPK), ALU.mult))
            for j in range(1, TOPK):
                chained(nc.vector.tensor_tensor(cum[:, :, j], cum[:, :, j - 1], cum[:, :, j], ALU.add))
            nc.vector.tensor_copy(kept[:, :, 0], top[:, :, 0])
            nc.vector.tensor_copy(find[:, :, 0], top[:, :, 0])
            nc.vector.tensor_scalar(left[:, :, 1:], cum[:, :, 0:TOPK - 1], THRESHOLD, 1.0, ALU.is_lt, ALU.subtract)
            chained(nc.vector.scalar_tensor_tensor(kept[:, :, 1:], cum[:, :, 0:TOPK - 1], THRESHOLD, top[:, :, 1:],
                                                   ALU.is_lt, ALU.mult))
            nc.vector.tensor_tensor(find[:, :, 1:], kept[:, :, 1:], left[:, :, 1:], ALU.add)
            chained(nc.vector.tensor_reduce(tsum[:, 1, :], kept[:, :, :], AX_X, ALU.add))
            chained(nc.vector.tensor_scalar(tsum[:, 1, :], tsum[:, 1, :], 1e-12, None, ALU.max))
            chained(nc.vector.reciprocal(tinv[:, 1, :], tsum[:, 1, :]))
            for t in range(B):
                last = nc.vector.match_replace(rest[:, t, :], find[:, t, :], prob[:, t, :], -2.0)
            chained(last)
            chained(nc.vector.tensor_tensor(sel[:, :, :], rest[:, :, 0:NE], prob[:, :, 0:NE], ALU.not_equal))
            chained(nc.vector.tensor_tensor(sel[:, :, :], sel[:, :, :], prob[:, :, 0:NE], ALU.mult))
            nc.vector.tensor_tensor(comb[:, :, :], sel[:, :, :], by_token(tinv[:, 1, :], NE), ALU.mult).then_inc(s["comb_ready"], 1)
            dve.wait_ge(wf_loaded[2], 16)
            nc.vector.tensor_reduce(wsum[:, 2:3], k.wf[:, 2, :], AX_X, ALU.add, apply_absolute_value=True).then_inc(s["sums"], 1)
            dve.wait_ge(s["comb_turned"], 1)
            nc.vector.tensor_copy(comb_t[:, 0:T // 2], ps_comb[0][0:NE, :]).then_inc(s["comb_kept"], 1)
            dve.wait_ge(s["gamma_made"], 1)
            chained(nc.vector.tensor_scalar(k.gamma[:, :], ps_logit_t[0][:, 0:3], 1.0 / (D * HIDDEN), 1e-5, ALU.mult, ALU.max))
            nc.vector.reciprocal(k.ginv[:, :], k.gamma[:, :])

        @block.scalar
        def _(act):
            act.wait_ge(s["gw_loaded"], 16)
            nc.scalar.activation(gw_hi[:, :, :], gw[:, :, :], ACT.Copy).then_inc(s["gw_hi"], 1)
            for t in range(B):
                act.wait_ge(s["x_turned"], t + 1)
                nc.scalar.activation(k.xn_hi[:, :, t * P:(t + 1) * P], bank[t][:, 0:D].rearrange("p (c n) -> p c n", c=KC),
                                     ACT.Copy).then_inc(s["x_hi"], 1)
            nc.scalar.activation(ctx_hi[:, :, :], k.ctx_t[:, :, :], ACT.Copy).then_inc(s["kv_hi"], 1)
            act.wait_ge(s["wkv_loaded"], 16)
            nc.scalar.activation(wkv_hi[:, :, :], wkv[:, :, :], ACT.Copy).then_inc(s["kv_hi"], 1)
            act.wait_ge(s["logits_t"], 2)
            nc.scalar.activation(logit_t[:, T // 2:], ps_logit_t[1][0:NE, :], ACT.Copy).then_inc(s["logits_t_kept"], 1)
            act.wait_ge(s["probs"], 1)
            nc.scalar.activation(ex[:, :, :], logit[:, :, :], ACT.Exp).then_inc(s["exps"], 1)

            def keep_side(n):
                act.wait_ge(s["side_made"], n + 1)
                if n < 4:
                    c, half = n // 2, n % 2
                    keep = nc.scalar.activation(k.k1_t[:, c, half * 512:(half + 1) * 512], side[n % 3][:, :], ACT.Identity,
                                                bias=bk[:, c:c + 1])
                else:
                    keep = nc.scalar.activation(k.v1[:, 2 * (n - 4):2 * (n - 3), :],
                                                side[n % 3][:, :].rearrange("p (b d) -> p b d", b=2), ACT.Copy)
                keep.then_inc(s["side_kept"], 1)

            def sum_sizes(j):
                act.wait_ge(wf_loaded[j], 16)
                nc.scalar.activation(k.w_ffn[:, j, :], k.wf[:, j, :], ACT.Abs, accum_out=wsum[:, j:j + 1]).then_inc(s["sums"], 1)

            act.wait_ge(s["bk_loaded"], 16)
            keep_side(0)
            act.wait_ge(s["row_scales"], 3)
            for r in range(2 * KC):
                last = nc.scalar.activation(wqp[:, r, :], wqp[:, r, :], ACT.Copy, bias=RND, scale=inv[:, r:r + 1])
            last.then_inc(s["row_rounded"], 1)
            keep_side(1)
            keep_side(2)
            sum_sizes(0)
            keep_side(3)
            keep_side(4)
            sum_sizes(1)
            keep_side(5)
            keep_side(6)
            act.wait_ge(k.w_loaded[0], 16)
            nc.scalar.activation(k.w_hi[:, 0, :], k.raw[:, 0, :], ACT.Copy).then_inc(s["w_hi"], 1)
            keep_side(7)
            act.wait_ge(s["comb_turned"], 1)
            nc.scalar.activation(comb_t[:, T // 2:], ps_comb[1][0:NE, :], ACT.Copy).then_inc(s["comb_kept"], 1)
            for n in range(8, 10):
                act.wait_ge(s["side_made"], n + 1)
                nc.scalar.activation(k.wqp_t[:, n - 8, :, :], side[n % 3][:, :].rearrange("p (c n) -> p c n", c=KC),
                                     ACT.Copy, bias=-RND).then_inc(s["side_kept"], 1)
            act.wait_ge(s["side_made"], 11)
            nc.scalar.activation(k.scale_qp[:, :], side[10 % 3][:, :], ACT.Copy).then_inc(s["side_kept"], 1)
        @block.tensor
        def _(pe):
            for t in range(B):
                pe.wait_ge(s["xn_ready"], t + 1)
                for c in range(KC):
                    last = nc.tensor.transpose(bank[t][:, c * P:(c + 1) * P], xn[:, t, c * P:(c + 1) * P], k.ident[:, :])
                last.then_inc(s["x_turned"], 1)
            pe.wait_ge(s["gw_lo"], 1)
            pe.wait_ge(s["x_lo"], B)
            for half in range(2):
                for c in range(KC):
                    x_hi, x_lo = (x[:, c, half * T // 2:(half + 1) * T // 2] for x in (k.xn_hi, k.xn_lo))
                    out = ps_logit_t[half][0:NE, :]
                    nc.tensor.matmul(out, gw_hi[:, c, :], x_hi, start=c == 0, stop=False)
                    nc.tensor.matmul(out, gw_lo[:, c, :], x_hi, start=False, stop=False)
                    last = nc.tensor.matmul(out, gw_hi[:, c, :], x_lo, start=False, stop=c == KC - 1)
                last.then_inc(s["logits_t"], 1)
            pe.wait_ge(s["logits_t_kept"], 2)
            for t in range(B):
                last = nc.tensor.transpose(ps_logit[:, t * NE:(t + 1) * NE], logit_t[:, t * P:(t + 1) * P], k.ident[0:NE, 0:NE])
            last.then_inc(s["logits"], 1)

            def side_free(n):
                if n >= 3:
                    pe.wait_ge(s["side_kept"], n - 2)
                return side[n % 3]

            pe.wait_ge(s["ctx_lo"], 1)
            pe.wait_ge(s["wkv_lo"], 1)
            for n in range(4):
                c, half = n // 2, n % 2
                ps = side_free(n)
                for kc in range(KC):
                    w_hi, w_lo = (w[:, kc, c * P:(c + 1) * P] for w in (wkv_hi, wkv_lo))
                    c_hi, c_lo = (a[:, kc, half * 512:(half + 1) * 512] for a in (ctx_hi, ctx_lo))
                    nc.tensor.matmul(ps[:, :], w_hi, c_hi, start=kc == 0, stop=False)
                    nc.tensor.matmul(ps[:, :], w_hi, c_lo, start=False, stop=False)
                    last = nc.tensor.matmul(ps[:, :], w_lo, c_hi, start=False, stop=kc == KC - 1)
                last.then_inc(s["side_made"], 1)
            for n in range(4, 8):
                ps = side_free(n)
                for b in (2 * (n - 4), 2 * (n - 4) + 1):
                    out = ps[:, b % 2 * D:(b % 2 + 1) * D]
                    for kc in range(KC):
                        w_hi, w_lo = (w[:, kc, D:2 * D] for w in (wkv_hi, wkv_lo))
                        c_hi, c_lo = (a[:, kc, b * P:(b + 1) * P] for a in (ctx_hi, ctx_lo))
                        nc.tensor.matmul(out, c_hi, w_hi, start=kc == 0, stop=False)
                        nc.tensor.matmul(out, c_hi, w_lo, start=False, stop=False)
                        last = nc.tensor.matmul(out, c_lo, w_hi, start=False, stop=kc == KC - 1)
                last.then_inc(s["side_made"], 1)
            pe.wait_ge(s["comb_ready"], 1)
            for t in range(B):
                last = nc.tensor.transpose(ps_comb[t // 4][0:NE, t % 4 * P:(t % 4 + 1) * P], comb[:, t, :], k.ident[:, :])
            last.then_inc(s["comb_turned"], 1)
            pe.wait_ge(s["clipped"], 1)
            for n in range(8, 10):
                ps = side_free(n)
                for r in range(KC):
                    for c in range(KC):
                        last = nc.tensor.transpose(ps[:, c * D + r * P:c * D + (r + 1) * P],
                                                   rounded[:, (n - 8) * KC + r, c * P:(c + 1) * P], k.ident[:, :])
                last.then_inc(s["side_made"], 1)
            ps = side_free(10)
            pe.wait_ge(s["scale_cols"], 1)
            for r in range(2 * KC):
                last = nc.tensor.matmul(ps[:, r * P:(r + 1) * P], scale_cols[:, r, :], k.ident[:, :], start=True, stop=True)
            last.then_inc(s["side_made"], 1)
            pe.wait_ge(s["ones_set"], 1)
            pe.wait_ge(s["sums"], 3)
            nc.tensor.matmul(ps_logit_t[0][:, 0:3], ones[:, :], wsum[:, :], start=True, stop=True).then_inc(s["gamma_made"], 1)


def invert_stds(nc, pool, made, k, a, b):
    nc.gpsimd.tensor_tensor(k.vpe[:, a:b], k.mv[:, a:b, 1], k.eps[:, a:b], ALU.add).then_inc(made, 1)
    nc.gpsimd.tensor_tensor(k.neg_mean[:, a:b], k.mv[:, a:b, 0], k.minus_one[:, a:b], ALU.mult).then_inc(made, 1)
    pool.wait_ge(made, 1)
    nc.gpsimd.tensor_tensor(k.rstd[:, a:b], k.vpe[:, a:b], k.neg_half[:, a:b], ALU.pow).then_inc(made, 1)
    pool.wait_ge(made, 3)
    nc.gpsimd.tensor_tensor(k.nmr[:, a:b], k.neg_mean[:, a:b], k.rstd[:, a:b], ALU.mult).then_inc(made, 1)


def experts(nc, io, k):
    with ExitStack() as ctx:
        m = Mem(nc, ctx)
        ps_g, ps_u = banks(k, 0, 2), banks(k, 2, 2)
        acc = banks(k, 4, 4)
        HALF = T // 2
        raw, w_hi, w_lo, w_loaded = k.raw, k.w_hi, k.w_lo, k.w_loaded
        weight = m.sb("d_weight", [P, 3, T])
        silu = m.sb("d_silu", [P, 2, HALF])
        gu = m.sb("d_gu", [P, 2, HALF])
        h = m.sb("d_h", [P, 2, HALF])
        h_hi = m.sb("d_h_hi", [P, 2, HALF], F32R)
        h_lo = m.sb("d_h_lo", [P, 2, HALF], F32R)
        y_t = m.sb("d_y_t", [P, KC, T])
        stats = m.sb("d_stats", [P, FIRST, 6])
        seen = m.sb("d_seen", [P, 1])
        ahead = ("gu_done", "h_done", "down_done", "lo_done", "h_lo_done")
        plain = ("gate_up_done", "silu_done", "h_hi_done", "hi_done", "acc_kept0", "acc_kept1", "y_turned", "y_added",
                 "piece_rounded", "piece_clipped", "stats", "mv", "std")
        s = {n: m.sem(f"d_{n}") for n in ahead + plain}
        weight_loaded = [m.sem(f"d_weight_loaded{j}") for j in range(3)]
        block = ctx.enter_context(nc.Block())
        SEGMENTS = [(j, max(q * INTER, j * P) - j * P, min((q + 1) * INTER, (j + 1) * P) - j * P, q)
                    for j in range(3) for q in range(4) if q * INTER < (j + 1) * P and (q + 1) * INTER > j * P]

        def done(eng, name, n):
            eng.wait_ge(s[name], n + (2 if name in ahead else 1))

        def freed(eng, name, n):
            if type(n) is not int or n >= 2:
                eng.wait_ge(s[name], n)

        def stage(i, u, lag, work):
            i, u = (i, u - lag) if u >= lag else (i - 1, u - lag + 6)
            if type(i) is not int or 0 <= i < MT // 3:
                work(i, u // 2, u % 2, i * 6 + u)

        def program(eng, step):
            for u in range(6):
                step(0, u)
            with eng.Fori(1, MT // 3 - 1) as i:
                for u in range(6):
                    step(i, u)
            for i, steps in ((MT // 3 - 1, 6), (MT // 3, 2)):
                for u in range(steps):
                    step(i, u)

        def next_tile(i, u, work):
            j = u // 2 + 1
            if u % 2 == 0 and not (type(i) is int and i * 3 + j >= MT):
                work(*((i, j) if j < 3 else (i + 1, 0)))

        def piece(a, n):
            return a[:, n // 2, n % 2 * HIDDEN:(n % 2 + 1) * HIDDEN]

        @block.sync
        def _(sp):
            def load(i, j):
                if type(i) is not int:
                    sp.wait_ge(s["lo_done"], i * 3 + (j - 1))
                    sp.dma_start(raw[:, j, :], io["wm"][bass.ds(i * 3 + j, 1)].rearrange("o p n -> p (o n)")
                                 ).then_inc(w_loaded[j], 16)
                    sp.wait_ge(s["h_done"], i * 6 + (2 * j - 3))
                for jj, a, b, q in SEGMENTS:
                    if jj == j:
                        sp.dma_start(weight[a:b, j, :], k.comb_dram[bass.ds(i * 4 + q, 1), :].broadcast_to([b - a, T])
                                     ).then_inc(weight_loaded[j], 16)

            sp.wait_ge(k.comb_stored, 16)
            for j in range(3):
                load(0, j)
            with sp.Fori(1, MT // 3) as i:
                for j in range(3):
                    load(i, j)

        @block.tensor
        def _(pe):
            def gate_up(i, j, half, n):
                if half == 0:
                    done(pe, "lo_done", i * 3 + j)
                freed(pe, "gu_done", n)
                for ps, at in ((ps_g[half], 0), (ps_u[half], KC * P)):
                    for c in range(KC):
                        hi, lo = (w[:, j, at + c * P:at + (c + 1) * P] for w in (w_hi, w_lo))
                        x_hi, x_lo = (x[:, c, half * HALF:(half + 1) * HALF] for x in (k.xn_hi, k.xn_lo))
                        nc.tensor.matmul(ps[:, :], hi, x_hi, start=c == 0, stop=False)
                        nc.tensor.matmul(ps[:, :], hi, x_lo, start=False, stop=False)
                        last = nc.tensor.matmul(ps[:, :], lo, x_hi, start=False, stop=c == KC - 1)
                last.then_inc(s["gate_up_done"], 1)

            def down(i, j, half, n):
                done(pe, "h_lo_done", n)
                first = type(i) is int and i == 0 and j == 0
                for c in range(KC):
                    hi, lo = (w[:, j, 2 * KC * P + c * P:2 * KC * P + (c + 1) * P] for w in (w_hi, w_lo))
                    out = acc[2 * c + half]
                    nc.tensor.matmul(out[:, :], hi, h_hi[:, half, :], start=first, stop=False, skip_group_check=True)
                    nc.tensor.matmul(out[:, :], hi, h_lo[:, half, :], start=False, stop=False, skip_group_check=True)
                    last = nc.tensor.matmul(out[:, :], lo, h_hi[:, half, :], start=False, stop=True, skip_group_check=True)
                last.then_inc(s["down_done"], 1)

            def step(i, u):
                stage(i, u, 0, gate_up)
                stage(i, u, 2, down)

            pe.sem_inc(s["down_done"], 1)
            program(pe, step)
            for t in range(B):
                if t % 4 == 0:
                    pe.wait_ge(s[f"acc_kept{t // 4}"], 2)
                if t >= 4:
                    pe.wait_ge(s["y_added"], t - 3)
                ps = (ps_g + ps_u)[t % 4]
                for c in range(KC):
                    last = nc.tensor.transpose(ps[:, c * P:(c + 1) * P], y_t[:, c, t * P:(t + 1) * P], k.ident[:, :])
                last.then_inc(s["y_turned"], 1)

        @block.scalar
        def _(act):
            def hi_part(i, j):
                act.wait_ge(w_loaded[j], i * 16 + 16)
                if type(i) is not int or i > 0:
                    act.wait_ge(s["down_done"], i * 6 + (2 * j - 3))
                nc.scalar.activation(w_hi[:, j, :], raw[:, j, :], ACT.Copy).then_inc(s["hi_done"], 1)

            def silus(i, j, half, n):
                done(act, "gate_up_done", n)
                freed(act, "gu_done", n)
                nc.scalar.activation(silu[:, half, :], ps_g[half][:, :], ACT.Silu).then_inc(s["silu_done"], 1)

            def h_high(i, j, half, n):
                done(act, "h_done", n)
                freed(act, "down_done", n)
                nc.scalar.activation(h_hi[:, half, :], h[:, half, :], ACT.Copy).then_inc(s["h_hi_done"], 1)

            def step(i, u):
                stage(i, u, 0, silus)
                stage(i, u, 1, h_high)
                next_tile(i, u, hi_part)
                if type(i) is int and i == 0:
                    nc.scalar.activation(piece(k.wf, u), piece(k.wf, u), ACT.Copy, bias=RND, scale=k.ginv[:, u // 2:u // 2 + 1]
                                         ).then_inc(s["piece_rounded"], 1)
                    if u >= 1:
                        integers(u - 1)

            def integers(n):
                act.wait_ge(s["piece_clipped"], n + 1)
                nc.scalar.activation(piece(k.w_ffn, n), piece(k.wf, n), ACT.Copy, bias=-RND)

            act.sem_inc(s["hi_done"], 1)
            program(act, step)
            nc.scalar.activation(seen[:, :], k.ident[:, 0:1], ACT.Exp)
            for half in range(2):
                done(act, "down_done", 2 * MT - 2 + half)
                n = 2 + half
                nc.scalar.activation(y_t[:, n // 2, n % 2 * HALF:(n % 2 + 1) * HALF], acc[n][:, :], ACT.Copy).then_inc(s[f"acc_kept{half}"], 1)
            integers(5)

        @block.vector
        def _(dve):
            def lo_part(i, j):
                dve.wait_ge(s["hi_done"], i * 3 + (j + 1))
                nc.vector.tensor_tensor(w_lo[:, j, :], raw[:, j, :], w_hi[:, j, :].bitcast(F32),
                                        ALU.subtract).then_inc(s["lo_done"], 1)

            def gate_times_up(i, j, half, n):
                done(dve, "silu_done", n)
                freed(dve, "h_done", n)
                nc.vector.tensor_tensor(gu[:, half, :], silu[:, half, :], ps_u[half][:, :], ALU.mult).then_inc(s["gu_done"], 1)

            def h_low(i, j, half, n):
                done(dve, "h_hi_done", n)
                nc.vector.tensor_tensor(h_lo[:, half, :], h[:, half, :], h_hi[:, half, :].bitcast(F32),
                                        ALU.subtract).then_inc(s["h_lo_done"], 1)

            def step(i, u):
                stage(i, u, 0, gate_times_up)
                stage(i, u, 1, h_low)
                next_tile(i, u, lo_part)
                if type(i) is int and i == 0:
                    dve.wait_ge(s["piece_rounded"], u + 1)
                    nc.vector.tensor_scalar(piece(k.wf, u), piece(k.wf, u), RND + 1.0, RND - 1.0, ALU.min, ALU.max
                                            ).then_inc(s["piece_clipped"], 1)

            dve.sem_inc(s["gu_done"], 1)
            dve.sem_inc(s["lo_done"], 2)
            dve.sem_inc(s["h_lo_done"], 1)
            program(dve, step)
            for half in range(2):
                done(dve, "down_done", 2 * MT - 2 + half)
                nc.vector.tensor_copy(y_t[:, 0, half * HALF:(half + 1) * HALF], acc[half][:, :]).then_inc(
                    s[f"acc_kept{half}"], 1)
            for t in range(B):
                dve.wait_ge(s["y_turned"], t + 1)
                nc.vector.tensor_tensor(k.x_res[:, t, :], k.x_res[:, t, :], (ps_g + ps_u)[t % 4][:, 0:D],
                                        ALU.add).then_inc(s["y_added"], 1)
                if 1 <= t <= FIRST:
                    dve.wait_ge(s["y_added"], t)
                    nc.vector.bn_stats(stats[:, t - 1, :], k.x_res[:, t - 1, :]).then_inc(s["stats"], 1)
                if 2 <= t <= FIRST + 1:
                    dve.wait_ge(s["stats"], t - 1)
                    nc.vector.bn_aggr(k.mv[:, t - 2, :], stats[:, t - 2, :]).then_inc(s["mv"], 1)

        @block.gpsimd
        def _(pool):
            def weigh(i, j, half, n):
                done(pool, "gu_done", n)
                if half == 0:
                    pool.wait_ge(weight_loaded[j], i * 32 + 32)
                freed(pool, "h_lo_done", n)
                nc.gpsimd.tensor_tensor(h[:, half, :], gu[:, half, :], weight[:, j, half * HALF:(half + 1) * HALF],
                                        ALU.mult).then_inc(s["h_done"], 1)

            pool.sem_inc(s["h_done"], 1)
            program(pool, lambda i, u: stage(i, u, 0, weigh))
            pool.wait_ge(s["mv"], FIRST)
            invert_stds(nc, pool, s["std"], k, 0, FIRST)


def layer1(nc, io, k, out):
    with ExitStack() as ctx:
        m = Mem(nc, ctx)
        QH = NH1 // 4
        VW = P // QH
        FH = HIDDEN // 2
        ps_s = banks(k, 0, 2)
        (ps_t,) = banks(k, 2, 1)
        (ps_turn,) = banks(k, 3, 1)
        ps_g, ps_v, ps_m, ps_o = banks(k, 4, 4)
        ps_m = ps_m[:, 0:D]
        q0 = m.sb("f_q0", [P, D])
        q_t = m.sb("f_q_t", [P, KC, P])
        v_now = m.sb("f_v_now", [P, NH1, VW])
        o_t = m.sb("f_o_t", [P, QH * P])
        kd = m.sb("f_kd", [P, KC, HC, P])
        nmax = m.sb("f_nmax", [P, NH1])
        prob = m.sb("f_prob", [P, NH1, P])
        prob_t = m.sb("f_prob_t", [P, NH1, P])
        sinv = m.sb("f_sinv", [P, NH1])
        o = m.sb("f_o", [P, D])
        oi_t = m.sb("f_oi_t", [P, KC, P], BF16)
        y = m.sb("f_y", [P, D])
        stats = m.sb("f_stats", [P, B, 6])
        stats4 = m.sb("f_stats4", [P, 6])
        mv4 = m.sb("f_mv4", [P, 2])
        vpe4 = m.sb("f_vpe4", [P, 1])
        rstd4 = m.sb("f_rstd4", [P, 1])
        scale3 = m.sb("f_scale3", [P, B])
        xs = m.sb("f_xs", [P, D])
        seen = m.sb("f_seen", [P, 6])
        neg_mean4 = m.sb("f_neg_mean4", [P, 1])
        nmr4 = m.sb("f_nmr4", [P, 1])
        unit = m.sb("f_unit", [P, 2, B])
        gamma = m.sb("f_gamma", [P, 2])
        norm = {n: m.sb(f"f_xn{n}", [P, D]) for n in (3, 4)}
        width = {3: D, 4: D, "o": D, "h": HIDDEN}
        rnd = {n: m.sb(f"f_rnd_{n}", [P, w]) for n, w in width.items()}
        scale = {n: m.sb(f"f_scale_{n}", [P, 1]) for n in width}
        amax = {n: m.sb(f"f_amax_{n}", [P, 1]) for n in (3, 4, "o", "h")}
        inv = {n: m.sb(f"f_inv_{n}", [P, 1]) for n in (3, 4, "o", "h")}
        raw_rnd = {n: m.sb(f"f_raw_rnd_{n}", [P, w]) for n, w in width.items()}
        x3_t = m.sb("f_x3_t", [P, KC, T], BF16)
        x4_t = m.sb("f_x4_t", [P, KC, T], BF16)
        gate = m.sb("f_gate", [P, HIDDEN])
        tanh = m.sb("f_tanh", [P, HIDDEN])
        product = m.sb("f_gate_val", [P, HIDDEN])
        half_bv = m.sb("f_half_bv", [P, HIDDEN])
        val = m.sb("f_val", [P, HIDDEN])
        h = m.sb("f_h", [P, HIDDEN])
        h_unit = m.sb("f_h_unit", [P, 1])
        hi_t = m.sb("f_hi_t", [P, HIDDEN], BF16)
        names = ["halved", "later_stats", "later_mv", "later_std", "neg_mean4", "nmr4",
                 "q_proj", "q_scaled", "q_turned", "q_kept", "v_now", "o_t_kept", "o_back", "sinv", "o", "o_turned", "o_kept", "out", "out_read", "added", "xn3", "x3_turned", "x3_kept", "bias3",
                 "scale3_kept", "stats4", "mv4", "vpe4", "rstd4", "xn4", "x4_turned", "x4_kept", "bias4", "units", "h_raw",
                 "h_unit", "ffn_out", "x_done", "stored"]
        names += [f"{what}_{n}" for n in (3, 4, "o", "h") for what in ("amax", "scale", "inv", "raw", "rnd")]
        for n, count in (("scores", 4), ("nmax", 4), ("exps", 4), ("quarter", 4), ("quarter_kept", 4), ("pv", 4), ("keys", 2),
                         ("mm_gate", 2), ("mm_val", 2), ("gate", 2), ("val", 2), ("tanh", 2), ("product", 2), ("h", 2), ("h_turned", 2),
                         ("h_kept", 2)):
            names += [f"{n}{j}" for j in range(count)]
        s = {n: m.sem(f"f_{n}") for n in names}
        block = ctx.enter_context(nc.Block())

        ahead = ("h_kept1", "x_done", "h_turned1", "ffn_out", "h_raw", "rnd_h")

        def done(eng, name, b):
            if type(b) is not int or 0 <= b < B:
                eng.wait_ge(s[name], b + (2 if name in ahead else 1))

        def stage(b, work, *args):
            if type(b) is not int or 0 <= b < B:
                work(b, *args)

        def program(eng, step, last_step, early=None, early_after=0):
            for b in range(-2, 4):
                step(b)
                if early and b == early_after - 2:
                    early()
            with eng.Fori(4, B - 2) as b:
                step(b)
            for b in range(B - 2, B):
                step(b)
            for b in range(B, B + 4):
                last_step(b)

        def heads_of(ps):
            return ps[:, :].rearrange("p (h d) -> p h d", h=NH1)

        def x_of(b):
            return k.x_res[:, bass.ds(b, 1), :].rearrange("p o d -> p (o d)")

        def turn(src, n):
            for c in range(n):
                last = nc.tensor.transpose(ps_turn[:, c * P:(c + 1) * P], src[:, c * P:(c + 1) * P], k.ident[:, :])
            return last

        @block.tensor
        def _(pe):
            def bank_free(*uses):
                for name, b in uses:
                    done(pe, name, b)

            def scores(b, j):
                c = j // 2
                done(pe, "q_kept", b)
                done(pe, f"keys{c}", b)
                done(pe, f"exps{(j + 2) % 4}", b if j >= 2 else b - 1)
                nc.tensor.matmul(ps_s[j % 2][:, :], q_t[:, c, :], kd[:, c, j % 2 * QH:(j % 2 + 1) * QH, :],
                                 start=True, stop=True).then_inc(s[f"scores{j}"], 1)

            def turn_probs(b, j):
                done(pe, f"exps{j}", b)
                done(pe, f"quarter_kept{(j + 3) % 4}", b if j >= 1 else b - 1)
                for r in range(QH):
                    last = nc.tensor.transpose(ps_t[:, r * P:(r + 1) * P], prob[:, QH * j + r, :], k.ident[:, :])
                last.then_inc(s[f"quarter{j}"], 1)

            def attend(b, j):
                if j == 0:
                    done(pe, "o", b - 1)
                    done(pe, "v_now", b)
                done(pe, f"quarter_kept{j}", b)
                for r in range(QH):
                    last = nc.tensor.matmul(ps_o[r * VW:(r + 1) * VW, j * P:(j + 1) * P], v_now[:, QH * j + r, :],
                                            prob_t[:, QH * j + r, :], start=True, stop=True, tile_position=(0, r * VW))
                last.then_inc(s[f"pv{j}"], 1)

            def turn_back(b):
                done(pe, "o_t_kept", b)
                for j in range(4):
                    last = nc.tensor.transpose(ps_o[:, j * P:(j + 1) * P], o_t[:, j * P:(j + 1) * P], k.ident[:, :])
                last.then_inc(s["o_back"], 1)

            def turn_x3(b):
                done(pe, "rnd_3", b)
                bank_free(("x3_kept", b - 1), ("x4_kept", b - 4), ("o_kept", b - 4), ("h_kept1", b - 6))
                turn(rnd[3], KC).then_inc(s["x3_turned"], 1)

            def q_proj(b):
                done(pe, "x3_kept", b)
                bank_free(("q_kept", b - 1), ("out_read", b - 3))
                for c in range(KC):
                    last = nc.tensor.matmul(ps_m, x3_t[:, c, cols(b, 0, P)], k.wqp_t[:, 0, c, :], start=c == 0, stop=c == KC - 1)
                last.then_inc(s["q_proj"], 1)

            def turn_q(b):
                bank_free(("q_scaled", b), ("x_done", b - 5))
                for c in range(KC):
                    last = nc.tensor.transpose(ps_m[:, c * P:(c + 1) * P], q0[:, c * P:(c + 1) * P], k.ident[:, :])
                last.then_inc(s["q_turned"], 1)

            def turn_o(b):
                done(pe, "rnd_o", b)
                bank_free(("o_kept", b - 1), ("x3_kept", b + 3), ("x4_kept", b - 1), ("h_kept1", b - 3))
                turn(rnd["o"], KC).then_inc(s["o_turned"], 1)

            def out_proj(b):
                done(pe, "o_kept", b)
                bank_free(("out_read", b - 1), ("q_kept", b + 2), ("x_done", b - 3))
                for c in range(KC):
                    last = nc.tensor.matmul(ps_m, oi_t[:, c, :], k.wqp_t[:, 1, c, :], start=c == 0, stop=c == KC - 1)
                last.then_inc(s["out"], 1)

            def turn_x4(b):
                done(pe, "rnd_4", b)
                bank_free(("o_kept", b), ("h_kept1", b - 2))
                turn(rnd[4], KC).then_inc(s["x4_turned"], 1)

            def gate_val(b, half):
                done(pe, "x4_kept", b)
                for name, ps, j in (("gate", ps_g, 0), ("val", ps_v, 1)):
                    done(pe, f"{name}{1 - half}", b if half else b - 1)
                    for c in range(KC):
                        at = c * HIDDEN + half * FH
                        last = nc.tensor.matmul(ps[:, :], x4_t[:, c, cols(b, 0, P)], k.w_ffn[:, j, at:at + FH],
                                                start=c == 0, stop=c == KC - 1)
                    last.then_inc(s[f"mm_{name}{half}"], 1)

            def turn_h(b, j):
                done(pe, "rnd_h", b)
                if j == 0:
                    bank_free(("h_kept1", b - 1), ("o_kept", b + 2), ("x4_kept", b + 1), ("x3_kept", b + 5))
                else:
                    bank_free(("h_kept0", b))
                turn(rnd["h"][:, j * FH:(j + 1) * FH], FH // P).then_inc(s[f"h_turned{j}"], 1)

            def ffn_out(b):
                for j in range(2):
                    done(pe, f"h_kept{j}", b)
                bank_free(("x_done", b - 1), ("out_read", b + 2), ("q_scaled", b + 5))
                for c in range(HIDDEN // P):
                    last = nc.tensor.matmul(ps_m, hi_t[:, c * P:(c + 1) * P], k.w_ffn[:, 2, c * D:(c + 1) * D],
                                            start=c == 0, stop=c == HIDDEN // P - 1)
                last.then_inc(s["ffn_out"], 1)

            def step(b):
                stage(b - 1, turn_probs, 2)
                stage(b - 2, out_proj)
                stage(b - 3, gate_val, 0)
                stage(b - 1, attend, 1)
                stage(b - 4, turn_h, 0)

                stage(b, scores, 1)
                stage(b - 1, turn_probs, 3)
                stage(b - 4, turn_h, 1)
                stage(b + 1, q_proj)
                stage(b - 3, gate_val, 1)
                stage(b - 1, attend, 2)

                stage(b, scores, 2)
                stage(b, turn_probs, 0)
                stage(b - 4, ffn_out)
                stage(b - 1, attend, 3)

                stage(b, scores, 3)
                stage(b - 1, turn_back)
                stage(b + 1, turn_q)
                stage(b - 2, turn_x4)
                stage(b, turn_probs, 1)
                stage(b, attend, 0)
                stage(b + 1, scores, 0)
                stage(b + 2, turn_x3)
                stage(b - 1, turn_o)

            def last_step(b):
                stage(b - 1, turn_probs, 2)
                stage(b - 2, out_proj)
                stage(b - 3, gate_val, 0)
                stage(b - 4, turn_h, 0)
                stage(b - 1, turn_probs, 3)
                stage(b - 1, attend, 1)
                stage(b - 3, gate_val, 1)
                stage(b - 4, turn_h, 1)
                stage(b - 1, attend, 2)
                stage(b - 1, attend, 3)
                stage(b - 1, turn_back)
                stage(b - 4, ffn_out)
                stage(b - 2, turn_x4)
                stage(b - 1, turn_o)

            pe.sem_inc(s["h_turned1"], 1)
            pe.sem_inc(s["ffn_out"], 1)
            program(pe, step, last_step)

        @block.vector
        def _(dve):
            def maxima(b, j):
                done(dve, f"scores{j}", b)
                done(dve, f"exps{j}", b - 1)
                nc.vector.tensor_reduce(nmax[:, QH * j:QH * (j + 1)], ps_s[j % 2][:, :].rearrange("p (h e) -> p h e", h=QH),
                                        AX_X, ALU.max, negate=True).then_inc(s[f"nmax{j}"], 1)

            def largest(b, n):
                src = {3: norm[3], 4: norm[4], "o": o, "h": h}[n]
                done(dve, {3: "xn3", 4: "xn4", "o": "o"}.get(n, "h0"), b)
                if n == "h":
                    done(dve, "h1", b)
                nc.vector.tensor_reduce(amax[n][:, :], src[:, :], AX_X, ALU.max, apply_absolute_value=True).then_inc(s[f"amax_{n}"], 1)

            def scale_of(b, n):
                done(dve, f"amax_{n}", b)
                if n in (4, "h"):
                    steps = (1e-5, 1.0 / 127.0, ALU.max, ALU.mult)
                else:
                    steps = (1.0 / 127.0, 1e-8, ALU.mult, ALU.max)
                nc.vector.tensor_scalar(scale[n][:, :], amax[n][:, :], *steps).then_inc(s[f"scale_{n}"], 1)
                if n == 3:
                    nc.vector.tensor_scalar(scale3[:, bass.ds(b, 1)], amax[n][:, :], *steps).then_inc(s["scale3_kept"], 1)

            def invert_scale(b, n):
                done(dve, f"scale_{n}", b)
                if n == "h":
                    done(dve, "h_raw", b - 1)
                nc.vector.reciprocal(inv[n][:, :], scale[n][:, :]).then_inc(s[f"inv_{n}"], 1)

            def over_scale(b, n):
                src = {3: norm[3], 4: norm[4], "o": o}[n]
                done(dve, f"inv_{n}", b)
                nc.vector.tensor_scalar(raw_rnd[n][:, :], src[:, :], inv[n][:, 0:1], RND, ALU.mult, ALU.add).then_inc(s[f"raw_{n}"], 1)

            def between(b, n):
                low = -128.0 if n in (4, "h") else -127.0
                done(dve, "h_raw" if n == "h" else f"raw_{n}", b)
                done(dve, {3: "x3_turned", 4: "x4_turned", "o": "o_turned", "h": "h_turned1"}[n], b - 1)
                nc.vector.tensor_scalar(rnd[n][:, :], raw_rnd[n][:, :], RND + 127.0, RND + low, ALU.min, ALU.max
                                        ).then_inc(s[f"rnd_{n}"], 1)

            def units(b):
                for j in range(2):
                    last = nc.vector.tensor_tensor(unit[:, j, bass.ds(b, 1)], scale[4][:, :], gamma[:, j:j + 1], ALU.mult)
                last.then_inc(s["units"], 1)

            def unit_of_h(b):
                nc.vector.tensor_tensor(h_unit[:, :], scale["h"][:, :], k.gamma[:, 2:3], ALU.mult).then_inc(s["h_unit"], 1)

            def invert_sums(b):
                done(dve, "o_back", b)
                nc.vector.reciprocal(sinv[:, :], heads_of(ps_o)[:, :, HD1]).then_inc(s["sinv"], 1)

            def normed_o(b):
                done(dve, "sinv", b)
                nc.vector.tensor_tensor(o[:, :].rearrange("p (h d) -> p h d", h=NH1), heads_of(ps_o)[:, :, 0:HD1],
                                        sinv[:, :].rearrange("p (h o) -> p h o", o=1).broadcast_to([P, NH1, HD1]),
                                        ALU.mult).then_inc(s["o"], 1)

            def add_out(b):
                done(dve, "out", b)
                nc.vector.scalar_tensor_tensor(y[:, :], ps_m, scale["o"][:, :], k.scale_qp[:, D:2 * D],
                                               ALU.mult, ALU.mult).then_inc(s["out_read"], 1)
                done(dve, "out_read", b)
                done(dve, "bias3", b)
                done(dve, "bias4", b - 1)
                done(dve, "xn4", b - 1)
                nc.vector.tensor_tensor(xs[:, :], x_of(b), y[:, :], ALU.add).then_inc(s["added"], 1)

            def stats_of_x4(b):
                done(dve, "added", b)
                nc.vector.tensor_copy(seen[:, 0:1], xs[:, 0:1])
                nc.vector.bn_stats(stats4[:, :], xs[:, :]).then_inc(s["stats4"], 1)

            def mean_of_x4(b):
                done(dve, "stats4", b)
                done(dve, "nmr4", b - 1)
                nc.vector.tensor_copy(seen[:, :], stats4[:, :])
                nc.vector.bn_aggr(mv4[:, :], stats4[:, :]).then_inc(s["mv4"], 1)

            def biased(b, name, half):
                done(dve, f"mm_{name}{half}", b)
                done(dve, "units", b)
                done(dve, f"product{half}", b - 1)
                if name == "gate":
                    done(dve, f"tanh{half}", b - 1)
                j, to, ps, bias = (0, gate, ps_g, k.bias1[:, BG]) if name == "gate" else (1, val, ps_v, half_bv)
                nc.vector.scalar_tensor_tensor(to[:, half * FH:(half + 1) * FH], ps[:, :], unit[:, j, bass.ds(b, 1)],
                                               bias[:, half * FH:(half + 1) * FH],
                                               ALU.mult, ALU.add).then_inc(s[f"{name}{half}"], 1)

            def hidden(b, half):
                done(dve, f"tanh{half}", b)
                done(dve, f"product{half}", b)
                done(dve, "h_raw", b - 1)
                at = slice(half * FH, (half + 1) * FH)
                nc.vector.scalar_tensor_tensor(h[:, at], tanh[:, at], 1.0, product[:, at], ALU.add, ALU.mult
                                               ).then_inc(s[f"h{half}"], 1)

            def finish(b):
                done(dve, "ffn_out", b)
                done(dve, "bias4", b)
                done(dve, "h_unit", b)
                nc.vector.scalar_tensor_tensor(x_of(b), ps_m, h_unit[:, 0:1], x_of(b), ALU.mult, ALU.add).then_inc(s["x_done"], 1)

            def step(b):
                stage(b - 4, between, "h")
                stage(b - 2, add_out)
                stage(b - 2, stats_of_x4)
                stage(b - 3, biased, "gate", 0)
                stage(b - 2, mean_of_x4)
                stage(b - 3, biased, "val", 0)
                stage(b - 4, unit_of_h)

                stage(b, maxima, 1)
                stage(b + 2, largest, 3)
                stage(b - 3, biased, "gate", 1)
                stage(b + 2, scale_of, 3)
                stage(b + 2, invert_scale, 3)
                stage(b - 2, largest, 4)
                stage(b + 2, over_scale, 3)
                stage(b - 3, biased, "val", 1)
                stage(b - 2, scale_of, 4)
                stage(b, maxima, 2)
                stage(b + 2, between, 3)

                stage(b - 2, invert_scale, 4)
                stage(b - 2, over_scale, 4)
                stage(b - 3, hidden, 0)
                stage(b - 2, between, 4)
                stage(b - 2, units)
                stage(b - 4, finish)

                stage(b, maxima, 3)
                stage(b - 1, invert_sums)
                stage(b - 3, hidden, 1)
                stage(b - 1, normed_o)
                stage(b - 3, largest, "h")
                stage(b - 1, largest, "o")
                stage(b - 3, scale_of, "h")
                stage(b - 1, scale_of, "o")
                stage(b - 1, invert_scale, "o")
                stage(b - 3, invert_scale, "h")
                stage(b - 1, over_scale, "o")
                stage(b - 1, between, "o")
                stage(b + 1, maxima, 0)

            def last_step(b):
                stage(b - 4, between, "h")
                stage(b - 2, add_out)
                stage(b - 4, unit_of_h)
                stage(b - 3, biased, "gate", 0)
                stage(b - 2, stats_of_x4)
                stage(b - 2, mean_of_x4)
                stage(b - 3, biased, "val", 0)
                stage(b - 3, biased, "gate", 1)
                stage(b - 3, biased, "val", 1)
                stage(b - 2, largest, 4)
                stage(b - 2, scale_of, 4)
                stage(b - 2, invert_scale, 4)
                stage(b - 3, hidden, 0)
                stage(b - 2, over_scale, 4)
                stage(b - 1, invert_sums)
                stage(b - 2, between, 4)
                stage(b - 3, hidden, 1)
                stage(b - 2, units)
                stage(b - 4, finish)
                stage(b - 1, normed_o)
                stage(b - 3, largest, "h")
                stage(b - 1, largest, "o")
                stage(b - 3, scale_of, "h")
                stage(b - 1, scale_of, "o")
                stage(b - 1, invert_scale, "o")
                stage(b - 3, invert_scale, "h")
                stage(b - 1, over_scale, "o")
                stage(b - 1, between, "o")

            nc.vector.tensor_scalar(half_bv[:, :], k.bias1[:, BV], 0.5, None, ALU.mult)
            nc.vector.tensor_copy(gamma[:, 0:1], k.gamma[:, 0:1])
            nc.vector.tensor_scalar(gamma[:, 1:2], k.gamma[:, 1:2], 0.5, None, ALU.mult).then_inc(s["halved"], 1)
            dve.wait_ge(s["halved"], 1)

            def later_stats():
                for t in range(FIRST, B):
                    nc.vector.bn_stats(stats[:, t, :], k.x_res[:, t, :]).then_inc(s["later_stats"], 1)
                for t in range(FIRST, B):
                    dve.wait_ge(s["later_stats"], t - FIRST + 1)
                    nc.vector.bn_aggr(k.mv[:, t, :], stats[:, t, :]).then_inc(s["later_mv"], 1)

            dve.sem_inc(s["x_done"], 1)
            dve.sem_inc(s["rnd_h"], 1)
            program(dve, step, last_step, later_stats)

        @block.scalar
        def _(act):
            def exps(b, j):
                done(act, f"nmax{j}", b)
                done(act, f"quarter{j}", b - 1)
                for r in range(QH):
                    i = QH * j + r
                    last = nc.scalar.activation(prob[:, i, :], ps_s[j % 2][:, r * P:(r + 1) * P], ACT.Exp, bias=nmax[:, i:i + 1])
                last.then_inc(s[f"exps{j}"], 1)

            def keep_quarter(b, j):
                done(act, f"quarter{j}", b)
                done(act, f"pv{j}", b - 1)
                nc.scalar.activation(prob_t[:, QH * j:QH * (j + 1), :], ps_t[:, :].rearrange("p (r e) -> p r e", r=QH),
                                     ACT.Copy).then_inc(s[f"quarter_kept{j}"], 1)

            def scale_q(b):
                done(act, "q_proj", b)
                done(act, "q_turned", b - 1)
                done(act, "scale3_kept", b)
                nc.scalar.activation(q0[:, :], ps_m, ACT.Copy, scale=scale3[:, bass.ds(b, 1)]).then_inc(s["q_scaled"], 1)

            def keep_q(b):
                done(act, "q_turned", b)
                done(act, "scores3", b - 1)
                for c in range(KC):
                    last = nc.scalar.activation(q_t[:, c, :], ps_m[:, c * P:(c + 1) * P], ACT.Identity,
                                                bias=k.bq[:, c:c + 1], scale=k.wq_scale[:, c:c + 1])
                last.then_inc(s["q_kept"], 1)

            def keep_o_t(b):
                done(act, "pv3", b)
                done(act, "o_back", b - 1)
                nc.scalar.activation(o_t[:, :], ps_o[:, :], ACT.Copy).then_inc(s["o_t_kept"], 1)

            def keep_x(b, name, to):
                done(act, f"{name}_turned", b)
                nc.scalar.activation(to[:, :, cols(b, 0, P)], ps_turn[:, 0:D].rearrange("p (c n) -> p c n", c=KC), ACT.Copy,
                                     bias=-RND).then_inc(s[f"{name}_kept"], 1)

            def keep_o(b):
                done(act, "o_turned", b)
                done(act, "out", b - 1)
                nc.scalar.activation(oi_t[:, :, :], ps_turn[:, 0:D].rearrange("p (c n) -> p c n", c=KC), ACT.Copy,
                                     bias=-RND).then_inc(s["o_kept"], 1)

            def keep_h(b, j):
                done(act, f"h_turned{j}", b)
                done(act, "ffn_out", b - 1)
                nc.scalar.activation(hi_t[:, j * FH:(j + 1) * FH], ps_turn[:, :], ACT.Copy,
                                     bias=-RND).then_inc(s[f"h_kept{j}"], 1)

            def norm_x(b, n, src, rstd, nmr):
                if n == 4:
                    done(act, "added", b)
                    done(act, "nmr4", b)
                done(act, f"raw_{n}", b - 1)
                nc.scalar.activation(norm[n][:, :], src, ACT.Identity, bias=nmr, scale=rstd).then_inc(s[f"xn{n}"], 1)

            def norm_x3(b):
                norm_x(b, 3, x_of(b), k.rstd[:, bass.ds(b, 1)], k.nmr[:, bass.ds(b, 1)])

            def norm_x4(b):
                norm_x(b, 4, xs[:, :], rstd4[:, 0:1], nmr4[:, 0:1])

            def over_scale_h(b):
                done(act, "inv_h", b)
                done(act, "rnd_h", b - 1)
                nc.scalar.activation(raw_rnd["h"][:, :], h[:, :], ACT.Copy, bias=RND, scale=inv["h"][:, 0:1]).then_inc(s["h_raw"], 1)

            def tanhs(b, half):
                done(act, f"gate{half}", b)
                done(act, f"h{half}", b - 1)
                at = slice(half * FH, (half + 1) * FH)
                nc.scalar.activation(tanh[:, at], gate[:, at], ACT.Tanh, scale=0.5).then_inc(s[f"tanh{half}"], 1)

            def step(b):
                stage(b + 2, norm_x3)
                stage(b - 1, keep_quarter, 2)
                stage(b, exps, 0)
                stage(b - 4, keep_h, 0)
                stage(b - 3, tanhs, 0)

                stage(b - 1, keep_quarter, 3)
                stage(b + 1, scale_q)
                stage(b - 4, keep_h, 1)
                stage(b - 2, norm_x4)
                stage(b, exps, 1)
                stage(b - 3, tanhs, 1)

                stage(b - 1, keep_o_t)
                stage(b, keep_quarter, 0)
                stage(b, exps, 2)

                stage(b + 1, keep_q)
                stage(b - 2, keep_x, "x4", x4_t)
                stage(b, keep_quarter, 1)
                stage(b, exps, 3)
                stage(b + 2, keep_x, "x3", x3_t)
                stage(b - 3, over_scale_h)
                stage(b - 1, keep_o)

            def last_step(b):
                stage(b - 1, keep_quarter, 2)
                stage(b - 3, tanhs, 0)
                stage(b - 1, keep_quarter, 3)
                stage(b - 4, keep_h, 0)
                stage(b - 3, tanhs, 1)
                stage(b - 4, keep_h, 1)
                stage(b - 2, norm_x4)
                stage(b - 1, keep_o_t)
                stage(b - 2, keep_x, "x4", x4_t)
                stage(b - 3, over_scale_h)
                stage(b - 1, keep_o)

            act.sem_inc(s["h_kept1"], 1)
            act.sem_inc(s["h_raw"], 1)
            program(act, step, last_step, lambda: act.wait_ge(s["later_std"], 4), 1)

        @block.gpsimd
        def _(pool):
            def spread_keys(b, c):
                done(pool, f"scores{2 * c + 1}", b - 1)
                keys = k.k1_t[:, c, cols(b, 0, P)].rearrange("p (o e) -> p o e", o=1).broadcast_to([P, HC, P])
                mask = k.head_mask[:, :].rearrange("p (h o) -> p h o", o=1).broadcast_to([P, HC, P])
                nc.gpsimd.tensor_tensor(kd[:, c, :, :], keys, mask, ALU.mult).then_inc(s[f"keys{c}"], 1)

            def spread_values(b):
                done(pool, "pv3", b - 1)
                heads = lambda a: a.rearrange("p (h d) -> p h d", h=NH1)
                v_b = k.v1[:, bass.ds(b, 1), :].rearrange("p o (h d) -> p (o h) d", h=NH1)
                nc.gpsimd.tensor_tensor(v_now[:, :, 0:HD1], v_b, heads(k.bv[:, :]), ALU.add).then_inc(s["v_now"], 1)

            def add_bias3(b):
                done(pool, "xn3", b)
                nc.gpsimd.tensor_tensor(x_of(b), x_of(b), k.bias1[:, BP], ALU.add).then_inc(s["bias3"], 1)

            def add_bias4(b):
                done(pool, "added", b)
                nc.gpsimd.tensor_tensor(x_of(b), xs[:, :], k.bias1[:, BO], ALU.add).then_inc(s["bias4"], 1)

            def invert_std(b):
                done(pool, "mv4", b)
                nc.gpsimd.tensor_tensor(vpe4[:, :], mv4[:, 1:2], k.eps[:, 0:1], ALU.add).then_inc(s["vpe4"], 1)
                nc.gpsimd.tensor_tensor(neg_mean4[:, :], mv4[:, 0:1], k.minus_one[:, 0:1], ALU.mult).then_inc(s["neg_mean4"], 1)
                done(pool, "vpe4", b)
                done(pool, "xn4", b - 1)
                nc.gpsimd.tensor_tensor(rstd4[:, :], vpe4[:, :], k.neg_half[:, 0:1], ALU.pow).then_inc(s["rstd4"], 1)
                done(pool, "rstd4", b)
                done(pool, "neg_mean4", b)
                nc.gpsimd.tensor_tensor(nmr4[:, :], neg_mean4[:, :], rstd4[:, :], ALU.mult).then_inc(s["nmr4"], 1)

            def times(b, half):
                done(pool, f"gate{half}", b)
                done(pool, f"val{half}", b)
                done(pool, f"h{half}", b - 1)
                at = slice(half * FH, (half + 1) * FH)
                nc.gpsimd.tensor_tensor(product[:, at], gate[:, at], val[:, at], ALU.mult).then_inc(s[f"product{half}"], 1)

            def step(b):
                stage(b, spread_keys, 1)
                stage(b - 2, invert_std)
                stage(b - 2, add_bias4)
                stage(b - 3, times, 0)
                stage(b + 1, spread_keys, 0)
                stage(b + 1, add_bias3)
                stage(b - 3, times, 1)
                stage(b, spread_values)

            def last_step(b):
                stage(b - 2, invert_std)
                stage(b - 3, times, 0)
                stage(b - 2, add_bias4)
                stage(b - 3, times, 1)

            nc.gpsimd.memset(v_now[:, :, HD1 + 1:], 0.0)
            nc.gpsimd.memset(v_now[:, :, HD1:HD1 + 1], 1.0)

            def later_stds():
                pool.wait_ge(s["later_mv"], B - FIRST)
                invert_stds(nc, pool, s["later_std"], k, FIRST, B)

            program(pool, step, last_step, later_stds, 1)

        @block.sync
        def _(sp):
            with sp.Fori(0, B) as b:
                done(sp, "x_done", b)
                sp.dma_start(out[bass.ds(b, 1)].rearrange("o p d -> p (o d)"), x_of(b)).then_inc(s["stored"], 16)
            sp.wait_ge(s["stored"], 16 * B)


class Kept:
    pass


def build(nc, io, out):
    with ExitStack() as ctx:
        Mem.held.clear()
        m = Mem(nc, ctx)
        k = Kept()
        k.psum = ctx.enter_context(nc.psum_tensor("psum", [P, 8 * BANK], F32))
        k.x_res = m.sb("x_res", [P, B, D])
        k.xn_t = m.sb("xn_t", [P, KC, T])
        k.ctx_t = m.sb("ctx_t", [P, KC, T])
        k.ident = m.sb("ident", [P, P])
        k.neg_half = m.sb("neg_half", [P, 16])
        k.head_mask = m.sb("head_mask", [P, HC])
        k.mv = m.sb("mv", [P, B, 2])
        k.vpe = m.sb("vpe", [P, B])
        k.rstd = m.sb("rstd", [P, B])
        k.neg_mean = m.sb("neg_mean", [P, B])
        k.nmr = m.sb("nmr", [P, B])
        k.eps = m.sb("eps", [P, B])
        k.minus_one = m.sb("minus_one", [P, B])
        with ExitStack() as layer0:
            a = Mem(nc, layer0)
            k.wa_hi = a.sb("wa_hi", [P, NKV0, WA], F32R)
            k.wa_lo = a.sb("wa_lo", [P, NKV0, WA], F32R)
            k.wa_raw = a.sb("wa_raw", [P, NKV0, WA])
            k.mask = a.sb("mask", [P, S])
            k.bias_a = a.sb("bias_a", [P, NKV0 * 6 * P])
            k.eps_a = a.sb("eps_a", [P, 5])
            k.norm_w = a.sb("norm_w", [P, 2])
            k.key_scale = a.sb("key_scale", [P, 1])
            constants_and_first_norm(nc, io, k)
            layer0_attention(nc, io, k)
        k.comb_dram = nc.dram_tensor("expert_weights", (NE, T), F32, kind="Internal").ap()
        k.k1_t = m.sb("k1_t", [P, KC, T])
        k.v1 = m.sb("v1", [P, B, D])
        k.bv = m.sb("bv", [P, D])
        k.wqp_t = m.sb("wqp_t", [P, 2, KC, D], BF16)
        k.scale_qp = m.sb("scale_qp", [P, 2 * D])
        k.bias1 = m.sb("bias1", [P, 3 * D + 2 * HIDDEN])
        k.w_ffn = m.sb("w_ffn", [P, 3, KC * HIDDEN], BF16)
        k.gamma = m.sb("gamma", [P, 3])
        k.bq = m.sb("bq", [P, KC])
        k.wq_scale = m.sb("wq_scale", [P, KC])
        with ExitStack() as ffn0:
            a = Mem(nc, ffn0)
            k.wf = a.sb("wf", [P, 3, KC * HIDDEN])
            k.ginv = a.sb("ginv", [P, 3])
            k.comb_t = a.sb("comb_t", [NE, T])
            k.raw = a.sb("wm_raw", [P, 3, WM])
            k.w_hi = a.sb("wm_hi", [P, 3, WM], F32R)
            k.w_lo = a.sb("wm_lo", [P, 3, WM], F32R)
            k.xn_hi = a.sb("xn_hi", [P, KC, T], F32R)
            k.xn_lo = a.sb("xn_lo", [P, KC, T], F32R)
            router_and_layer1_keys(nc, io, k)
            experts(nc, io, k)
        m.end_of_layer()
        layer1(nc, io, k, out)


def lay_out(i):
    import numpy as np

    a = {n: np.asarray(v) for n, v in i.items()}

    def chunked(w):
        return w.reshape(-1, P, w.shape[1]).transpose(1, 0, 2)

    groups, biases = [], []
    for g in range(NKV0):
        q, kv = slice(g * GH * HD0, (g + 1) * GH * HD0), slice(g * HD0, (g + 1) * HD0)
        w_kv = np.concatenate([a["L0_xattn_Wk"][:, kv], a["L0_xattn_Wv"][:, kv]], axis=1)
        parts = (chunked(a["L0_xattn_Wq"][:, q]), chunked(w_kv), chunked(a["L0_xattn_Wo"][q]))
        groups.append(np.concatenate([p.reshape(P, -1) for p in parts], axis=1))
        biases += [a["L0_xattn_bq"][q], a["L0_xattn_bk"][kv], a["L0_xattn_bv"][kv]]
    gu, down = a["L0_ffn_gate_up_proj"], a["L0_ffn_down_proj"]
    inner = [w.reshape(MT, P, KC, P).transpose(0, 3, 2, 1).reshape(MT, P, KC * P) for w in (gu[:, :INTER], gu[:, INTER:])]
    inner.append(down.transpose(0, 2, 1).reshape(MT, P, D))
    return {
        "wkv_t": chunked(a["L1_xattn_wkv"].T),
        "wqp": np.concatenate([w.reshape(KC, P, D) for w in (a["L1_xattn_wq"], a["L1_xattn_wp"])]).transpose(1, 0, 2),
        "bk1": a["L1_xattn_bkv"][:D].reshape(KC, P).T,
        "bq1": a["L1_xattn_bq"].reshape(KC, P).T,
        "bv1": a["L1_xattn_bkv"][D:],
        "bias1": np.concatenate([a[n] for n in ("L1_xattn_bq", "L1_xattn_bp", "L1_ffn_gate_b", "L1_ffn_val_b", "L1_ffn_out_b")]),
        "gate_w": chunked(a["L1_ffn_gate_w"].T).reshape(P, -1),
        "val_w": chunked(a["L1_ffn_val_w"].T).reshape(P, -1),
        "out_w": chunked(a["L1_ffn_out_w"].T).reshape(P, -1),
        "gate_t": chunked(a["L0_ffn_gate_weight"].T),
        "wm": np.concatenate(inner, axis=2),
        "x": a["x"],
        "ctx_t": chunked(a["ctx_2048"].reshape(T, D).T),
        "mask": a["mask_1xSxS2_ff0"],
        "wa": np.stack(groups),
        "bias_a": np.concatenate(biases),
        "norm_w": np.stack([a["L0_xattn_qn_w"], a["L0_xattn_kn_w"]], axis=1),
    }


def kernel(**inputs):
    import numpy as np
    import concourse.bacc as bacc
    from concourse.bass_utils import run_bass_kernel_spmd

    nc = bacc.Bacc("TRN2", target_bir_lowering=False, num_devices=1)
    arrays = {f"in_{n}": np.ascontiguousarray(v) for n, v in lay_out(inputs).items()}
    io = {n[3:]: nc.dram_tensor(n, v.shape, mybir.dt.from_np(v.dtype), kind="ExternalInput").ap() for n, v in arrays.items()}
    out = nc.dram_tensor("out", (B, S, D), F32, kind="ExternalOutput").ap()
    build(nc, io, out)
    r = run_bass_kernel_spmd(nc, [arrays], core_ids=[0])
    return r.results[0]["out"]
```
